# Optimizing a Trainium2 kernel written in Bass

```python
import numpy as np
import jax
import jax.numpy as jnp

def _softmax(x, axis=-1):
    return jax.nn.softmax(x, axis=axis)

def _gelu(x):
    return jax.nn.gelu(x, approximate=True)

def _silu(x):
    return jax.nn.silu(x)

def _sigmoid(x):
    return jax.nn.sigmoid(x)

def _layernorm(x, axis=-1, eps=1e-05):
    m = jnp.mean(x, axis=axis, keepdims=True)
    v = jnp.var(x, axis=axis, keepdims=True)
    return (x - m) / jnp.sqrt(v + eps)

def _scatter_add(tgt, idx, src, axis=0):
    return tgt.at[idx].add(src)

def _segment_sum(src, seg, n):
    return jax.ops.segment_sum(src, seg, n)
kernel_name = 'mk_perceiver_d2_seqx_r4_9fb2d1'

def setup_inputs(seed: int=0):
    np.random.seed(seed)
    _w = jnp.asarray

    def _rec_inputs():
        import jax
        import jax.numpy as jnp
        _rk = jax.random.key(seed)
        x = -0.0002928 + 1 * jax.random.normal(jax.random.fold_in(_rk, 1), (1, 128, 256), jnp.float32)
        _lenS = 128 - jax.random.randint(jax.random.fold_in(_rk, 7), (1,), 0, max(1, 128 // 4) + 1, jnp.int32)
        _lenS2 = 12544 - jax.random.randint(jax.random.fold_in(_rk, 8), (1,), 0, max(1, 12544 // 4) + 1, jnp.int32)
        _ctx_1024P = jax.random.normal(jax.random.fold_in(_rk, 11), (1, 16, 256), jnp.float32)
        _ctx_1024c = jax.random.dirichlet(jax.random.fold_in(_rk, 511), 0.3 * jnp.ones((16,), jnp.float32), (1, 12544))
        _ctx_1024t = jnp.einsum('bsk,bkd->bsd', _ctx_1024c, _ctx_1024P)
        _ctx_1024t = _ctx_1024t * jax.lax.rsqrt(jnp.mean(jnp.square(_ctx_1024t)) + 1e-12) * 0.953939
        ctx_1024 = 4.13588e-05 + 0.999923 * (_ctx_1024t + 0.3 * jax.random.normal(jax.random.fold_in(_rk, 611), (1, 12544, 256), jnp.float32))
        return (x, ctx_1024)
    x, ctx_1024 = _rec_inputs()

    def _L0_xattn_setup():
        import jax, jax.numpy as jnp
        import numpy as np
        DIM = 256
        NUM_HEADS = 16
        DIM_HEAD = 64
        INNER = NUM_HEADS * DIM_HEAD
        SCALE = DIM_HEAD ** (-0.5)

        def _layernorm(x, gamma, beta, eps=1e-05):
            mu = jnp.mean(x, axis=-1, keepdims=True)
            var = jnp.mean(jnp.square(x - mu), axis=-1, keepdims=True)
            return (x - mu) * jax.lax.rsqrt(var + eps) * gamma + beta
        key = jax.random.key(seed)
        ks = jax.random.split(key, 8)
        B, SQ, SK = (2, 512, 1024)
        x = jax.random.normal(ks[0], (B, SQ, DIM), dtype=jnp.float32)
        context = jax.random.normal(ks[1], (B, SK, DIM), dtype=jnp.float32)
        ln_gamma = jnp.ones((DIM,), jnp.float32)
        ln_beta = jnp.zeros((DIM,), jnp.float32)
        w_q = jax.random.normal(ks[2], (DIM, INNER), dtype=jnp.float32) / np.sqrt(DIM)
        w_kv = jax.random.normal(ks[3], (DIM, 2 * INNER), dtype=jnp.float32) / np.sqrt(DIM)
        w_out = jax.random.normal(ks[4], (INNER, DIM), dtype=jnp.float32) / np.sqrt(INNER)
        b_out = jnp.zeros((DIM,), jnp.float32)
        gate = jnp.array([0.5], jnp.float32)
        return {'x': x, 'context': context, 'ln_gamma': ln_gamma, 'ln_beta': ln_beta, 'w_q': w_q, 'w_kv': w_kv, 'w_out': w_out, 'b_out': b_out, 'gate': gate}
    _L0_xattn_all = _L0_xattn_setup()
    _L0_xattn_in = {k: v for k, v in _L0_xattn_all.items() if k in ('ln_gamma', 'ln_beta', 'w_q', 'w_kv', 'w_out', 'b_out', 'gate')}
    del _L0_xattn_all

    def _L0_attn_setup():
        import jax, jax.numpy as jnp
        import numpy as np
        key = jax.random.key(seed)
        ks = jax.random.split(key, 7)
        B, P, D = (4, 512, 256)
        s = 1.0 / np.sqrt(D)
        return {'x': jax.random.normal(ks[0], (B, P, D), dtype=jnp.float32), 'Wq': jax.random.normal(ks[1], (D, D), dtype=jnp.float32) * s, 'bq': jnp.zeros((D,), dtype=jnp.float32), 'Wk': jax.random.normal(ks[2], (D, D), dtype=jnp.float32) * s, 'bk': jnp.zeros((D,), dtype=jnp.float32), 'Wv': jax.random.normal(ks[3], (D, D), dtype=jnp.float32) * s, 'bv': jnp.zeros((D,), dtype=jnp.float32)}
    _L0_attn_all = _L0_attn_setup()
    _L0_attn_in = {k: v for k, v in _L0_attn_all.items() if k in ('Wq', 'bq', 'Wk', 'bk', 'Wv', 'bv')}
    del _L0_attn_all

    def _L0_ffn_setup():
        import jax, jax.numpy as jnp
        import numpy as np
        HIDDEN = 256
        INNER = 1024

        def _weight_quant(w):
            scale = 1.0 / jnp.clip(jnp.mean(jnp.abs(w)), 1e-05)
            wq = jnp.clip(jnp.round(w * scale), -1.0, 1.0) / scale
            return w + jax.lax.stop_gradient(wq - w)

        def _act_quant(x):
            scale = 127.0 / jnp.clip(jnp.max(jnp.abs(x), axis=-1, keepdims=True), 1e-05)
            xq = jnp.clip(jnp.round(x * scale), -128.0, 127.0) / scale
            return x + jax.lax.stop_gradient(xq - x)

        def _bitlinear(x, w):
            return jnp.einsum('bsi,oi->bso', _act_quant(x), _weight_quant(w))
        key = jax.random.key(seed)
        k0, k1, k2, k3 = jax.random.split(key, 4)
        x = jax.random.normal(k0, (4, 512, HIDDEN), dtype=jnp.float32)
        w_gate = jax.random.normal(k1, (INNER, HIDDEN), dtype=jnp.float32) / np.sqrt(HIDDEN)
        w_up = jax.random.normal(k2, (INNER, HIDDEN), dtype=jnp.float32) / np.sqrt(HIDDEN)
        w_down = jax.random.normal(k3, (HIDDEN, INNER), dtype=jnp.float32) / np.sqrt(INNER)
        return {'x': x, 'w_gate': w_gate, 'w_up': w_up, 'w_down': w_down}
    _L0_ffn_all = _L0_ffn_setup()
    _L0_ffn_in = {k: v for k, v in _L0_ffn_all.items() if k in ('w_gate', 'w_up', 'w_down')}
    del _L0_ffn_all

    def _L1_xattn_setup():
        import jax, jax.numpy as jnp
        import numpy as np
        IN_CH = 256
        ATT_DIM = 256
        B, L1, L2 = (8, 512, 512)
        key = jax.random.key(seed)
        ks = jax.random.split(key, 8)
        s = 1.0 / np.sqrt(IN_CH)
        return {'input_1': jax.random.normal(ks[0], (B, L1, IN_CH), dtype=jnp.float32), 'input_2': jax.random.normal(ks[1], (B, L2, IN_CH), dtype=jnp.float32), 'Wq': jax.random.uniform(ks[2], (IN_CH, ATT_DIM), jnp.float32, -s, s), 'bq': jnp.zeros((ATT_DIM,), jnp.float32), 'Wk': jax.random.uniform(ks[3], (IN_CH, ATT_DIM), jnp.float32, -s, s), 'bk': jnp.zeros((ATT_DIM,), jnp.float32), 'Wv': jax.random.uniform(ks[4], (IN_CH, ATT_DIM), jnp.float32, -s, s), 'bv': jnp.zeros((ATT_DIM,), jnp.float32)}
    _L1_xattn_all = _L1_xattn_setup()
    _L1_xattn_in = {k: v for k, v in _L1_xattn_all.items() if k in ('Wq', 'bq', 'Wk', 'bk', 'Wv', 'bv')}
    del _L1_xattn_all

    def _L1_attn_setup():
        import jax, jax.numpy as jnp
        from jax import lax
        import numpy as np
        import math
        D_MODEL = 256
        D_STATE = 32
        D_CONV = 4
        EXPAND = 2
        D_INNER = EXPAND * D_MODEL
        DT_RANK = math.ceil(D_MODEL / 16)
        B, L = (4, 512)
        EPS = 1e-06

        def _rmsnorm(x, w):
            var = jnp.mean(x * x, axis=-1, keepdims=True)
            return x * lax.rsqrt(var + EPS) * w

        def _causal_depthwise_conv(x, conv_w, conv_b):
            xc = jnp.swapaxes(x, 1, 2)
            k = conv_w[:, None, :]
            y = lax.conv_general_dilated(xc, k, window_strides=(1,), padding=[(D_CONV - 1, 0)], dimension_numbers=('NCH', 'OIH', 'NCH'), feature_group_count=D_INNER)
            y = y + conv_b[None, :, None]
            return jnp.swapaxes(y, 1, 2)

        def _selective_scan(u, dt, A, Bm, Cm, D):

            def step(h, inp):
                ut, dtt, Bt, Ct = inp
                dA = jnp.exp(dtt[..., None] * A)
                h = dA * h + dtt[..., None] * Bt[:, None, :] * ut[..., None]
                y = jnp.einsum('bdn,bn->bd', h, Ct)
                return (h, y)
            h0 = jnp.zeros((u.shape[0], D_INNER, D_STATE), u.dtype)
            xs = (jnp.swapaxes(u, 0, 1), jnp.swapaxes(dt, 0, 1), jnp.swapaxes(Bm, 0, 1), jnp.swapaxes(Cm, 0, 1))
            _, ys = lax.scan(step, h0, xs)
            return jnp.swapaxes(ys, 0, 1) + u * D
        key = jax.random.key(seed)
        ks = jax.random.split(key, 10)
        x = jax.random.normal(ks[0], (B, L, D_MODEL), jnp.float32)
        norm_w = jnp.ones((D_MODEL,), jnp.float32)
        in_proj_w = jax.random.normal(ks[1], (2 * D_INNER, D_MODEL), jnp.float32) * 0.02
        conv_w = jax.random.normal(ks[2], (D_INNER, D_CONV), jnp.float32) * 0.1
        conv_b = jnp.zeros((D_INNER,), jnp.float32)
        x_proj_w = jax.random.normal(ks[3], (DT_RANK + 2 * D_STATE, D_INNER), jnp.float32) * 0.02
        dt_proj_w = jax.random.normal(ks[4], (D_INNER, DT_RANK), jnp.float32) * DT_RANK ** (-0.5)
        dt = jnp.exp(jax.random.uniform(ks[5], (D_INNER,)) * (np.log(0.1) - np.log(0.001)) + np.log(0.001))
        dt_proj_b = dt + jnp.log(-jnp.expm1(-dt))
        A_log = jnp.log(jnp.tile(jnp.arange(1, D_STATE + 1, dtype=jnp.float32)[None, :], (D_INNER, 1)))
        D_param = jnp.ones((D_INNER,), jnp.float32)
        out_proj_w = jax.random.normal(ks[6], (D_MODEL, D_INNER), jnp.float32) * 0.02
        return {'x': x, 'norm_w': norm_w, 'in_proj_w': in_proj_w, 'conv_w': conv_w, 'conv_b': conv_b, 'x_proj_w': x_proj_w, 'dt_proj_w': dt_proj_w, 'dt_proj_b': dt_proj_b, 'A_log': A_log, 'D_param': D_param, 'out_proj_w': out_proj_w}
    _L1_attn_all = _L1_attn_setup()
    _L1_attn_in = {k: v for k, v in _L1_attn_all.items() if k in ('norm_w', 'in_proj_w', 'conv_w', 'conv_b', 'x_proj_w', 'dt_proj_w', 'dt_proj_b', 'A_log', 'D_param', 'out_proj_w')}
    del _L1_attn_all

    def _L1_ffn_setup():
        import jax, jax.numpy as jnp
        import numpy as np
        LN_EPS = 1e-05

        def _swiglu(h, w_gate_up, w_down):
            gu = h @ w_gate_up.T
            gate, up = jnp.split(gu, 2, axis=-1)
            return jax.nn.silu(gate) * up @ w_down.T
        key = jax.random.key(seed)
        ks = jax.random.split(key, 6)
        d_model, d_ff, E = (256, 1024, 8)
        shared_d_ff = d_ff // 4
        routed_d_ff = d_ff - shared_d_ff
        B, S = (4, 512)
        x = jax.random.normal(ks[0], (B, S, d_model), dtype=jnp.float32)
        ln_gamma = jnp.ones((d_model,), jnp.float32)
        ln_beta = jnp.zeros((d_model,), jnp.float32)
        router_w = jax.random.normal(ks[1], (E, d_model), jnp.float32) * 0.02
        gate_up_w = jax.random.normal(ks[2], (E, 2 * routed_d_ff, d_model), jnp.float32) * (1.0 / np.sqrt(d_model))
        down_w = jax.random.normal(ks[3], (E, d_model, routed_d_ff), jnp.float32) * (1.0 / np.sqrt(routed_d_ff))
        shared_gate_up_w = jax.random.normal(ks[4], (2 * shared_d_ff, d_model), jnp.float32) * (1.0 / np.sqrt(d_model))
        shared_down_w = jax.random.normal(ks[5], (d_model, shared_d_ff), jnp.float32) * (1.0 / np.sqrt(shared_d_ff))
        return dict(x=x, ln_gamma=ln_gamma, ln_beta=ln_beta, router_w=router_w, gate_up_w=gate_up_w, down_w=down_w, shared_gate_up_w=shared_gate_up_w, shared_down_w=shared_down_w)
    _L1_ffn_all = _L1_ffn_setup()
    _L1_ffn_in = {k: v for k, v in _L1_ffn_all.items() if k in ('ln_gamma', 'ln_beta', 'router_w', 'gate_up_w', 'down_w', 'shared_gate_up_w', 'shared_down_w')}
    del _L1_ffn_all
    return {'x': x, 'ctx_1024': ctx_1024, 'L0_xattn_ln_gamma': _L0_xattn_in['ln_gamma'], 'L0_xattn_ln_beta': _L0_xattn_in['ln_beta'], 'L0_xattn_w_q': _L0_xattn_in['w_q'], 'L0_xattn_w_kv': _L0_xattn_in['w_kv'], 'L0_xattn_w_out': _L0_xattn_in['w_out'], 'L0_xattn_b_out': _L0_xattn_in['b_out'], 'L0_xattn_gate': _L0_xattn_in['gate'], 'L0_attn_Wq': _L0_attn_in['Wq'], 'L0_attn_bq': _L0_attn_in['bq'], 'L0_attn_Wk': _L0_attn_in['Wk'], 'L0_attn_bk': _L0_attn_in['bk'], 'L0_attn_Wv': _L0_attn_in['Wv'], 'L0_attn_bv': _L0_attn_in['bv'], 'L0_ffn_w_gate': _L0_ffn_in['w_gate'], 'L0_ffn_w_up': _L0_ffn_in['w_up'], 'L0_ffn_w_down': _L0_ffn_in['w_down'], 'L1_xattn_Wq': _L1_xattn_in['Wq'], 'L1_xattn_bq': _L1_xattn_in['bq'], 'L1_xattn_Wk': _L1_xattn_in['Wk'], 'L1_xattn_bk': _L1_xattn_in['bk'], 'L1_xattn_Wv': _L1_xattn_in['Wv'], 'L1_xattn_bv': _L1_xattn_in['bv'], 'L1_attn_norm_w': _L1_attn_in['norm_w'], 'L1_attn_in_proj_w': _L1_attn_in['in_proj_w'], 'L1_attn_conv_w': _L1_attn_in['conv_w'], 'L1_attn_conv_b': _L1_attn_in['conv_b'], 'L1_attn_x_proj_w': _L1_attn_in['x_proj_w'], 'L1_attn_dt_proj_w': _L1_attn_in['dt_proj_w'], 'L1_attn_dt_proj_b': _L1_attn_in['dt_proj_b'], 'L1_attn_A_log': _L1_attn_in['A_log'], 'L1_attn_D_param': _L1_attn_in['D_param'], 'L1_attn_out_proj_w': _L1_attn_in['out_proj_w'], 'L1_ffn_ln_gamma': _L1_ffn_in['ln_gamma'], 'L1_ffn_ln_beta': _L1_ffn_in['ln_beta'], 'L1_ffn_router_w': _L1_ffn_in['router_w'], 'L1_ffn_gate_up_w': _L1_ffn_in['gate_up_w'], 'L1_ffn_down_w': _L1_ffn_in['down_w'], 'L1_ffn_shared_gate_up_w': _L1_ffn_in['shared_gate_up_w'], 'L1_ffn_shared_down_w': _L1_ffn_in['shared_down_w']}

def reference(x, ctx_1024, L0_xattn_ln_gamma, L0_xattn_ln_beta, L0_xattn_w_q, L0_xattn_w_kv, L0_xattn_w_out, L0_xattn_b_out, L0_xattn_gate, L0_attn_Wq, L0_attn_bq, L0_attn_Wk, L0_attn_bk, L0_attn_Wv, L0_attn_bv, L0_ffn_w_gate, L0_ffn_w_up, L0_ffn_w_down, L1_xattn_Wq, L1_xattn_bq, L1_xattn_Wk, L1_xattn_bk, L1_xattn_Wv, L1_xattn_bv, L1_attn_norm_w, L1_attn_in_proj_w, L1_attn_conv_w, L1_attn_conv_b, L1_attn_x_proj_w, L1_attn_dt_proj_w, L1_attn_dt_proj_b, L1_attn_A_log, L1_attn_D_param, L1_attn_out_proj_w, L1_ffn_ln_gamma, L1_ffn_ln_beta, L1_ffn_router_w, L1_ffn_gate_up_w, L1_ffn_down_w, L1_ffn_shared_gate_up_w, L1_ffn_shared_down_w):
    import jax
    import jax.numpy as jnp

    def _L0_xattn_ref(x, context, ln_gamma, ln_beta, w_q, w_kv, w_out, b_out, gate):
        import jax, jax.numpy as jnp
        import numpy as np
        DIM = 256
        NUM_HEADS = 16
        DIM_HEAD = 64
        INNER = NUM_HEADS * DIM_HEAD
        SCALE = DIM_HEAD ** (-0.5)

        def _layernorm(x, gamma, beta, eps=1e-05):
            mu = jnp.mean(x, axis=-1, keepdims=True)
            var = jnp.mean(jnp.square(x - mu), axis=-1, keepdims=True)
            return (x - mu) * jax.lax.rsqrt(var + eps) * gamma + beta
        B, SQ, _ = x.shape
        SK = context.shape[1]
        xn = _layernorm(x, ln_gamma, ln_beta)
        q = (xn @ w_q).reshape(B, SQ, NUM_HEADS, DIM_HEAD)
        kv = context @ w_kv
        k, v = jnp.split(kv, 2, axis=-1)
        k = k.reshape(B, SK, NUM_HEADS, DIM_HEAD)
        v = v.reshape(B, SK, NUM_HEADS, DIM_HEAD)
        scores = jnp.einsum('bqhd,bkhd->bhqk', q * SCALE, k)
        attn = jax.nn.softmax(scores, axis=-1)
        out = jnp.einsum('bhqk,bkhd->bqhd', attn, v).reshape(B, SQ, INNER)
        out = out @ w_out + b_out
        return out * jnp.tanh(gate[0])

    def _L0_attn_ref(x, Wq, bq, Wk, bk, Wv, bv):
        import jax, jax.numpy as jnp
        import numpy as np
        b, p, d = x.shape
        q = jnp.einsum('bpd,ed->bpe', x, Wq) + bq
        k = jnp.einsum('bpd,ed->bpe', x, Wk) + bk
        v = jnp.einsum('bpd,ed->bpe', x, Wv) + bv
        attn = jnp.einsum('bqd,bkd->bqk', q, k)
        causal = jnp.triu(jnp.ones((p, p), dtype=bool), k=1)
        attn = jnp.where(causal, -jnp.inf, attn)
        attn = attn / jnp.sqrt(jnp.asarray(d, dtype=attn.dtype))
        scores = jax.nn.softmax(attn, axis=-1)
        return jnp.einsum('bqk,bkd->bqd', scores, v)

    def _L0_ffn_ref(x, w_gate, w_up, w_down):
        import jax, jax.numpy as jnp
        import numpy as np
        HIDDEN = 256
        INNER = 1024

        def _weight_quant(w):
            scale = 1.0 / jnp.clip(jnp.mean(jnp.abs(w)), 1e-05)
            wq = jnp.clip(jnp.round(w * scale), -1.0, 1.0) / scale
            return w + jax.lax.stop_gradient(wq - w)

        def _act_quant(x):
            scale = 127.0 / jnp.clip(jnp.max(jnp.abs(x), axis=-1, keepdims=True), 1e-05)
            xq = jnp.clip(jnp.round(x * scale), -128.0, 127.0) / scale
            return x + jax.lax.stop_gradient(xq - x)

        def _bitlinear(x, w):
            return jnp.einsum('bsi,oi->bso', _act_quant(x), _weight_quant(w))
        gate = jax.nn.silu(_bitlinear(x, w_gate))
        up = _bitlinear(x, w_up)
        return _bitlinear(gate * up, w_down)

    def _L1_xattn_ref(input_1, input_2, Wq, bq, Wk, bk, Wv, bv):
        import jax, jax.numpy as jnp
        import numpy as np
        IN_CH = 256
        ATT_DIM = 256
        B, L1, L2 = (8, 512, 512)
        scale = 1.0 / np.sqrt(ATT_DIM).astype(np.float32)
        Q = jnp.einsum('bld,de->ble', input_1, Wq) + bq
        K = jnp.einsum('bld,de->ble', input_2, Wk) + bk
        V = jnp.einsum('bld,de->ble', input_2, Wv) + bv
        scores = jnp.einsum('bqd,bkd->bqk', Q, K) * scale
        scores = jnp.clip(scores, -100.0, 100.0)
        weights = jax.nn.softmax(scores, axis=-1)
        return jnp.einsum('bqk,bkd->bqd', weights, V)

    def _L1_attn_ref(x, norm_w, in_proj_w, conv_w, conv_b, x_proj_w, dt_proj_w, dt_proj_b, A_log, D_param, out_proj_w):
        import jax, jax.numpy as jnp
        from jax import lax
        import numpy as np
        import math
        D_MODEL = 256
        D_STATE = 32
        D_CONV = 4
        EXPAND = 2
        D_INNER = EXPAND * D_MODEL
        DT_RANK = math.ceil(D_MODEL / 16)
        B, L = (4, 512)
        EPS = 1e-06

        def _rmsnorm(x, w):
            var = jnp.mean(x * x, axis=-1, keepdims=True)
            return x * lax.rsqrt(var + EPS) * w

        def _causal_depthwise_conv(x, conv_w, conv_b):
            xc = jnp.swapaxes(x, 1, 2)
            k = conv_w[:, None, :]
            y = lax.conv_general_dilated(xc, k, window_strides=(1,), padding=[(D_CONV - 1, 0)], dimension_numbers=('NCH', 'OIH', 'NCH'), feature_group_count=D_INNER)
            y = y + conv_b[None, :, None]
            return jnp.swapaxes(y, 1, 2)

        def _selective_scan(u, dt, A, Bm, Cm, D):

            def step(h, inp):
                ut, dtt, Bt, Ct = inp
                dA = jnp.exp(dtt[..., None] * A)
                h = dA * h + dtt[..., None] * Bt[:, None, :] * ut[..., None]
                y = jnp.einsum('bdn,bn->bd', h, Ct)
                return (h, y)
            h0 = jnp.zeros((u.shape[0], D_INNER, D_STATE), u.dtype)
            xs = (jnp.swapaxes(u, 0, 1), jnp.swapaxes(dt, 0, 1), jnp.swapaxes(Bm, 0, 1), jnp.swapaxes(Cm, 0, 1))
            _, ys = lax.scan(step, h0, xs)
            return jnp.swapaxes(ys, 0, 1) + u * D
        xn = _rmsnorm(x, norm_w)
        xz = jnp.einsum('bld,ed->ble', xn, in_proj_w)
        u, z = jnp.split(xz, 2, axis=-1)
        u = jax.nn.silu(_causal_depthwise_conv(u, conv_w, conv_b))
        dbl = jnp.einsum('bld,ed->ble', u, x_proj_w)
        dt, Bm, Cm = jnp.split(dbl, [DT_RANK, DT_RANK + D_STATE], axis=-1)
        dt = jax.nn.softplus(jnp.einsum('blr,dr->bld', dt, dt_proj_w) + dt_proj_b)
        A = -jnp.exp(A_log)
        y = _selective_scan(u, dt, A, Bm, Cm, D_param)
        y = y * jax.nn.silu(z)
        out = jnp.einsum('ble,de->bld', y, out_proj_w)
        return x + out

    def _L1_ffn_ref(x, ln_gamma, ln_beta, router_w, gate_up_w, down_w, shared_gate_up_w, shared_down_w):
        import jax, jax.numpy as jnp
        import numpy as np
        LN_EPS = 1e-05

        def _swiglu(h, w_gate_up, w_down):
            gu = h @ w_gate_up.T
            gate, up = jnp.split(gu, 2, axis=-1)
            return jax.nn.silu(gate) * up @ w_down.T
        B, S, D = x.shape
        E = router_w.shape[0]
        top_k = 2
        xt = x.reshape(-1, D)
        mu = jnp.mean(xt, axis=-1, keepdims=True)
        var = jnp.mean(jnp.square(xt - mu), axis=-1, keepdims=True)
        normed = (xt - mu) * jax.lax.rsqrt(var + LN_EPS) * ln_gamma + ln_beta
        logits = normed.astype(jnp.float32) @ router_w.T
        probs = jax.nn.softmax(logits, axis=-1)
        top_v, top_i = jax.lax.top_k(probs, top_k)
        gates = jax.nn.softmax(top_v, axis=-1)
        comb = jnp.sum(jax.nn.one_hot(top_i, E, dtype=gates.dtype) * gates[..., None], axis=1)
        out = jnp.zeros_like(normed)
        for e in range(E):
            y = _swiglu(normed, gate_up_w[e], down_w[e])
            out = out + comb[:, e, None] * y
        out = out + _swiglu(normed, shared_gate_up_w, shared_down_w)
        return out.reshape(B, S, D)
    x = x + _L0_xattn_ref(_layernorm(x, axis=-1), ctx_1024, L0_xattn_ln_gamma, L0_xattn_ln_beta, L0_xattn_w_q, L0_xattn_w_kv, L0_xattn_w_out, L0_xattn_b_out, L0_xattn_gate)
    x = x + _L0_attn_ref(_layernorm(x, axis=-1), L0_attn_Wq, L0_attn_bq, L0_attn_Wk, L0_attn_bk, L0_attn_Wv, L0_attn_bv)
    x = x + _L0_ffn_ref(_layernorm(x, axis=-1), L0_ffn_w_gate, L0_ffn_w_up, L0_ffn_w_down)
    x = x + _L1_xattn_ref(_layernorm(x, axis=-1), ctx_1024, L1_xattn_Wq, L1_xattn_bq, L1_xattn_Wk, L1_xattn_bk, L1_xattn_Wv, L1_xattn_bv)
    x = x + _L1_attn_ref(_layernorm(x, axis=-1), L1_attn_norm_w, L1_attn_in_proj_w, L1_attn_conv_w, L1_attn_conv_b, L1_attn_x_proj_w, L1_attn_dt_proj_w, L1_attn_dt_proj_b, L1_attn_A_log, L1_attn_D_param, L1_attn_out_proj_w)
    x = x + _L1_ffn_ref(_layernorm(x, axis=-1), L1_ffn_ln_gamma, L1_ffn_ln_beta, L1_ffn_router_w, L1_ffn_gate_up_w, L1_ffn_down_w, L1_ffn_shared_gate_up_w, L1_ffn_shared_down_w)
    return x

_drawn_inputs = setup_inputs


def setup_inputs(seed=0):
    import zlib

    import numpy as np

    out = dict(_drawn_inputs(seed))
    spreads = {'L0_xattn_ln_gamma': (1.0, 0.2),
     'L0_xattn_ln_beta': (0.0, 0.1),
     'L0_xattn_b_out': (0.0, 0.1),
     'L0_attn_bq': (0.0, 0.1),
     'L0_attn_bk': (0.0, 0.1),
     'L0_attn_bv': (0.0, 0.1),
     'L1_xattn_bq': (0.0, 0.1),
     'L1_xattn_bk': (0.0, 0.1),
     'L1_xattn_bv': (0.0, 0.1),
     'L1_attn_norm_w': (1.0, 0.2),
     'L1_attn_conv_b': (0.0, 0.1),
     'L1_attn_D_param': (1.0, 0.2),
     'L1_ffn_ln_gamma': (1.0, 0.2),
     'L1_ffn_ln_beta': (0.0, 0.1)}
    factors = {}
    for name, (base, spread) in spreads.items():
        noise = np.random.default_rng([zlib.crc32(name.encode()), seed]).standard_normal(out[name].shape)
        drawn = base * np.exp(spread * noise) if base else spread * noise
        out[name] = jnp.asarray(drawn.astype(out[name].dtype))
    for name, factor in factors.items():
        out[name] = (out[name] * factor).astype(out[name].dtype)
    return out
```

```python
from contextlib import ExitStack

import concourse.bass as bass
from concourse import mybir

ALU = mybir.AluOpType
ACT = mybir.ActivationFunctionType
AX = mybir.AxisListType
F32 = mybir.dt.float32
F32R = mybir.dt.float32r
F16 = mybir.dt.float16
BF16 = mybir.dt.bfloat16
I32 = mybir.dt.int32

P = 128
D = 256
DC = D // P
S = 128
SK = 12544
TILES = 7
CH = TILES * P
NCH = SK // CH
HCH = CH // 2
H0, DH = 16, 64
INNER = H0 * DH
VW = DH + 2
T0 = 4
LN_K = 14 * 0.6931471805599453
V_TOP = 32768.0
BIG = 3.0e38
LN_EPS = 1e-5

R_LN_G, R_LN_B, R_BOUT, R_A_BV, R_X_BV, R_RMS_W, R_F_G, R_F_B = range(8)
NROWS = 8
C_A_BQ, C_A_BK, C_X_BQ, C_X_BK = 0, 2, 4, 6
C_CONVB, C_DTB, C_DPAR = 8, 12, 16
NCOLS = 20


def at_least(engine, sem, value):
    if isinstance(value, int) and value <= 0:
        return
    engine.wait_ge(sem, value)


class Linker:

    def __init__(self, engine, sem):
        self.engine, self.sem, self.count = engine, sem, 0

    def on(self, engine):
        self.engine = engine
        return self

    def __call__(self, ins):
        self.count += 1
        ins.then_inc(self.sem, 1)
        self.engine.wait_ge(self.sem, self.count)


def layer_norm_scale(v, link, st, eps):
    t, y, a = st[:, 2:3], st[:, 3:4], st[:, 4:5]
    link(v.tensor_scalar(t, st[:, 1:2], eps, None, ALU.add))
    link(v.tensor_scalar(y.bitcast(I32), t.bitcast(I32), 1, None, ALU.logical_shift_right))
    link(v.tensor_scalar(y.bitcast(I32), y.bitcast(I32), -1.0, float(0x5F3759DF), ALU.mult, ALU.add))
    for _ in range(3):
        link(v.scalar_tensor_tensor(out=a, in0=y, scalar=t, in1=y, op0=ALU.mult, op1=ALU.mult))
        link(v.tensor_scalar(a, a, -0.5, 1.5, ALU.mult, ALU.add))
        link(v.tensor_tensor(y, y, a, ALU.mult))


def layer_norm(v, link, out, x, st, stats, eps=LN_EPS):
    link(v.bn_stats(stats[:, :], x))
    link(v.bn_aggr(st[:, 0:2], stats[:, :]))
    layer_norm_scale(v, link, st, eps)
    return v.tensor_scalar(out, x, st[:, 0:1], st[:, 3:4], ALU.subtract, ALU.mult)


def perceiver(nc, a, out):
    with ExitStack() as ctx:
        def sb(name, shape, dt=F32, scope=ctx):
            return scope.enter_context(nc.sbuf_tensor(name, shape, dt))

        def sem(name):
            return ctx.enter_context(nc.semaphore(name))

        x = sb("x", [P, D])
        z = sb("z", [P, D])
        y = sb("y", [P, D])
        zT = sb("zT", [P, DC, S])
        ident = sb("ident", [P, P])
        st = sb("st", [P, 8])
        stats = sb("stats", [P, 6])
        rows = sb("rows", [P, NROWS, D])
        cols = sb("cols", [P, NCOLS])
        gate = sb("gate", [P, 2])
        w_out = sb("w_out", [P, INNER // P, D])
        ps = ctx.enter_context(nc.psum_tensor("ps", [P, 8, 512], F32))

        vlink = Linker(None, sem("vector_chain"))
        alink = Linker(None, sem("scalar_chain"))
        plink = Linker(None, sem("pool_chain"))
        links = (vlink, alink, plink)
        stored = sem("stored")
        shared = {n: sem(n) for n in ("z_ready", "zT_done", "zT_ready", "out_done", "logits_done", "max_ready",
                                      "exp_ready", "turned", "turned_copied")}
        loaded = {n: sem("loaded_" + n) for n in ("x", "rows", "wq", "wkT", "wv", "w_out")}
        base = (x, z, y, zT, ident, st, stats, rows, cols, ps)

        first_cross_attention(nc, ctx, a, sb, sem, *base[:9], gate, w_out, ps, *links, shared, loaded)
        causal_attention(nc, a, sb, sem, base, links, shared)
        ternary_ffn(nc, a, sb, sem, base, links, shared)
        second_cross_attention(nc, a, sb, sem, base, links, shared)
        selective_scan(nc, a, sb, sem, base, links, shared)
        expert_ffn(nc, a, sb, sem, base, links, shared)

        with nc.Block() as block:
            @block.sync
            def _(sp):
                sp.dma_start(out, x[:, :]).then_inc(stored, 16)
                sp.wait_ge(stored, 16)


def first_cross_attention(nc, ctx, a, sb, sem, x, z, y, zT, ident, st, stats, rows, cols, gate, w_out, ps,
                          vlink, alink, plink, shared, loaded):
    with ExitStack() as own:
        def t(name, shape, dt=F32):
            return sb(name, shape, dt, own)

        wq = t("wq", [P, DC, INNER])
        wkT = t("wkT", [P, INNER // P, D])
        wv = t("wv", [P, DC, INNER])
        wv_hi = t("wv_hi", [P, DC, INNER], F32R)
        wv_lo = t("wv_lo", [P, DC, INNER], F32R)
        wv_abs = t("wv_abs", [P, DC])
        wv_bound = t("wv_bound", [P, DC, P])
        qT = t("qT", [P, INNER // P, S])
        q_hi = t("q_hi", [P, DC, H0, S], F32R)
        q_lo = t("q_lo", [P, DC, H0, S], F32R)
        c_raw = t("c_raw", [P, DC, CH])
        c_hi = t("c_hi", [P, 2, DC, CH], F32R)
        c_lo = t("c_lo", [P, 2, DC, CH], F32R)
        c_abs = t("c_abs", [P, 2, DC])
        v_scale = t("v_scale", [P, 2])
        v_unscale = t("v_unscale", [P, 2])
        v_hi = t("v_hi", [P, TILES, H0, VW], F16)
        v_lo = t("v_lo", [P, TILES, H0, VW], F16)
        p_exp = t("p_exp", [P, 2, CH])
        pT_hi = t("pT_hi", [P, 2, TILES, S], F16)
        pT_lo = t("pT_lo", [P, 2, TILES, S], F16)
        neg_row = t("neg_row", [P, 2])
        neg_max = t("neg_max", [P, 2, H0])
        drop = t("drop", [P, H0])
        decay = t("decay", [P, H0])
        acc = t("acc", [P, H0, DH + 1])
        rec = t("rec", [P, H0])
        o = t("o", [P, INNER])
        oT = t("oT", [P, INNER // P, S])
        tg = t("tg", [P, 1])
        one = t("one", [P, 1, 1])

        s_scores = [ps[:, 0:2, 0:HCH], ps[:, 2:4, 0:HCH]]
        s_t = [ps[:, 4, :], ps[:, 5, :]]
        s_v = ps[:, 6, :]
        s_pv = ps[:, 7, 0:4 * (DH + 1)].rearrange("p (h e) -> p h e", e=DH + 1)

        raw_loaded = sem("raw_loaded")
        ident_ready = sem("ident_ready")
        q_done, qT_ready = sem("q_done"), sem("qT_ready")
        qk_done, q_hi_ready, q_ready = sem("qk_done"), sem("q_hi_ready"), sem("q_ready")
        wv_hi_ready, wv_ready = sem("wv_hi_ready"), sem("wv_ready")
        bound_w_ready, ones_ready = sem("bound_w_ready"), sem("ones_ready")
        split_done, absmax_done, scale_ready = sem("split_done"), sem("absmax_done"), sem("scale_ready")
        scores_done, neg_max_ready, exp_done = sem("scores_done"), sem("neg_max_ready"), sem("exp_done")
        row_max_done = sem("row_max_done")
        t0_done, t1_done = sem("t0_done"), sem("t1_done")
        pT_hi_ready, pT_lo_ready = sem("pT_hi_ready"), sem("pT_lo_ready")
        v_bank_written, v_bank_free, v_hi_ready = sem("v_bank_written"), sem("v_bank_free"), sem("v_hi_ready")
        pv_done, drop_ready, decay_ready = sem("pv_done"), sem("drop_ready"), sem("decay_ready")
        acc_scaled, acc_num, flushed = sem("acc_scaled"), sem("acc_num"), sem("flushed")
        o_ready, oT_done, oT_ready = sem("o_ready"), sem("oT_done"), sem("oT_ready")
        gate_ready = sem("gate_ready")
        split_hi = sem("split_hi")

        ctxT = a["ctxT"].rearrange("(c p) k -> p c k", p=P)

        def chunk_pairs(engine, two_chunks):
            two_chunks(0, True, False)
            with engine.Fori(1, NCH // 2 - 1) as i:
                two_chunks(i * 2, False, False)
            two_chunks(NCH - 2, False, True)

        def steps(c0, last):
            for par in range(2):
                for h in range(H0):
                    c = c0 + par
                    yield c, par, h, c * H0 + h, last and par == 1

        def four_heads(q, k):
            h = 8 * (k // 4) + k // 2 % 2
            return q[:, k % 2, h:h + 7:2, :]

        def v_use(c, h):
            return c * 15 + (8 + h)

        def v_tile(c, h):
            return c * 14 + (7 + h if h < 7 else 6 + h)

        with nc.Block() as block:
            @block.sync
            def _(sp):
                sp.dma_start(x[:, :], a["x"]).then_inc(loaded["x"], 16)
                sp.dma_start(c_raw[:, :, :], ctxT[:, :, 0:CH]).then_inc(raw_loaded, 16)
                sp.dma_start(wv[:, :, :], a["wv"].rearrange("(c p) n -> p c n", p=P)).then_inc(loaded["wv"], 16)
                sp.dma_start(w_out[:, :, :], a["w_out"].rearrange("(c p) n -> p c n", p=P)).then_inc(loaded["w_out"], 16)

                def two_chunks(c0, first, last):
                    for par in range(2):
                        if last and par == 1:
                            break
                        c = c0 + par
                        sp.wait_ge(split_done, c + 1)
                        sp.wait_ge(absmax_done, c + 1)
                        sp.dma_start(c_raw[:, :, :], ctxT[:, :, bass.ds((c + 1) * CH, CH)]).then_inc(raw_loaded, 16)

                chunk_pairs(sp, two_chunks)

            @block.gpsimd
            def _(pool):
                link = plink.on(pool)
                link(nc.gpsimd.memset(ident[:, :], 0.0))
                nc.gpsimd.affine_select(out=ident[:, :], in_=ident[:, :], compare_op=ALU.not_equal, fill=1.0, base=0,
                                        pattern=[[-1, P]], channel_multiplier=1).then_inc(ident_ready, 1)
                nc.gpsimd.memset(v_hi[:, :, :, DH:VW], 1.0).then_inc(ones_ready, 1)
                nc.gpsimd.memset(acc[:, :, :], 0.0).then_inc(ones_ready, 1)
                nc.gpsimd.memset(one[:, :, :], 1.0).then_inc(ones_ready, 1)
                nc.gpsimd.memset(neg_max[:, 1, :], BIG).then_inc(ones_ready, 1)

                def split(c, par):
                    pool.wait_ge(raw_loaded, (c + 1) * 16)
                    at_least(pool, scores_done, (c - 1) * H0)
                    nc.gpsimd.tensor_tensor(c_hi[:, par, :, :], c_raw[:, :, :], one[:, :, :].to_broadcast([P, DC, CH]), ALU.mult).then_inc(split_hi, 1)
                    pool.wait_ge(split_hi, c + 1)
                    nc.gpsimd.tensor_tensor(c_lo[:, par, :, :], c_raw[:, :, :], c_hi[:, par, :, :].bitcast(F32),
                                            ALU.subtract).then_inc(split_done, 1)

                def two_chunks(c0, first, last):
                    for c, par, h, n, end in steps(c0, last):
                        if h == 0 and not end:
                            split(c + 1, 1 - par)
                        if h % 4 == 3:
                            g = h // 4
                            pool.wait_ge(decay_ready, c * 4 + (g + 1))
                            at_least(pool, flushed, (c - 1) * 4 + (g + 1))
                            grp = acc[:, 4 * g:4 * g + 4, :]
                            nc.gpsimd.tensor_tensor(grp, grp, decay[:, 4 * g:4 * g + 4].unsqueeze(2).to_broadcast([P, 4, DH + 1]),
                                                    ALU.mult).then_inc(acc_scaled, 1)

                pool.wait_ge(ones_ready, 4)
                split(0, 0)
                chunk_pairs(pool, two_chunks)

            @block.scalar
            def _(act):
                link = alink.on(act)
                act.dma_start(wq[:, :, :], a["wq"].rearrange("(c p) n -> p c n", p=P)).then_inc(loaded["wq"], 16)
                act.dma_start(wkT[:, :, :], a["wkT"].rearrange("(c p) n -> p c n", p=P)).then_inc(loaded["wkT"], 16)
                act.dma_start(rows[:, :, :], a["rows"].rearrange("(o r) d -> o r d", o=1).to_broadcast([P, NROWS, D])).then_inc(loaded["rows"], 16)
                act.dma_start(gate[:, 0:1], a["gate"].to_broadcast([P, 1])).then_inc(loaded["rows"], 16)
                act.dma_start(cols[:, :], a["cols"]).then_inc(loaded["rows"], 16)
                act.wait_ge(loaded["wv"], 16)
                nc.scalar.activation(wv_hi[:, :, :], wv[:, :, :], ACT.Copy).then_inc(wv_hi_ready, 1)

                def v_high(tile, half, par, use, number):
                    act.wait_ge(v_bank_written, use + 1)
                    nc.scalar.activation(v_hi[:, tile, 8 * half:8 * half + 8, 0:DH],
                                         s_v.rearrange("p (h e) -> p h e", e=DH), ACT.Copy,
                                         scale=v_scale[:, par:par + 1]).then_inc(v_hi_ready, 1)

                def exponent(n, h, par):
                    act.wait_ge(neg_max_ready, n + 1)
                    at_least(act, t1_done, n - 1)
                    nc.scalar.activation(p_exp[:, h % 2, :].rearrange("p (b k) -> p b k", b=2), s_scores[h % 2], ACT.Exp,
                                         bias=neg_max[:, par, h:h + 1]).then_inc(exp_done, 1)

                act.wait_ge(scale_ready, 1)
                for k in range(TILES):
                    v_high(k, 0, 0, 1 + k, k)
                for k in range(8):
                    act.wait_ge(qk_done, k + 1)
                    nc.scalar.activation(four_heads(q_hi, k),
                                         ps[:, k % 4, :].rearrange("p (h s) -> p h s", h=4), ACT.Copy).then_inc(q_hi_ready, 1)
                exponent(0, 0, 0)

                def two_chunks(c0, first, last):
                    for c, par, h, n, end in steps(c0, last):
                        if not (end and h == H0 - 1):
                            exponent(n + 1, (h + 1) % H0, par if h < H0 - 1 else 1 - par)
                        if h < 7:
                            if h == 0:
                                at_least(act, pv_done, c * H0)
                            v_high(h, 1, par, v_use(c, h), v_tile(c, h))
                        elif 8 <= h < 15 and not end:
                            if h == 8:
                                act.wait_ge(pv_done, c * H0 + 8)
                                act.wait_ge(scale_ready, c + 2)
                            v_high(h - 8, 0, 1 - par, v_use(c, h), v_tile(c, h))
                        if h % 4 == 3:
                            g = h // 4
                            act.wait_ge(drop_ready, c * 4 + (g + 1))
                            at_least(act, acc_scaled, (c - 1) * 4 + (g + 1))
                            nc.scalar.activation(decay[:, 4 * g:4 * g + 4], drop[:, 4 * g:4 * g + 4], ACT.Exp).then_inc(decay_ready, 1)
                        at_least(act, pv_done, n - 1)
                        act.wait_ge(t0_done, n + 1)
                        nc.scalar.activation(pT_hi[:, h % 2, 0:T0, :], s_t[0].rearrange("p (t s) -> p t s", t=T0), ACT.Copy).then_inc(pT_hi_ready, 1)
                        act.wait_ge(t1_done, n + 1)
                        nc.scalar.activation(pT_hi[:, h % 2, T0:TILES, :], s_t[1][:, 0:(TILES - T0) * S].rearrange("p (t s) -> p t s", s=S),
                                             ACT.Copy).then_inc(pT_hi_ready, 1)

                chunk_pairs(act, two_chunks)
                act.wait_ge(loaded["rows"], 48)
                nc.scalar.activation(tg[:, :], gate[:, 0:1], ACT.Tanh).then_inc(gate_ready, 1)
                for k in range(2):
                    act.wait_ge(oT_done, k + 1)
                    nc.scalar.activation(oT[:, 4 * k:4 * k + 4, :], ps[:, k, :].rearrange("p (j s) -> p j s", j=4), ACT.Copy).then_inc(oT_ready, 1)

            @block.vector
            def _(v):
                link = vlink.on(v)
                v.wait_ge(loaded["x"], 16)
                link(layer_norm(nc.vector, link, z[:, :], x[:, :], st, stats))
                link(layer_norm(nc.vector, link, y[:, :], z[:, :], st, stats))
                v.wait_ge(loaded["rows"], 48)
                link(nc.vector.tensor_tensor(y[:, :], y[:, :], rows[:, R_LN_G, :], ALU.mult))
                nc.vector.tensor_tensor(y[:, :], y[:, :], rows[:, R_LN_B, :], ALU.add).then_inc(shared["z_ready"], 1)

                def absmax(c, par):
                    v.wait_ge(raw_loaded, (c + 1) * 16)
                    nc.vector.tensor_reduce(c_abs[:, par, :], c_raw[:, :, :], AX.X, ALU.max,
                                            apply_absolute_value=True).then_inc(absmax_done, 1)

                def scale(c, par, use):
                    v.wait_ge(v_bank_written, use + 1)
                    nc.vector.tensor_scalar(v_unscale[:, par:par + 1], s_v[:, 0:1], 1.0 / V_TOP, 1e-30, ALU.mult, ALU.max).then_inc(v_bank_free, 1)
                    v.wait_ge(v_bank_free, use + 1)
                    nc.vector.reciprocal(v_scale[:, par:par + 1], v_unscale[:, par:par + 1]).then_inc(scale_ready, 1)

                def v_low(tile, half, par, use, number):
                    v.wait_ge(v_hi_ready, number + 1)
                    nc.vector.scalar_tensor_tensor(out=v_lo[:, tile, 8 * half:8 * half + 8, 0:DH],
                                                   in0=s_v.rearrange("p (h e) -> p h e", e=DH), scalar=v_scale[:, par:par + 1],
                                                   in1=v_hi[:, tile, 8 * half:8 * half + 8, 0:DH],
                                                   op0=ALU.mult, op1=ALU.subtract).then_inc(v_bank_free, 1)

                def row_max(n, h, par):
                    v.wait_ge(scores_done, n + 1)
                    nc.vector.tensor_reduce(neg_row[:, h % 2:h % 2 + 1], s_scores[h % 2], AX.XY, ALU.max, negate=True).then_inc(row_max_done, 1)
                    v.wait_ge(row_max_done, n + 1)
                    nc.vector.scalar_tensor_tensor(out=neg_max[:, par, h:h + 1], in0=neg_row[:, h % 2:h % 2 + 1], scalar=LN_K,
                                                   in1=neg_max[:, 1 - par, h:h + 1], op0=ALU.add, op1=ALU.min).then_inc(neg_max_ready, 1)

                def flush(f, g, par):
                    v.wait_ge(pv_done, (f + 1) * 4)
                    v.wait_ge(acc_scaled, f + 1)
                    nc.vector.scalar_tensor_tensor(out=acc[:, 4 * g:4 * g + 4, 0:DH], in0=s_pv[:, :, 0:DH],
                                                   scalar=v_unscale[:, par:par + 1], in1=acc[:, 4 * g:4 * g + 4, 0:DH],
                                                   op0=ALU.mult, op1=ALU.add).then_inc(acc_num, 1)
                    nc.vector.tensor_tensor(acc[:, 4 * g:4 * g + 4, DH:DH + 1], acc[:, 4 * g:4 * g + 4, DH:DH + 1],
                                            s_pv[:, :, DH:DH + 1], ALU.add).then_inc(flushed, 1)

                v.wait_ge(loaded["wv"], 16)
                link(nc.vector.tensor_reduce(wv_abs[:, :], wv[:, :, :], AX.X, ALU.max, apply_absolute_value=True))
                absmax(0, 0)
                nc.vector.tensor_copy(wv_bound[:, :, :], wv_abs[:, :].unsqueeze(2).to_broadcast([P, DC, P])).then_inc(bound_w_ready, 1)
                v.wait_ge(wv_hi_ready, 1)
                nc.vector.tensor_tensor(wv_lo[:, :, :], wv[:, :, :], wv_hi[:, :, :].bitcast(F32), ALU.subtract).then_inc(wv_ready, 1)
                v.wait_ge(shared["zT_done"], 1)
                nc.vector.tensor_copy(zT[:, :, :], ps[:, 0, 0:DC * S].rearrange("p (c s) -> p c s", c=DC)).then_inc(shared["zT_ready"], 1)
                scale(0, 0, 0)
                for k in range(2):
                    v.wait_ge(q_done, k + 1)
                    nc.vector.tensor_scalar(qT[:, 4 * k:4 * k + 4, :], ps[:, 1 + k, :].rearrange("p (j s) -> p j s", j=4),
                                            DH ** -0.5, None, ALU.mult).then_inc(qT_ready, 1)
                for k in range(TILES):
                    v_low(k, 0, 0, 1 + k, k)
                for k in range(8):
                    v.wait_ge(q_hi_ready, k + 1)
                    nc.vector.tensor_tensor(four_heads(q_lo, k), ps[:, k % 4, :].rearrange("p (h s) -> p h s", h=4),
                                            four_heads(q_hi, k).bitcast(F32), ALU.subtract).then_inc(q_ready, 1)
                v.wait_ge(ones_ready, 4)
                row_max(0, 0, 0)

                def two_chunks(c0, first, last):
                    for c, par, h, n, end in steps(c0, last):
                        if not (end and h == H0 - 1):
                            row_max(n + 1, (h + 1) % H0, par if h < H0 - 1 else 1 - par)
                        if h == 2 and not end:
                            absmax(c + 1, 1 - par)
                        if h < 7:
                            v_low(h, 1, par, v_use(c, h), v_tile(c, h))
                        elif h == 7 and not end:
                            scale(c + 1, 1 - par, v_use(c, h))
                        elif h < 15 and not end:
                            v_low(h - 8, 0, 1 - par, v_use(c, h), v_tile(c, h))
                        if h % 4 == 0 and not (first and par == 0 and h == 0):
                            flush(c * 4 + (h // 4 - 1), (h // 4 - 1) % 4, par if h else 1 - par)
                        if h % 4 == 3:
                            g = h // 4
                            at_least(v, decay_ready, (c - 1) * 4 + (g + 1))
                            v.wait_ge(neg_max_ready, n + 1)
                            nc.vector.tensor_tensor(drop[:, 4 * g:4 * g + 4], neg_max[:, par, 4 * g:4 * g + 4],
                                                    neg_max[:, 1 - par, 4 * g:4 * g + 4], ALU.subtract).then_inc(drop_ready, 1)
                        for b, (t0, t1) in enumerate(((0, T0), (T0, TILES))):
                            v.wait_ge(pT_hi_ready, n * 2 + (b + 1))
                            nc.vector.tensor_tensor(pT_lo[:, h % 2, t0:t1, :], s_t[b][:, 0:(t1 - t0) * S].rearrange("p (t s) -> p t s", s=S),
                                                    pT_hi[:, h % 2, t0:t1, :], ALU.subtract).then_inc(pT_lo_ready, 1)

                chunk_pairs(v, two_chunks)
                flush(NCH * 4 - 1, 3, 1)
                v.wait_ge(flushed, NCH * 4)
                v.wait_ge(acc_num, NCH * 4)
                link(nc.vector.reciprocal(rec[:, :], acc[:, :, DH]))
                nc.vector.tensor_tensor(o[:, :].rearrange("p (h e) -> p h e", e=DH), acc[:, :, 0:DH],
                                        rec[:, :].unsqueeze(2).to_broadcast([P, H0, DH]), ALU.mult).then_inc(o_ready, 1)
                v.wait_ge(shared["out_done"], 1)
                link(nc.vector.tensor_tensor(y[:, :], ps[:, 2, 0:D], rows[:, R_BOUT, :], ALU.add))
                v.wait_ge(gate_ready, 1)
                link(nc.vector.scalar_tensor_tensor(out=x[:, :], in0=y[:, :], scalar=tg[:, 0:1], in1=x[:, :], op0=ALU.mult, op1=ALU.add))

            @block.tensor
            def _(pe):
                def v_project(tile, half, par, use):
                    pe.wait_ge(v_bank_free, use)
                    k = 0
                    for c in range(DC):
                        lh = c_hi[:, par, c, tile * P:(tile + 1) * P]
                        ll = c_lo[:, par, c, tile * P:(tile + 1) * P]
                        rh = wv_hi[:, c, 512 * half:512 * half + 512]
                        rl = wv_lo[:, c, 512 * half:512 * half + 512]
                        for lhs, rhs in ((lh, rh), (lh, rl), (ll, rh)):
                            mm = nc.tensor.matmul(s_v, lhs, rhs, start=(k == 0), stop=(k == 5))
                            k += 1
                    mm.then_inc(v_bank_written, 1)

                def bound(par, use):
                    at_least(pe, v_bank_free, use)
                    for c in range(DC):
                        mm = nc.tensor.matmul(s_v[:, 0:1], wv_bound[:, c, :], c_abs[:, par, c:c + 1], start=(c == 0), stop=(c == DC - 1))
                    mm.then_inc(v_bank_written, 1)

                def scores(n, h, par):
                    at_least(pe, exp_done, n - 1)
                    k = 0
                    for c in range(DC):
                        for qq, cc in ((q_hi, c_hi), (q_hi, c_lo), (q_lo, c_hi)):
                            for b in range(2):
                                mm = nc.tensor.matmul(s_scores[h % 2][:, b, :], qq[:, c, h, :], cc[:, par, c, b * HCH:(b + 1) * HCH],
                                                      start=(k == 0), stop=(k == 5))
                            k += 1
                    mm.then_inc(scores_done, 1)

                def weigh(n, h):
                    pe.wait_ge(pT_lo_ready, n * 2 + 2)
                    for tile in range(TILES):
                        ph, pl = pT_hi[:, h % 2, tile, :], pT_lo[:, h % 2, tile, :]
                        nc.tensor.matmul(s_pv[:, h % 4, :], ph, v_hi[:, tile, h, 0:DH + 1], start=(tile == 0), stop=False)
                        nc.tensor.matmul(s_pv[:, h % 4, 0:DH], ph, v_lo[:, tile, h, 0:DH], start=False, stop=False)
                        mm = nc.tensor.matmul(s_pv[:, h % 4, :], pl, v_hi[:, tile, h, 0:DH + 1], start=False, stop=(tile == TILES - 1))
                    mm.then_inc(pv_done, 1)

                def transpose_p(n, h):
                    pe.wait_ge(exp_done, n + 1)
                    for tile in range(TILES):
                        b, s = (0, tile) if tile < T0 else (1, tile - T0)
                        mm = nc.tensor.transpose(s_t[b][:, s * S:(s + 1) * S], p_exp[:, h % 2, tile * P:(tile + 1) * P], ident[:, :])
                        if tile == T0 - 1:
                            mm.then_inc(t0_done, 1)
                    mm.then_inc(t1_done, 1)

                pe.wait_ge(ident_ready, 1)
                pe.wait_ge(bound_w_ready, 1)
                pe.wait_ge(absmax_done, 1)
                bound(0, 0)
                pe.wait_ge(shared["z_ready"], 1)
                for c in range(DC):
                    mm = nc.tensor.transpose(ps[:, 0, c * S:(c + 1) * S], y[:, c * P:(c + 1) * P], ident[:, :])
                mm.then_inc(shared["zT_done"], 1)
                pe.wait_ge(shared["zT_ready"], 1)
                pe.wait_ge(loaded["wq"], 16)
                for k in range(2):
                    for j in range(4):
                        for c in range(DC):
                            mm = nc.tensor.matmul(ps[:, 1 + k, j * S:(j + 1) * S], wq[:, c, (4 * k + j) * P:(4 * k + j + 1) * P],
                                                  zT[:, c, :], start=(c == 0), stop=(c == DC - 1))
                    mm.then_inc(q_done, 1)
                pe.wait_ge(split_done, 1)
                pe.wait_ge(wv_ready, 1)
                for k in range(TILES):
                    v_project(k, 0, 0, 1 + k)
                pe.wait_ge(loaded["wkT"], 16)
                for k in range(8):
                    if k == 0:
                        pe.wait_ge(qT_ready, 2)
                    at_least(pe, q_ready, k - 3)
                    for i in range(4):
                        r = DH * (k // 2 % 2)
                        j = 4 * (k // 4) + i
                        mm = nc.tensor.matmul(ps[:, k % 4, i * S:(i + 1) * S], wkT[r:r + DH, j, (k % 2) * P:(k % 2 + 1) * P],
                                              qT[r:r + DH, j, :], start=True, stop=True)
                    mm.then_inc(qk_done, 1)
                pe.wait_ge(q_ready, 8)
                scores(0, 0, 0)

                def two_chunks(c0, first, last):
                    for c, par, h, n, end in steps(c0, last):
                        if not (end and h == H0 - 1):
                            if h == H0 - 1:
                                pe.wait_ge(split_done, c + 2)
                            scores(n + 1, (h + 1) % H0, par if h < H0 - 1 else 1 - par)
                        if h < 7:
                            v_project(h, 1, par, v_use(c, h))
                        elif h == 7 and not end:
                            pe.wait_ge(absmax_done, c + 2)
                            bound(1 - par, v_use(c, h))
                        elif h < 15 and not end:
                            if h == 8:
                                pe.wait_ge(split_done, c + 2)
                            v_project(h - 8, 0, 1 - par, v_use(c, h))
                        if not (first and par == 0 and h == 0):
                            hp = (h - 1) % H0
                            if hp % 4 == 0:
                                at_least(pe, flushed, c * 4 + hp // 4)
                            if hp % 8 == 0:
                                pe.wait_ge(v_bank_free, c * 15 + (8 if hp == 0 else 15))
                            weigh(n - 1, hp)
                        transpose_p(n, h)

                chunk_pairs(pe, two_chunks)
                weigh(NCH * H0 - 1, H0 - 1)
                pe.wait_ge(o_ready, 1)
                for k in range(2):
                    for j in range(4):
                        mm = nc.tensor.transpose(ps[:, k, j * S:(j + 1) * S], o[:, (4 * k + j) * P:(4 * k + j + 1) * P], ident[:, :])
                    mm.then_inc(oT_done, 1)
                pe.wait_ge(loaded["w_out"], 16)
                for k in range(8):
                    if k % 4 == 0:
                        pe.wait_ge(oT_ready, k // 4 + 1)
                    mm = nc.tensor.matmul(ps[:, 2, 0:D], oT[:, k, :], w_out[:, k, :], start=(k == 0), stop=(k == 7))
                mm.then_inc(shared["out_done"], 1)


def transpose_z(nc, pe, ps, z, ident, done):
    for c in range(DC):
        mm = nc.tensor.transpose(ps[:, 0, c * S:(c + 1) * S], z[:, c * P:(c + 1) * P], ident[:, :])
    mm.then_inc(done, 1)


def causal_attention(nc, a, sb, sem, base, links, shared):
    x, z, y, zT, ident, st, stats, rows, cols, ps = base
    vlink, alink, plink = links
    with ExitStack() as own:
        def t(name, shape, dt=F32):
            return sb("ca_" + name, shape, dt, own)

        w = {n: t(n, [P, DC, D]) for n in ("wq", "wk", "wv")}
        qT, kT, val = t("qT", [P, DC, S]), t("kT", [P, DC, S]), t("val", [P, D])
        sc, p, pT = t("sc", [P, S]), t("p", [P, S]), t("pT", [P, S])
        neg_max, total, rec = t("neg_max", [P, 1]), t("total", [P, 1]), t("rec", [P, 1])
        E = {n: sem("ca_" + n) for n in ("w_loaded", "proj_done", "q_ready", "kv_ready",
                                         "copied", "masked", )}
        with nc.Block() as block:
            @block.sync
            def _(sp):
                for n in ("wq", "wk", "wv"):
                    sp.dma_start(w[n][:, :, :], a["ca_" + n].rearrange("(c p) n -> p c n", p=P)).then_inc(E["w_loaded"], 16)

            @block.vector
            def _(v):
                link = vlink.on(v)
                layer_norm(nc.vector, link, z[:, :], x[:, :], st, stats).then_inc(shared["z_ready"], 1)
                v.wait_ge(shared["zT_done"], 2)
                nc.vector.tensor_copy(zT[:, :, :], ps[:, 0, 0:DC * S].rearrange("p (c s) -> p c s", c=DC)).then_inc(shared["zT_ready"], 1)
                v.wait_ge(E["proj_done"], 1)
                nc.vector.tensor_tensor(kT[:, :, :], ps[:, 2, 0:DC * S].rearrange("p (c s) -> p c s", c=DC),
                                        cols[:, C_A_BK:C_A_BK + DC].unsqueeze(2).to_broadcast([P, DC, S]), ALU.add).then_inc(E["kv_ready"], 1)
                nc.vector.tensor_tensor(val[:, :], ps[:, 3, 0:D], rows[:, R_A_BV, :], ALU.add).then_inc(E["kv_ready"], 1)
                v.wait_ge(E["masked"], 1)
                link(nc.vector.tensor_reduce(neg_max[:, :], sc[:, :], AX.X, ALU.max, negate=True))
                nc.vector.tensor_scalar(neg_max[:, :], neg_max[:, :], D ** -0.5, None, ALU.mult).then_inc(shared["max_ready"], 1)
                v.wait_ge(shared["exp_ready"], 1)
                link(nc.vector.reciprocal(rec[:, :], total[:, :]))
                v.wait_ge(shared["out_done"], 2)
                link(nc.vector.scalar_tensor_tensor(out=x[:, :], in0=ps[:, 6, 0:D], scalar=rec[:, 0:1], in1=x[:, :],
                                                    op0=ALU.mult, op1=ALU.add))

            @block.scalar
            def _(act):
                link = alink.on(act)
                act.wait_ge(E["proj_done"], 1)
                for c in range(DC):
                    nc.scalar.activation(qT[:, c, :], ps[:, 1, c * S:(c + 1) * S], ACT.Identity,
                                         bias=cols[:, C_A_BQ + c:C_A_BQ + c + 1]).then_inc(E["q_ready"], 1)
                act.wait_ge(shared["logits_done"], 1)
                nc.scalar.activation(sc[:, :], ps[:, 4, 0:S], ACT.Copy).then_inc(E["copied"], 1)
                act.wait_ge(shared["max_ready"], 1)
                nc.scalar.activation(p[:, :], sc[:, :], ACT.Exp, bias=neg_max[:, 0:1], scale=D ** -0.5,
                                     accum_out=total[:, :]).then_inc(shared["exp_ready"], 1)
                act.wait_ge(shared["turned"], 1)
                nc.scalar.activation(pT[:, :], ps[:, 5, 0:S], ACT.Copy).then_inc(shared["turned_copied"], 1)

            @block.gpsimd
            def _(pool):
                pool.wait_ge(E["copied"], 1)
                nc.gpsimd.affine_select(out=sc[:, :], in_=sc[:, :], compare_op=ALU.is_ge, fill=-BIG, base=0,
                                        pattern=[[-1, S]], channel_multiplier=1).then_inc(E["masked"], 1)

            @block.tensor
            def _(pe):
                pe.wait_ge(shared["z_ready"], 2)
                transpose_z(nc, pe, ps, z, ident, shared["zT_done"])
                pe.wait_ge(shared["zT_ready"], 2)
                pe.wait_ge(E["w_loaded"], 48)
                for bank, n in ((1, "wq"), (2, "wk")):
                    for e in range(DC):
                        for c in range(DC):
                            nc.tensor.matmul(ps[:, bank, e * S:(e + 1) * S], w[n][:, c, e * P:(e + 1) * P], zT[:, c, :],
                                             start=(c == 0), stop=(c == DC - 1))
                for c in range(DC):
                    mm = nc.tensor.matmul(ps[:, 3, 0:D], zT[:, c, :], w["wv"][:, c, :], start=(c == 0), stop=(c == DC - 1))
                mm.then_inc(E["proj_done"], 1)
                pe.wait_ge(E["q_ready"], 2)
                pe.wait_ge(E["kv_ready"], 2)
                for c in range(DC):
                    mm = nc.tensor.matmul(ps[:, 4, 0:S], qT[:, c, :], kT[:, c, :], start=(c == 0), stop=(c == DC - 1))
                mm.then_inc(shared["logits_done"], 1)
                pe.wait_ge(shared["exp_ready"], 1)
                nc.tensor.transpose(ps[:, 5, 0:S], p[:, :], ident[:, :]).then_inc(shared["turned"], 1)
                pe.wait_ge(shared["turned_copied"], 1)
                nc.tensor.matmul(ps[:, 6, 0:D], pT[:, :], val[:, :], start=True, stop=True).then_inc(shared["out_done"], 1)


ROUND = 12582912.0


def quantise_rows(v, link, q, src, am, inv):
    link(v.tensor_reduce(am[:, 0:1], src, AX.X, ALU.max, apply_absolute_value=True))
    link(v.tensor_scalar(am[:, 0:1], am[:, 0:1], 1e-5, None, ALU.max))
    link(v.reciprocal(am[:, 1:2], am[:, 0:1]))
    link(v.tensor_scalar(am[:, 1:2], am[:, 1:2], 127.0, None, ALU.mult))
    link(v.tensor_scalar(inv, am[:, 0:1], 1.0 / 127.0, None, ALU.mult))
    link(v.tensor_scalar(q, src, am[:, 1:2], ROUND, ALU.mult, ALU.add))
    link(v.tensor_scalar(q, q, ROUND, 127.0, ALU.subtract, ALU.min))
    return v.tensor_scalar(q, q, -128.0, None, ALU.max)


def ternary_ffn(nc, a, sb, sem, base, links, shared):
    x, z, y, zT, ident, st, stats, rows, cols, ps = base
    vlink, alink, plink = links
    F = INNER
    with ExitStack() as own:
        def t(name, shape, dt=F32):
            return sb("tf_" + name, shape, dt, own)

        names = ("gate", "up", "down")
        w = {n: t(n, [P, 2 * F]) for n in names}
        wq = {n: t(n + "_q", [P, 2 * F], BF16) for n in names}
        wsum, mean, inv_mean = t("wsum", [P, 3]), t("mean", [P, 3]), t("inv_mean", [P, 3])
        ones = t("ones", [P, P])
        zqT = t("zqT", [P, DC, S], BF16)
        am, inv, sg = t("am", [P, 2]), t("inv", [P, 2]), t("sg", [P, 4])
        e, h, hqT = t("e", [P, F]), t("h", [P, F]), t("hqT", [P, 8, S], BF16)
        E = {n: sem("tf_" + n) for n in ("w_gate", "w_up", "w_down", "wsum_ready", "ones_ready", "sums_done", "mean_ready",
                                         "scaled", "wq_ready", "gu_done", "sg_ready",
                                         "e_ready", "hq_ready", "hT_done", "hT_ready", )}
        with nc.Block() as block:
            @block.sync
            def _(sp):
                for n in names:
                    c = 8 if n == "down" else DC
                    sp.dma_start(w[n][:, :].rearrange("p (c n) -> p c n", c=c),
                                 a["tf_" + n].rearrange("(c p) n -> p c n", p=P)).then_inc(E["w_" + n], 16)

            @block.gpsimd
            def _(pool):
                link = plink.on(pool)
                nc.gpsimd.memset(ones[:, :], 1.0).then_inc(E["ones_ready"], 1)
                for k, n in enumerate(names):
                    pool.wait_ge(E["scaled"], k + 1)
                    link(nc.gpsimd.tensor_scalar(w[n][:, :], w[n][:, :], -ROUND, 1.0, ALU.add, ALU.min))
                    nc.gpsimd.tensor_scalar(wq[n][:, :], w[n][:, :], -1.0, None, ALU.max).then_inc(E["wq_ready"], 1)

            @block.scalar
            def _(act):
                link = alink.on(act)
                act.wait_ge(E["mean_ready"], 1)
                for k, n in enumerate(names):
                    link(nc.scalar.activation(w[n][:, :], w[n][:, :], ACT.Copy, scale=inv_mean[:, k:k + 1]))
                    nc.scalar.activation(w[n][:, :], w[n][:, :], ACT.Copy, bias=ROUND).then_inc(E["scaled"], 1)
                act.wait_ge(E["sg_ready"], 1)
                act.wait_ge(E["gu_done"], 1)
                nc.scalar.activation(e[:, :].rearrange("p (b n) -> p b n", b=2), ps[:, 0:2, :], ACT.Exp, scale=sg[:, 2:3]).then_inc(E["e_ready"], 1)
                for k in range(2):
                    act.wait_ge(E["hT_done"], k + 1)
                    nc.scalar.activation(hqT[:, 4 * k:4 * k + 4, :], ps[:, 5 + k, :].rearrange("p (j s) -> p j s", j=4), ACT.Copy).then_inc(E["hT_ready"], 1)

            @block.vector
            def _(v):
                link = vlink.on(v)
                for k, n in enumerate(names):
                    v.wait_ge(E["w_" + n], 16)
                    nc.vector.tensor_reduce(wsum[:, k:k + 1], w[n][:, :], AX.X, ALU.add, apply_absolute_value=True).then_inc(E["wsum_ready"], 1)
                v.wait_ge(E["sums_done"], 1)
                link(nc.vector.tensor_scalar(mean[:, :], ps[:, 7, 0:3], 1.0 / (D * F), 1e-5, ALU.mult, ALU.max))
                nc.vector.reciprocal(inv_mean[:, :], mean[:, :]).then_inc(E["mean_ready"], 1)
                link(layer_norm(nc.vector, link, z[:, :], x[:, :], st, stats))
                quantise_rows(nc.vector, link, y[:, :], z[:, :], am, inv[:, 0:1]).then_inc(shared["z_ready"], 1)
                link(nc.vector.tensor_tensor(sg[:, 0:2], mean[:, 0:2], inv[:, 0:1].to_broadcast([P, 2]), ALU.mult))
                nc.vector.tensor_scalar(sg[:, 2:3], sg[:, 0:1], -1.0, None, ALU.mult).then_inc(E["sg_ready"], 1)
                v.wait_ge(shared["zT_done"], 3)
                nc.vector.tensor_copy(zqT[:, :, :], ps[:, 0, 0:DC * S].rearrange("p (c s) -> p c s", c=DC)).then_inc(shared["zT_ready"], 1)
                v.wait_ge(E["e_ready"], 1)
                link(nc.vector.tensor_scalar(e[:, :], e[:, :], 1.0, None, ALU.add))
                link(nc.vector.reciprocal(e[:, :], e[:, :]))
                gp = ps[:, 0:2, :].rearrange("p b n -> p (b n)")
                up = ps[:, 2:4, :].rearrange("p b n -> p (b n)")
                link(nc.vector.scalar_tensor_tensor(out=e[:, :], in0=gp, scalar=sg[:, 0:1], in1=e[:, :], op0=ALU.mult, op1=ALU.mult))
                link(nc.vector.scalar_tensor_tensor(out=h[:, :], in0=up, scalar=sg[:, 1:2], in1=e[:, :], op0=ALU.mult, op1=ALU.mult))
                quantise_rows(nc.vector, link, h[:, :], h[:, :], am, inv[:, 1:2]).then_inc(E["hq_ready"], 1)
                link(nc.vector.tensor_tensor(sg[:, 3:4], mean[:, 2:3], inv[:, 1:2], ALU.mult))
                v.wait_ge(shared["out_done"], 3)
                link(nc.vector.scalar_tensor_tensor(out=x[:, :], in0=ps[:, 4, 0:D], scalar=sg[:, 3:4], in1=x[:, :],
                                                    op0=ALU.mult, op1=ALU.add))

            @block.tensor
            def _(pe):
                pe.wait_ge(E["ones_ready"], 1)
                pe.wait_ge(E["wsum_ready"], 3)
                nc.tensor.matmul(ps[:, 7, 0:3], ones[:, :], wsum[:, :], start=True, stop=True).then_inc(E["sums_done"], 1)
                pe.wait_ge(shared["z_ready"], 3)
                transpose_z(nc, pe, ps, y, ident, shared["zT_done"])
                pe.wait_ge(shared["zT_ready"], 3)
                for k, n in enumerate(("gate", "up")):
                    pe.wait_ge(E["wq_ready"], k + 1)
                    for b in range(2):
                        for c in range(DC):
                            mm = nc.tensor.matmul(ps[:, 2 * k + b, :], zqT[:, c, :], wq[n][:, c * F + 512 * b:c * F + 512 * b + 512],
                                                  start=(c == 0), stop=(c == DC - 1))
                mm.then_inc(E["gu_done"], 1)
                pe.wait_ge(E["hq_ready"], 1)
                for k in range(2):
                    for j in range(4):
                        mm = nc.tensor.transpose(ps[:, 5 + k, j * S:(j + 1) * S], h[:, (4 * k + j) * P:(4 * k + j + 1) * P], ident[:, :])
                    mm.then_inc(E["hT_done"], 1)
                pe.wait_ge(E["wq_ready"], 3)
                for j in range(8):
                    if j % 4 == 0:
                        pe.wait_ge(E["hT_ready"], j // 4 + 1)
                    mm = nc.tensor.matmul(ps[:, 4, 0:D], hqT[:, j, :], wq["down"][:, j * D:(j + 1) * D], start=(j == 0), stop=(j == 7))
                mm.then_inc(shared["out_done"], 1)


def second_cross_attention(nc, a, sb, sem, base, links, shared):
    x, z, y, zT, ident, st, stats, rows, cols, ps = base
    vlink, alink, plink = links
    CW = D + 2
    with ExitStack() as own:
        def t(name, shape, dt=F32):
            return sb("xa_" + name, shape, dt, own)

        w = {n: t(n, [P, DC, D]) for n in ("wq", "wkT", "wv")}
        qT, q2T = t("qT", [P, DC, S]), t("q2T", [P, DC, S])
        lim = t("lim", [P, 2])
        sc = t("sc", [P, SK])
        chunk_max, top, neg_top = t("chunk_max", [P, NCH]), t("top", [P, 1]), t("neg_top", [P, 1])
        ct = t("ct", [P, 2, DC, CH])
        cn = t("cn", [P, 2, TILES, CW])
        p = t("p", [P, 2, CH])
        pT = t("pT", [P, 2, TILES, S])
        rec, u, uT = t("rec", [P, 1]), t("u", [P, D]), t("uT", [P, DC, S])
        E = {n: sem("xa_" + n) for n in ("w_loaded", "q_done", "q_ready", "q2_done", "q2_ready",
                                         "lim_ready", "scores_done", "max_done", "clipped", "top_ready", "p_ready",
                                         "t0_done", "t1_done", "pT0_ready", "pT1_ready", "weighed", "u_ready",
                                         "ones_ready")}
        ct_loaded = [sem("xa_ct_loaded0"), sem("xa_ct_loaded1")]
        cn_loaded = [sem("xa_cn_loaded0"), sem("xa_cn_loaded1")]
        ctxT = a["ctxT"].rearrange("(c p) k -> p c k", p=P)
        ctxN = a["ctx"].rearrange("(n t p) d -> n p t d", t=TILES, p=P)
        sc_ps = [ps[:, 2:4, 0:HCH], ps[:, 4:6, 0:HCH]]
        t_ps = [ps[:, 4, :], ps[:, 5, :]]

        def chunk_pairs(engine, two_chunks):
            two_chunks(0, True)
            with engine.Fori(1, NCH // 2) as i:
                two_chunks(i, False)

        with nc.Block() as block:
            @block.sync
            def _(sp):
                for n in ("wq", "wkT", "wv"):
                    sp.dma_start(w[n][:, :, :], a["xa_" + n].rearrange("(c p) n -> p c n", p=P)).then_inc(E["w_loaded"], 16)

                def two_chunks(i, first):
                    for par in range(2):
                        at_least(sp, E["scores_done"], i * 2 + (par - 1))
                        sp.dma_start(ct[:, par, :, :], ctxT[:, :, bass.ds((i * 2 + par) * CH, CH)]).then_inc(ct_loaded[par], 16)

                def context_rows(i, first):
                    for par in range(2):
                        at_least(sp, E["weighed"], i * 2 + (par - 1))
                        sp.dma_start(cn[:, par, :, 0:D], ctxN[bass.ds(i * 2 + par, 1), :, :, :].rearrange("o p t d -> p (o t) d")
                                     if not first else ctxN[par]).then_inc(cn_loaded[par], 16)

                chunk_pairs(sp, two_chunks)
                chunk_pairs(sp, context_rows)

            @block.gpsimd
            def _(pool):
                nc.gpsimd.memset(cn[:, :, :, D:CW], 1.0).then_inc(E["ones_ready"], 1)


            @block.scalar
            def _(act):
                link = alink.on(act)
                act.wait_ge(shared["zT_done"], 4)
                nc.scalar.activation(zT[:, :, :], ps[:, 0, 0:DC * S].rearrange("p (c s) -> p c s", c=DC), ACT.Copy).then_inc(shared["zT_ready"], 1)
                act.wait_ge(E["q2_done"], 1)
                nc.scalar.activation(q2T[:, :, :], ps[:, 2, 0:DC * S].rearrange("p (c s) -> p c s", c=DC), ACT.Copy).then_inc(E["q2_ready"], 1)
                act.wait_ge(E["top_ready"], 1)

                def two_chunks(i, first):
                    for par in range(2):
                        c = i * 2 + par
                        at_least(act, E["t1_done"], c - 1)
                        nc.scalar.activation(p[:, par, :], sc[:, bass.ds(c * CH, CH)], ACT.Exp, bias=neg_top[:, 0:1]).then_inc(E["p_ready"], 1)
                        act.wait_ge(E["t1_done"], c + 1)
                        at_least(act, E["weighed"], c - 1)
                        nc.scalar.activation(pT[:, par, T0:TILES, :], t_ps[1][:, 0:(TILES - T0) * S].rearrange("p (t s) -> p t s", s=S),
                                             ACT.Copy).then_inc(E["pT1_ready"], 1)

                chunk_pairs(act, two_chunks)
                act.wait_ge(shared["turned"], 2)
                nc.scalar.activation(uT[:, :, :], ps[:, 0, 0:DC * S].rearrange("p (c s) -> p c s", c=DC), ACT.Copy).then_inc(shared["turned_copied"], 1)

            @block.vector
            def _(v):
                link = vlink.on(v)
                layer_norm(nc.vector, link, z[:, :], x[:, :], st, stats).then_inc(shared["z_ready"], 1)
                v.wait_ge(E["q_done"], 1)
                link(nc.vector.tensor_tensor(qT[:, :, :], ps[:, 1, 0:DC * S].rearrange("p (c s) -> p c s", c=DC),
                                             cols[:, C_X_BQ:C_X_BQ + DC].unsqueeze(2).to_broadcast([P, DC, S]), ALU.add))
                nc.vector.tensor_scalar(qT[:, :, :], qT[:, :, :], D ** -0.5, None, ALU.mult).then_inc(E["q_ready"], 1)
                v.wait_ge(E["q2_done"], 1)
                nc.vector.tensor_scalar(lim[:, 0:1], ps[:, 6, 0:1], -1.0, -100.0, ALU.mult, ALU.add).then_inc(E["lim_ready"], 1)
                nc.vector.tensor_scalar(lim[:, 1:2], ps[:, 6, 0:1], -1.0, 100.0, ALU.mult, ALU.add).then_inc(E["lim_ready"], 1)
                v.wait_ge(E["lim_ready"], 2)

                def two_chunks(i, first):
                    for par in range(2):
                        c = i * 2 + par
                        v.wait_ge(E["scores_done"], c + 1)
                        nc.vector.tensor_reduce(chunk_max[:, bass.ds(c, 1)], sc_ps[par], AX.XY, ALU.max).then_inc(E["max_done"], 1)
                        nc.vector.tensor_scalar(sc[:, bass.ds(c * CH, CH)].rearrange("p (b k) -> p b k", b=2), sc_ps[par],
                                                lim[:, 0:1], lim[:, 1:2], ALU.max, ALU.min).then_inc(E["clipped"], 1)

                chunk_pairs(v, two_chunks)
                v.wait_ge(E["max_done"], NCH)
                link(nc.vector.tensor_reduce(top[:, :], chunk_max[:, :], AX.X, ALU.max))
                link(nc.vector.tensor_scalar(top[:, :], top[:, :], lim[:, 0:1], lim[:, 1:2], ALU.max, ALU.min))
                v.wait_ge(E["clipped"], NCH)
                nc.vector.tensor_scalar(neg_top[:, :], top[:, :], -1.0, None, ALU.mult).then_inc(E["top_ready"], 1)

                def two_more(i, first):
                    for par in range(2):
                        c = i * 2 + par
                        v.wait_ge(E["t0_done"], c + 1)
                        at_least(v, E["weighed"], c - 1)
                        nc.vector.tensor_copy(pT[:, par, 0:T0, :], t_ps[0].rearrange("p (t s) -> p t s", s=S)).then_inc(E["pT0_ready"], 1)

                chunk_pairs(v, two_more)
                v.wait_ge(E["weighed"], NCH)
                link(nc.vector.reciprocal(rec[:, :], ps[:, 7, D:D + 1]))
                nc.vector.tensor_scalar(u[:, :], ps[:, 7, 0:D], rec[:, 0:1], None, ALU.mult).then_inc(E["u_ready"], 1)
                link(nc.vector.tensor_tensor(x[:, :], x[:, :], rows[:, R_X_BV, :], ALU.add))
                v.wait_ge(shared["out_done"], 4)
                link(nc.vector.tensor_tensor(x[:, :], ps[:, 1, 0:D], x[:, :], ALU.add))

            @block.tensor
            def _(pe):
                pe.wait_ge(shared["z_ready"], 4)
                transpose_z(nc, pe, ps, z, ident, shared["zT_done"])
                pe.wait_ge(shared["zT_ready"], 4)
                pe.wait_ge(E["w_loaded"], 48)
                for e in range(DC):
                    for c in range(DC):
                        mm = nc.tensor.matmul(ps[:, 1, e * S:(e + 1) * S], w["wq"][:, c, e * P:(e + 1) * P], zT[:, c, :],
                                              start=(c == 0), stop=(c == DC - 1))
                mm.then_inc(E["q_done"], 1)
                pe.wait_ge(E["q_ready"], 1)
                for c in range(DC):
                    nc.tensor.matmul(ps[:, 6, 0:1], qT[:, c, :], cols[:, C_X_BK + c:C_X_BK + c + 1], start=(c == 0), stop=(c == DC - 1))
                for e in range(DC):
                    for c in range(DC):
                        mm = nc.tensor.matmul(ps[:, 2, e * S:(e + 1) * S], w["wkT"][:, c, e * P:(e + 1) * P], qT[:, c, :],
                                              start=(c == 0), stop=(c == DC - 1))
                mm.then_inc(E["q2_done"], 1)
                pe.wait_ge(E["q2_ready"], 1)

                def two_chunks(i, first):
                    for par in range(2):
                        c = i * 2 + par
                        pe.wait_ge(ct_loaded[par], i * 16 + 16)
                        at_least(pe, E["clipped"], c - 1)
                        for k in range(DC):
                            for b in range(2):
                                mm = nc.tensor.matmul(sc_ps[par][:, b, :], q2T[:, k, :], ct[:, par, k, b * HCH:(b + 1) * HCH],
                                                      start=(k == 0), stop=(k == DC - 1))
                        mm.then_inc(E["scores_done"], 1)

                chunk_pairs(pe, two_chunks)
                pe.wait_ge(E["ones_ready"], 1)
                pe.wait_ge(E["clipped"], NCH)

                def turn(c, par):
                    pe.wait_ge(E["p_ready"], c + 1)
                    at_least(pe, E["pT0_ready"], c)
                    at_least(pe, E["pT1_ready"], c)
                    for tile in range(TILES):
                        b, s = (0, tile) if tile < T0 else (1, tile - T0)
                        mm = nc.tensor.transpose(t_ps[b][:, s * S:(s + 1) * S], p[:, par, tile * P:(tile + 1) * P], ident[:, :])
                        if tile == T0 - 1:
                            mm.then_inc(E["t0_done"], 1)
                    mm.then_inc(E["t1_done"], 1)

                def weigh(c, par, loads, start):
                    pe.wait_ge(cn_loaded[par], loads)
                    pe.wait_ge(E["pT0_ready"], c + 1)
                    pe.wait_ge(E["pT1_ready"], c + 1)
                    for tile in range(TILES):
                        mm = nc.tensor.matmul(ps[:, 7, 0:D + 2], pT[:, par, tile, :], cn[:, par, tile, 0:D + 2],
                                              start=(start and tile == 0), stop=True, skip_group_check=True)
                    mm.then_inc(E["weighed"], 1)

                turn(0, 0)
                turn(1, 1)
                weigh(0, 0, 16, True)
                with pe.Fori(1, NCH // 2) as i:
                    turn(i * 2, 0)
                    weigh(i * 2 - 1, 1, i * 16, False)
                    turn(i * 2 + 1, 1)
                    weigh(i * 2, 0, i * 16 + 16, False)
                weigh(NCH - 1, 1, NCH // 2 * 16, False)
                pe.wait_ge(E["u_ready"], 1)
                for c in range(DC):
                    mm = nc.tensor.transpose(ps[:, 0, c * S:(c + 1) * S], u[:, c * P:(c + 1) * P], ident[:, :])
                mm.then_inc(shared["turned"], 1)
                pe.wait_ge(shared["turned_copied"], 2)
                for c in range(DC):
                    mm = nc.tensor.matmul(ps[:, 1, 0:D], uT[:, c, :], w["wv"][:, c, :], start=(c == 0), stop=(c == DC - 1))
                mm.then_inc(shared["out_done"], 1)


NS = 32
RANK = 16
CI = 512
CT = CI // P
TAPS = 4
HALF_N = 16


def selective_scan(nc, a, sb, sem, base, links, shared):
    x, z, y, zT, ident, st, stats, rows, cols, ps = base
    vlink, alink, plink = links
    with ExitStack() as own:
        def t(name, shape, dt=F32):
            return sb("ss_" + name, shape, dt, own)

        ip = t("in_proj", [P, DC, 2 * CI])
        op = t("out_proj", [P, CT, D])
        xp = t("x_proj", [P, CT, RANK + 2 * NS])
        dp = t("dt_proj", [RANK, CI])
        cw, al = t("conv_w", [P, CT, TAPS]), t("a_log", [P, CT, NS])
        up = t("up", [P, CT, TAPS - 1 + S])
        u, th, zg = t("u", [P, CT, S]), t("th", [P, CT, S]), t("zg", [P, CT, S])
        dbl = t("dbl", [RANK + 2 * NS, S])
        dt_, e, r, r2, du = (t(n, [P, CT, S]) for n in ("dt", "e", "r", "r2", "du"))
        b_all, c_all = t("b_all", [P, NS, S]), t("c_all", [P, NS, S])
        arg = t("arg", [P, 2, NS, S])
        decay = t("decay", [P, 2, NS, S])
        h = t("h", [P, NS, S])
        ys = t("ys", [P, CT, S])
        E = {n: sem("ss_" + n) for n in ("ip_loaded", "op_loaded", "xp_loaded", "small_loaded", "uz_done",
                                         "up_ready", "zero_ready", "conv", "conv_done", "th_ready", "u_ready", "dbl_done", "dbl_ready",
                                         "dt_done", "abs_ready", "e_ready", "dt_ready", "al_ready", "bc_done", "bc_ready",
                                         "arg_ready", "decay_ready", "zero_col", "driven", "scanned", "read", "summed", "zth_ready",
                                         "sum_copied", "y_ready", )}
        with nc.Block() as block:
            @block.sync
            def _(sp):
                sp.dma_start(ip[:, :, :], a["ss_in"].rearrange("(c p) n -> p c n", p=P)).then_inc(E["ip_loaded"], 16)
                sp.dma_start(cw[:, :, :], a["ss_conv"].rearrange("(j p) k -> p j k", p=P)).then_inc(E["small_loaded"], 16)
                sp.dma_start(xp[:, :, :], a["ss_x"].rearrange("(j p) k -> p j k", p=P)).then_inc(E["xp_loaded"], 16)
                sp.dma_start(dp[:, :], a["ss_dt"]).then_inc(E["xp_loaded"], 16)
                sp.dma_start(al[:, :, :], a["ss_alog"].rearrange("(j p) k -> p j k", p=P)).then_inc(E["small_loaded"], 16)
                sp.dma_start(op[:, :, :], a["ss_out"].rearrange("(j p) n -> p j n", p=P)).then_inc(E["op_loaded"], 16)

            @block.gpsimd
            def _(pool):
                link = plink.on(pool)
                nc.gpsimd.memset(up[:, :, 0:TAPS - 1], 0.0).then_inc(E["zero_ready"], 1)
                nc.gpsimd.memset(decay[:, :, :, 0:1], 0.0).then_inc(E["zero_col"], 1)
                pool.wait_ge(E["al_ready"], 1)
                pool.wait_ge(E["dt_ready"], 1)
                for j in range(CT):
                    at_least(pool, E["decay_ready"], j - 1)
                    nc.gpsimd.tensor_tensor(arg[:, j % 2, :, :], dt_[:, j, :].unsqueeze(1).to_broadcast([P, NS, S]),
                                            al[:, j, :].unsqueeze(2).to_broadcast([P, NS, S]), ALU.mult).then_inc(E["arg_ready"], 1)

            @block.scalar
            def _(act):
                link = alink.on(act)
                act.wait_ge(shared["zT_done"], 5)
                nc.scalar.activation(zT[:, :, :], ps[:, 0, 0:DC * S].rearrange("p (c s) -> p c s", c=DC), ACT.Copy).then_inc(shared["zT_ready"], 1)
                act.wait_ge(E["small_loaded"], 32)
                nc.scalar.activation(al[:, :, :], al[:, :, :], ACT.Exp).then_inc(E["al_ready"], 1)
                act.wait_ge(E["uz_done"], 1)
                nc.scalar.activation(up[:, :, TAPS - 1:], ps[:, 1, :].rearrange("p (j s) -> p j s", j=CT), ACT.Copy).then_inc(E["up_ready"], 1)
                nc.scalar.activation(zg[:, :, :], ps[:, 2, :].rearrange("p (j s) -> p j s", j=CT), ACT.Tanh, scale=0.5).then_inc(E["zth_ready"], 1)
                act.wait_ge(E["conv_done"], CT)
                nc.scalar.activation(th[:, :, :], u[:, :, :], ACT.Tanh, scale=0.5).then_inc(E["th_ready"], 1)
                act.wait_ge(E["dbl_done"], 1)
                nc.scalar.activation(dbl[:, :], ps[0:RANK + 2 * NS, 3, 0:S], ACT.Copy).then_inc(E["dbl_ready"], 1)
                act.wait_ge(E["abs_ready"], 1)
                link(nc.scalar.activation(e[:, :, :], r[:, :, :], ACT.Abs))
                nc.scalar.activation(e[:, :, :], e[:, :, :], ACT.Exp, scale=-1.0).then_inc(E["e_ready"], 1)
                for k in range(2 * NS // 4):
                    act.wait_ge(E["bc_done"], k + 1)
                    dst = b_all if k < NS // 4 else c_all
                    n = 4 * (k % (NS // 4))
                    nc.scalar.activation(dst[:, n:n + 4, :], ps[:, 5 + k % 3, :].rearrange("p (n s) -> p n s", n=4), ACT.Copy).then_inc(E["bc_ready"], 1)
                act.wait_ge(E["zero_col"], 1)
                for j in range(CT):
                    act.wait_ge(E["arg_ready"], j + 1)
                    at_least(act, E["scanned"], j - 1)
                    nc.scalar.activation(decay[:, j % 2, :, 1:S], arg[:, j % 2, :, 1:S], ACT.Exp, scale=-1.0).then_inc(E["decay_ready"], 1)

            @block.vector
            def _(v):
                link = vlink.on(v)
                link(layer_norm(nc.vector, link, z[:, :], x[:, :], st, stats))
                link(nc.vector.bn_stats(stats[:, :], z[:, :]))
                link(nc.vector.bn_aggr(st[:, 0:2], stats[:, :]))
                link(nc.vector.scalar_tensor_tensor(out=st[:, 1:2], in0=st[:, 0:1], scalar=st[:, 0:1], in1=st[:, 1:2], op0=ALU.mult, op1=ALU.add))
                layer_norm_scale(nc.vector, link, st, 1e-6)
                nc.vector.scalar_tensor_tensor(out=y[:, :], in0=z[:, :], scalar=st[:, 3:4], in1=rows[:, R_RMS_W, :],
                                               op0=ALU.mult, op1=ALU.mult).then_inc(shared["z_ready"], 1)
                link(nc.vector.tensor_tensor(x[:, :], x[:, :], z[:, :], ALU.add))
                v.wait_ge(E["up_ready"], 1)
                v.wait_ge(E["zero_ready"], 1)
                for k in range(TAPS):
                    for j in range(CT):
                        src, wk = up[:, j, k:k + S], cw[:, j, k:k + 1]
                        if k == 0:
                            nc.vector.tensor_scalar(u[:, j, :], src, wk, cols[:, C_CONVB + j:C_CONVB + j + 1], ALU.mult, ALU.add).then_inc(E["conv"], 1)
                        else:
                            v.wait_ge(E["conv"], (k - 1) * CT + j + 1)
                            nc.vector.scalar_tensor_tensor(out=u[:, j, :], in0=src, scalar=wk, in1=u[:, j, :], op0=ALU.mult,
                                                           op1=ALU.add).then_inc(E["conv_done" if k == TAPS - 1 else "conv"], 1)
                v.wait_ge(E["th_ready"], 1)
                link(nc.vector.scalar_tensor_tensor(out=u[:, :, :], in0=th[:, :, :], scalar=1.0, in1=u[:, :, :], op0=ALU.add, op1=ALU.mult))
                nc.vector.tensor_scalar(u[:, :, :], u[:, :, :], 0.5, None, ALU.mult).then_inc(E["u_ready"], 1)
                v.wait_ge(E["dt_done"], 1)
                nc.vector.tensor_tensor(r[:, :, :], ps[:, 4, :].rearrange("p (j s) -> p j s", j=CT),
                                        cols[:, C_DTB:C_DTB + CT].unsqueeze(2).to_broadcast([P, CT, S]), ALU.add).then_inc(E["abs_ready"], 1)
                v.wait_ge(E["e_ready"], 1)
                link(nc.vector.tensor_scalar(dt_[:, :, :], e[:, :, :], 2.0, None, ALU.add))
                link(nc.vector.reciprocal(dt_[:, :, :], dt_[:, :, :]))
                link(nc.vector.tensor_tensor(e[:, :, :], e[:, :, :], dt_[:, :, :], ALU.mult))
                link(nc.vector.tensor_tensor(r2[:, :, :], e[:, :, :], e[:, :, :], ALU.mult))
                link(nc.vector.tensor_scalar(dt_[:, :, :], r2[:, :, :], 1.0 / 15, 1.0 / 13, ALU.mult, ALU.add))
                link(nc.vector.tensor_tensor(dt_[:, :, :], dt_[:, :, :], r2[:, :, :], ALU.mult))
                for k in (11, 9, 7, 5, 3):
                    link(nc.vector.scalar_tensor_tensor(out=dt_[:, :, :], in0=dt_[:, :, :], scalar=1.0 / k, in1=r2[:, :, :], op0=ALU.add, op1=ALU.mult))
                link(nc.vector.scalar_tensor_tensor(out=dt_[:, :, :], in0=dt_[:, :, :], scalar=1.0, in1=e[:, :, :], op0=ALU.add, op1=ALU.mult))
                link(nc.vector.tensor_scalar(r[:, :, :], r[:, :, :], 0.0, None, ALU.max))
                link(nc.vector.scalar_tensor_tensor(out=dt_[:, :, :], in0=dt_[:, :, :], scalar=2.0, in1=r[:, :, :], op0=ALU.mult, op1=ALU.add))
                nc.vector.tensor_tensor(du[:, :, :], dt_[:, :, :], u[:, :, :], ALU.mult).then_inc(E["dt_ready"], 1)
                v.wait_ge(E["dt_ready"], 1)
                for j in range(CT):
                    if j == 0:
                        v.wait_ge(E["bc_ready"], NS // 4)
                    at_least(v, E["summed"], j)
                    nc.vector.tensor_tensor(h[:, :, :], du[:, j, :].unsqueeze(1).to_broadcast([P, NS, S]), b_all[:, :, :], ALU.mult).then_inc(E["driven"], 1)
                    v.wait_ge(E["decay_ready"], j + 1)
                    v.wait_ge(E["driven"], j + 1)
                    flat = "p n s -> p (n s)"
                    nc.vector.tensor_tensor_scan(h[:, :, :].rearrange(flat), decay[:, j % 2, :, :].rearrange(flat), h[:, :, :].rearrange(flat),
                                                 0.0, ALU.mult, ALU.add).then_inc(E["scanned"], 1)
                    v.wait_ge(E["scanned"], j + 1)
                    if j == 0:
                        v.wait_ge(E["bc_ready"], NS // 2)
                    nc.vector.tensor_tensor(h[:, :, :], h[:, :, :], c_all[:, :, :], ALU.mult).then_inc(E["read"], 1)
                    v.wait_ge(E["summed"], j + 1)
                    nc.vector.tensor_reduce(ys[:, j, :], ps[:, 3 + j % 2, :].rearrange("p (n s) -> p s n", n=4), AX.X, ALU.add).then_inc(E["sum_copied"], 1)
                v.wait_ge(E["sum_copied"], CT)
                link(nc.vector.tensor_tensor(u[:, :, :], u[:, :, :], cols[:, C_DPAR:C_DPAR + CT].unsqueeze(2).to_broadcast([P, CT, S]), ALU.mult))
                v.wait_ge(E["zth_ready"], 1)
                link(nc.vector.scalar_tensor_tensor(out=zg[:, :, :], in0=zg[:, :, :], scalar=1.0, in1=ps[:, 2, :].rearrange("p (j s) -> p j s", j=CT),
                                                    op0=ALU.add, op1=ALU.mult))
                link(nc.vector.tensor_tensor(ys[:, :, :], ys[:, :, :], u[:, :, :], ALU.add))
                nc.vector.scalar_tensor_tensor(out=ys[:, :, :], in0=ys[:, :, :], scalar=0.5, in1=zg[:, :, :], op0=ALU.mult,
                                               op1=ALU.mult).then_inc(E["y_ready"], 1)
                v.wait_ge(shared["out_done"], 5)
                link(nc.vector.tensor_tensor(x[:, :], ps[:, 0, 0:D], x[:, :], ALU.add))

            @block.tensor
            def _(pe):
                pe.wait_ge(shared["z_ready"], 5)
                transpose_z(nc, pe, ps, y, ident, shared["zT_done"])
                pe.wait_ge(shared["zT_ready"], 5)
                pe.wait_ge(E["ip_loaded"], 16)
                for half in range(2):
                    for j in range(CT):
                        for c in range(DC):
                            col = half * CI + j * P
                            mm = nc.tensor.matmul(ps[:, 1 + half, j * S:(j + 1) * S], ip[:, c, col:col + P], zT[:, c, :],
                                                  start=(c == 0), stop=(c == DC - 1))
                mm.then_inc(E["uz_done"], 1)
                pe.wait_ge(E["u_ready"], 1)
                pe.wait_ge(E["xp_loaded"], 32)
                for j in range(CT):
                    mm = nc.tensor.matmul(ps[0:RANK + 2 * NS, 3, 0:S], xp[:, j, :], u[:, j, :], start=(j == 0), stop=(j == CT - 1))
                mm.then_inc(E["dbl_done"], 1)
                pe.wait_ge(E["dbl_ready"], 1)
                for j in range(CT):
                    mm = nc.tensor.matmul(ps[:, 4, j * S:(j + 1) * S], dp[:, j * P:(j + 1) * P], dbl[0:RANK, :], start=True, stop=True)
                mm.then_inc(E["dt_done"], 1)
                for k in range(2 * NS // 4):
                    at_least(pe, E["bc_ready"], k - 2)
                    for i in range(4):
                        row = RANK + 4 * k + i
                        mm = nc.tensor.matmul(ps[:, 5 + k % 3, i * S:(i + 1) * S],
                                              ident[0:RANK + 2 * NS, row:row + 1].to_broadcast([RANK + 2 * NS, P]),
                                              dbl[:, :], start=True, stop=True)
                    mm.then_inc(E["bc_done"], 1)
                pe.wait_ge(E["abs_ready"], 1)
                for j in range(CT):
                    pe.wait_ge(E["read"], j + 1)
                    at_least(pe, E["sum_copied"], j - 1)
                    for k in range(NS // 4):
                        mm = nc.tensor.matmul(ps[:, 3 + j % 2, :], ident[:, :], h[:, 4 * k:4 * k + 4, :].rearrange("p n s -> p (n s)"),
                                              start=(k == 0), stop=(k == NS // 4 - 1))
                    mm.then_inc(E["summed"], 1)
                pe.wait_ge(E["y_ready"], 1)
                pe.wait_ge(E["op_loaded"], 16)
                for j in range(CT):
                    mm = nc.tensor.matmul(ps[:, 0, 0:D], ys[:, j, :], op[:, j, :], start=(j == 0), stop=(j == CT - 1))
                mm.then_inc(shared["out_done"], 1)


NE = 8
FE, FS = 768, 256


def expert_ffn(nc, a, sb, sem, base, links, shared):
    x, z, y, zT, ident, st, stats, rows, cols, ps = base
    vlink, alink, plink = links
    with ExitStack() as own:
        def t(name, shape, dt=F32):
            return sb("me_" + name, shape, dt, own)

        router = t("router", [P, DC, NE])
        w1 = t("w1", [P, 2, DC, 2 * FE])
        w2 = t("w2", [P, 2, FE // P, D])
        s1, s2 = t("s1", [P, DC, 2 * FS]), t("s2", [P, FS // P, D])
        pr, total, rec = t("pr", [P, NE]), t("total", [P, 1]), t("rec", [P, 4])
        cmp, eq = t("cmp", [P, NE, NE]), t("eq", [P, NE, NE])
        before = t("before", [P, NE, NE])
        rank, pick, comb = t("rank", [P, NE]), t("pick", [P, 2, NE]), t("comb", [P, NE])
        best = t("best", [P, 2])
        th, hT = t("th", [P, 2, FE]), t("hT", [P, 2, FE])
        E = {n: sem("me_" + n) for n in ("router_loaded", "s_loaded", "before_ready", "best_ready", "ex_ready", "comb_ready", "up_done", "th_ready", "h_ready",
                                         "down_done", "added", "silu")}
        w1_loaded = [sem("me_w1_loaded0"), sem("me_w1_loaded1")]
        w2_loaded = [sem("me_w2_loaded0"), sem("me_w2_loaded1")]
        w1_dram = a["me_w1"].rearrange("e (c p) n -> p e c n", p=P)
        w2_dram = a["me_w2"].rearrange("e (c p) n -> p e c n", p=P)
        gu = [ps[:, 0:3, :].rearrange("p b n -> p (b n)"), ps[:, 3:6, :].rearrange("p b n -> p (b n)")]

        with nc.Block() as block:
            @block.sync
            def _(sp):
                sp.dma_start(router[:, :, :], a["me_router"].rearrange("(c p) n -> p c n", p=P)).then_inc(E["router_loaded"], 16)
                sp.dma_start(s1[:, :, :], a["me_s1"].rearrange("(c p) n -> p c n", p=P)).then_inc(E["s_loaded"], 16)
                sp.dma_start(s2[:, :, :], a["me_s2"].rearrange("(c p) n -> p c n", p=P)).then_inc(E["s_loaded"], 16)

                def pair(i):
                    for par in range(2):
                        sp.wait_ge(E["up_done"], i * 2 + par)
                        sp.dma_start(w1[:, par, :, :], w1_dram[:, bass.ds(i * 2 + par, 1), :, :].rearrange("p o c n -> p (o c) n")).then_inc(w1_loaded[par], 16)
                        sp.wait_ge(E["down_done"], i * 2 + par)
                        sp.dma_start(w2[:, par, :, :], w2_dram[:, bass.ds(i * 2 + par, 1), :, :].rearrange("p o c n -> p (o c) n")).then_inc(w2_loaded[par], 16)

                for par in range(2):
                    sp.dma_start(w1[:, par, :, :], w1_dram[:, par, :, :]).then_inc(w1_loaded[par], 16)
                    sp.dma_start(w2[:, par, :, :], w2_dram[:, par, :, :]).then_inc(w2_loaded[par], 16)
                with sp.Fori(1, NE // 2) as i:
                    pair(i)

            @block.gpsimd
            def _(pool):
                link = plink.on(pool)
                link(nc.gpsimd.memset(before[:, :, :], 1.0))
                nc.gpsimd.affine_select(out=before[:, :, :], in_=before[:, :, :], compare_op=ALU.is_gt, fill=0.0, base=0,
                                        pattern=[[1, NE], [-1, NE]], channel_multiplier=0).then_inc(E["before_ready"], 1)

            @block.scalar
            def _(act):
                link = alink.on(act)
                act.wait_ge(shared["zT_done"], 6)
                nc.scalar.activation(zT[:, :, :], ps[:, 6, 0:DC * S].rearrange("p (c s) -> p c s", c=DC), ACT.Copy).then_inc(shared["zT_ready"], 1)
                act.wait_ge(shared["max_ready"], 2)
                nc.scalar.activation(pr[:, :], ps[:, 7, 0:NE], ACT.Exp, bias=rec[:, 0:1], accum_out=total[:, :]).then_inc(shared["exp_ready"], 1)

                def half_tanh(n, par, width):
                    act.wait_ge(E["up_done"], n + 1)
                    at_least(act, E["h_ready"], n - 1)
                    nc.scalar.activation(th[:, par, 0:width], gu[par][:, 0:width], ACT.Tanh, scale=0.5).then_inc(E["th_ready"], 1)

                half_tanh(0, 1, FS)
                act.wait_ge(E["best_ready"], 1)
                nc.scalar.activation(rec[:, 2:3], best[:, 1:2], ACT.Exp, bias=rec[:, 1:2]).then_inc(E["ex_ready"], 1)

                def pair(i):
                    for par in range(2):
                        half_tanh(i * 2 + (par + 1), par, FE)

                with act.Fori(0, NE // 2) as i:
                    pair(i)

            @block.vector
            def _(v):
                link = vlink.on(v)
                link(layer_norm(nc.vector, link, z[:, :], x[:, :], st, stats))
                link(layer_norm(nc.vector, link, y[:, :], z[:, :], st, stats))
                link(nc.vector.tensor_tensor(y[:, :], y[:, :], rows[:, R_F_G, :], ALU.mult))
                nc.vector.tensor_tensor(y[:, :], y[:, :], rows[:, R_F_B, :], ALU.add).then_inc(shared["z_ready"], 1)
                v.wait_ge(shared["logits_done"], 2)
                nc.vector.tensor_reduce(rec[:, 0:1], ps[:, 7, 0:NE], AX.X, ALU.max, negate=True).then_inc(shared["max_ready"], 1)
                v.wait_ge(shared["exp_ready"], 2)
                link(nc.vector.reciprocal(total[:, :], total[:, :]))
                link(nc.vector.tensor_scalar(pr[:, :], pr[:, :], total[:, 0:1], None, ALU.mult))
                mine = pr[:, :].unsqueeze(2).to_broadcast([P, NE, NE])
                other = pr[:, :].unsqueeze(1).to_broadcast([P, NE, NE])
                link(nc.vector.tensor_tensor(cmp[:, :, :], other, mine, ALU.is_gt))
                link(nc.vector.tensor_tensor(eq[:, :, :], other, mine, ALU.is_equal))
                v.wait_ge(E["before_ready"], 1)
                link(nc.vector.tensor_tensor(eq[:, :, :], eq[:, :, :], before[:, :, :], ALU.mult))
                link(nc.vector.tensor_tensor(cmp[:, :, :], cmp[:, :, :], eq[:, :, :], ALU.add))
                link(nc.vector.tensor_reduce(rank[:, :], cmp[:, :, :], AX.X, ALU.add))
                for k in range(2):
                    link(nc.vector.tensor_scalar(pick[:, k, :], rank[:, :], float(k), None, ALU.is_equal))
                    link(nc.vector.tensor_tensor(comb[:, :], pick[:, k, :], pr[:, :], ALU.mult))
                    link(nc.vector.tensor_reduce(best[:, k:k + 1], comb[:, :], AX.X, ALU.add))
                nc.vector.tensor_scalar(rec[:, 1:2], best[:, 0:1], -1.0, None, ALU.mult).then_inc(E["best_ready"], 1)
                v.wait_ge(E["ex_ready"], 1)
                link(nc.vector.tensor_scalar(rec[:, 3:4], rec[:, 2:3], 1.0, None, ALU.add))
                link(nc.vector.reciprocal(rec[:, 3:4], rec[:, 3:4]))
                link(nc.vector.tensor_tensor(rec[:, 2:3], rec[:, 2:3], rec[:, 3:4], ALU.mult))
                link(nc.vector.tensor_scalar(comb[:, :], pick[:, 0, :], rec[:, 3:4], None, ALU.mult))
                link(nc.vector.scalar_tensor_tensor(out=comb[:, :], in0=pick[:, 1, :], scalar=rec[:, 2:3], in1=comb[:, :], op0=ALU.mult, op1=ALU.add))

                def hidden(n, par, width):
                    v.wait_ge(E["th_ready"], n + 1)
                    nc.vector.scalar_tensor_tensor(out=th[:, par, 0:width], in0=th[:, par, 0:width], scalar=1.0, in1=gu[par][:, 0:width],
                                                   op0=ALU.add, op1=ALU.mult).then_inc(E["silu"], 1)
                    v.wait_ge(E["silu"], n + 1)
                    at_least(v, E["down_done"], n - 1)
                    nc.vector.scalar_tensor_tensor(out=hT[:, par, 0:width], in0=th[:, par, 0:width], scalar=0.5, in1=gu[par][:, width:2 * width],
                                                   op0=ALU.mult, op1=ALU.mult).then_inc(E["h_ready"], 1)

                def weigh(n, bank, scalar):
                    v.wait_ge(E["down_done"], n + 1)
                    at_least(v, E["added"], n)
                    nc.vector.scalar_tensor_tensor(out=x[:, :], in0=ps[:, bank, 0:D], scalar=scalar, in1=x[:, :],
                                                   op0=ALU.mult, op1=ALU.add).then_inc(E["added"], 1)

                hidden(0, 1, FS)
                hidden(1, 0, FE)
                weigh(0, 7, 1.0)

                def pair(i, peeled):
                    hidden(i * 2 + 2, 1, FE)
                    weigh(i * 2 + 1, 6, comb[:, bass.ds(i * 2, 1)])
                    if not peeled:
                        hidden(i * 2 + 3, 0, FE)
                    weigh(i * 2 + 2, 7, comb[:, bass.ds(i * 2 + 1, 1)])

                with v.Fori(0, NE // 2 - 1) as i:
                    pair(i, False)
                pair(NE // 2 - 1, True)
                v.wait_ge(E["added"], NE + 1)

            @block.tensor
            def _(pe):
                pe.wait_ge(shared["z_ready"], 6)
                for c in range(DC):
                    mm = nc.tensor.transpose(ps[:, 6, c * S:(c + 1) * S], y[:, c * P:(c + 1) * P], ident[:, :])
                mm.then_inc(shared["zT_done"], 1)
                pe.wait_ge(shared["zT_ready"], 6)
                pe.wait_ge(E["router_loaded"], 16)
                for c in range(DC):
                    mm = nc.tensor.matmul(ps[:, 7, 0:NE], zT[:, c, :], router[:, c, :], start=(c == 0), stop=(c == DC - 1))
                mm.then_inc(shared["logits_done"], 1)

                def first_product(n, par, w, width):
                    at_least(pe, E["h_ready"], n - 1)
                    for j in range(2 * width // P):
                        for c in range(DC):
                            mm = nc.tensor.matmul(gu[par][:, j * P:(j + 1) * P], w[:, c, j * P:(j + 1) * P], zT[:, c, :],
                                                  start=(c == 0), stop=(c == DC - 1))
                    mm.then_inc(E["up_done"], 1)

                def second_product(n, par, w, width):
                    pe.wait_ge(E["h_ready"], n + 1)
                    at_least(pe, E["added"], n - 1)
                    for j in range(width // P):
                        mm = nc.tensor.matmul(ps[:, 7 - (1 - par), 0:D], hT[:, par, j * P:(j + 1) * P], w[:, j, :],
                                              start=(j == 0), stop=(j == width // P - 1))
                    mm.then_inc(E["down_done"], 1)

                pe.wait_ge(E["s_loaded"], 32)
                first_product(0, 1, s1, FS)
                pe.wait_ge(w1_loaded[0], 16)
                first_product(1, 0, w1[:, 0, :, :], FE)
                pe.wait_ge(shared["exp_ready"], 2)
                second_product(0, 1, s2, FS)

                def pair(i, peeled):
                    pe.wait_ge(w1_loaded[1], i * 16 + 16)
                    first_product(i * 2 + 2, 1, w1[:, 1, :, :], FE)
                    pe.wait_ge(w2_loaded[0], i * 16 + 16)
                    second_product(i * 2 + 1, 0, w2[:, 0, :, :], FE)
                    if not peeled:
                        pe.wait_ge(w1_loaded[0], i * 16 + 32)
                        first_product(i * 2 + 3, 0, w1[:, 0, :, :], FE)
                    pe.wait_ge(w2_loaded[1], i * 16 + 16)
                    second_product(i * 2 + 2, 1, w2[:, 1, :, :], FE)

                with pe.Fori(0, NE // 2 - 1) as i:
                    pair(i, False)
                pair(NE // 2 - 1, True)


_INS = {
    "ss_in": lambda i: i["L1_attn_in_proj_w"].T,
    "ss_conv": lambda i: i["L1_attn_conv_w"],
    "ss_x": lambda i: i["L1_attn_x_proj_w"].T,
    "ss_dt": lambda i: i["L1_attn_dt_proj_w"].T,
    "ss_alog": lambda i: i["L1_attn_A_log"],
    "ss_out": lambda i: i["L1_attn_out_proj_w"].T,
    "me_router": lambda i: i["L1_ffn_router_w"].T,
    "me_w1": lambda i: i["L1_ffn_gate_up_w"].transpose(0, 2, 1),
    "me_w2": lambda i: i["L1_ffn_down_w"].transpose(0, 2, 1),
    "me_s1": lambda i: i["L1_ffn_shared_gate_up_w"].T,
    "me_s2": lambda i: i["L1_ffn_shared_down_w"].T,
    "ctx": lambda i: i["ctx_1024"][0],
    "ca_wq": lambda i: i["L0_attn_Wq"].T,
    "ca_wk": lambda i: i["L0_attn_Wk"].T,
    "ca_wv": lambda i: i["L0_attn_Wv"].T,
    "tf_gate": lambda i: i["L0_ffn_w_gate"].T,
    "tf_up": lambda i: i["L0_ffn_w_up"].T,
    "tf_down": lambda i: i["L0_ffn_w_down"].T,
    "xa_wq": lambda i: i["L1_xattn_Wq"],
    "xa_wkT": lambda i: i["L1_xattn_Wk"].T,
    "xa_wv": lambda i: i["L1_xattn_Wv"],
    "x": lambda i: i["x"][0],
    "ctxT": lambda i: i["ctx_1024"][0].T,
    "wq": lambda i: i["L0_xattn_w_q"],
    "wkT": lambda i: i["L0_xattn_w_kv"][:, :INNER].T,
    "wv": lambda i: i["L0_xattn_w_kv"][:, INNER:],
    "w_out": lambda i: i["L0_xattn_w_out"],
    "gate": lambda i: i["L0_xattn_gate"].reshape(1, 1),
}


def kernel(**inputs):
    import numpy as np
    import concourse.bacc as bacc
    from concourse.bass_utils import run_bass_kernel_spmd

    given = {k: np.asarray(v) for k, v in inputs.items()}
    rows = np.stack([given["L0_xattn_ln_gamma"], given["L0_xattn_ln_beta"], given["L0_xattn_b_out"], given["L0_attn_bv"],
                     given["L1_xattn_bv"], given["L1_attn_norm_w"], given["L1_ffn_ln_gamma"], given["L1_ffn_ln_beta"]])
    cols = np.concatenate([given[n].reshape(-1, P).T for n in
                           ("L0_attn_bq", "L0_attn_bk", "L1_xattn_bq", "L1_xattn_bk", "L1_attn_conv_b",
                            "L1_attn_dt_proj_b", "L1_attn_D_param")], axis=1)
    arrays = {n: f(given) for n, f in _INS.items()}
    arrays["rows"], arrays["cols"] = rows, cols
    nc = bacc.Bacc("TRN2", target_bir_lowering=False, num_devices=1)
    feed, aps = {}, {}
    for n, v in arrays.items():
        feed["in_" + n] = np.ascontiguousarray(v)
        aps[n] = nc.dram_tensor("in_" + n, v.shape, mybir.dt.from_np(v.dtype), kind="ExternalInput").ap()
    out = nc.dram_tensor("out", (S, D), F32, kind="ExternalOutput").ap()
    perceiver(nc, aps, out)
    r = run_bass_kernel_spmd(nc, [feed], core_ids=[0])
    return r.results[0]["out"].reshape(1, S, D)
```

```python
from contextlib import ExitStack

import concourse.bass as bass
from concourse import mybir

ALU = mybir.AluOpType
ACT = mybir.ActivationFunctionType
AX = mybir.AxisListType
F32 = mybir.dt.float32
F32R = mybir.dt.float32r
F16 = mybir.dt.float16
BF16 = mybir.dt.bfloat16
I32 = mybir.dt.int32

P = 128
D = 256
DC = D // P
S = 128
SK = 12544
TILES = 7
CH = TILES * P
NCH = SK // CH
HCH = CH // 2
H0, DH = 16, 64
INNER = H0 * DH
VW = DH + 2
T0 = 4
LN_K = 14 * 0.6931471805599453
V_TOP = 32768.0
BIG = 3.0e38
LN_EPS = 1e-5
ROUND = 12582912.0

R_LN_G, R_LN_B, R_BOUT, R_A_BV, R_X_BV, R_RMS_W, R_F_G, R_F_B = range(8)
NROWS = 8
TERNARY = ("gate", "up", "down")
C_A_BQ, C_A_BK, C_X_BQ, C_X_BK = 0, 2, 4, 6
C_CONVB, C_DTB, C_DPAR = 8, 12, 16
NCOLS = 20


def at_least(engine, sem, value):
    if isinstance(value, int) and value <= 0:
        return
    engine.wait_ge(sem, value)


class Linker:

    def __init__(self, engine, sem):
        self.engine, self.sem, self.count = engine, sem, 0

    def on(self, engine):
        self.engine = engine
        return self

    def __call__(self, ins):
        self.count += 1
        ins.then_inc(self.sem, 1)
        self.engine.wait_ge(self.sem, self.count)


def layer_norm_scale(v, link, st, eps):
    t, y, a = st[:, 2:3], st[:, 3:4], st[:, 4:5]
    link(v.tensor_scalar(t, st[:, 1:2], eps, None, ALU.add))
    link(v.tensor_scalar(y.bitcast(I32), t.bitcast(I32), 1, None, ALU.logical_shift_right))
    link(v.tensor_scalar(y.bitcast(I32), y.bitcast(I32), -1.0, float(0x5F3759DF), ALU.mult, ALU.add))
    for _ in range(3):
        link(v.scalar_tensor_tensor(out=a, in0=y, scalar=t, in1=y, op0=ALU.mult, op1=ALU.mult))
        link(v.tensor_scalar(a, a, -0.5, 1.5, ALU.mult, ALU.add))
        link(v.tensor_tensor(y, y, a, ALU.mult))


def layer_norm(v, link, out, x, st, stats, eps=LN_EPS):
    link(v.bn_stats(stats[:, :], x))
    link(v.bn_aggr(st[:, 0:2], stats[:, :]))
    layer_norm_scale(v, link, st, eps)
    return v.tensor_scalar(out, x, st[:, 0:1], st[:, 3:4], ALU.subtract, ALU.mult)


def perceiver(nc, a, out):
    with ExitStack() as ctx:
        def sb(name, shape, dt=F32, scope=ctx):
            return scope.enter_context(nc.sbuf_tensor(name, shape, dt))

        def sem(name):
            return ctx.enter_context(nc.semaphore(name))

        x = sb("x", [P, D])
        z = sb("z", [P, D])
        y = sb("y", [P, D])
        zT = sb("zT", [P, DC, S])
        ident = sb("ident", [P, P])
        st = sb("st", [P, 8])
        stats = sb("stats", [P, 6])
        rows = sb("rows", [P, NROWS, D])
        cols = sb("cols", [P, NCOLS])
        gate = sb("gate", [P, 2])
        ca_w = {n: sb("ca_" + n, [P, DC, D]) for n in ("wq", "wk", "wv")}
        tf_wq = {n: sb("tf_" + n, [P, 2 * INNER], BF16) for n in ("gate", "up", "down")}
        tf_mean = sb("tf_mean", [P, 3])
        ps = ctx.enter_context(nc.psum_tensor("ps", [P, 8, 512], F32))

        vlink = Linker(None, sem("vector_chain"))
        alink = Linker(None, sem("scalar_chain"))
        plink = Linker(None, sem("pool_chain"))
        links = (vlink, alink, plink)
        stored = sem("stored")
        shared = {n: sem(n) for n in ("z_ready", "zT_done", "zT_ready", "out_done", "logits_done", "max_ready",
                                      "exp_ready", "turned", "turned_copied")}
        loaded = {n: sem("loaded_" + n) for n in ("x", "ln_rows", "rows", "wq", "wkT", "wv", "w_out", "ca")}
        base = (x, z, y, zT, ident, st, stats, rows, cols, ps)

        first_cross_attention(nc, ctx, a, sb, sem, *base[:9], gate, ps, *links, shared, loaded, ca_w, tf_wq, tf_mean)
        with ExitStack() as late:
            ss = scan_weights(a, late, sb, sem)
            with ExitStack() as mid:
                xa = context_stream(a, mid, sb, sem)
                causal_attention(nc, a, sb, sem, base, links, shared, ca_w, xa)
                ternary_ffn(nc, a, sb, sem, base, links, shared, tf_wq, tf_mean, ss)
                second_cross_attention(nc, a, sb, sem, base, links, shared, xa)
            me = expert_weights(a, late, sb, sem)
            selective_scan(nc, a, sb, sem, base, links, shared, ss, me)
            expert_ffn(nc, a, sb, sem, base, links, shared, me)

        with nc.Block() as block:
            @block.sync
            def _(sp):
                sp.dma_start(out, x[:, :]).then_inc(stored, 16)
                sp.wait_ge(stored, 16)


def first_cross_attention(nc, ctx, a, sb, sem, x, z, y, zT, ident, st, stats, rows, cols, gate, ps,
                          vlink, alink, plink, shared, loaded, ca_w, tf_wq, tf_mean):
    with ExitStack() as own:
        def t(name, shape, dt=F32):
            return sb(name, shape, dt, own)

        w_out = t("w_out", [P, INNER // P, D])
        wq = t("wq", [P, DC, INNER])
        wkT = t("wkT", [P, INNER // P, D])
        wv = t("wv", [P, DC, INNER])
        wv_hi = t("wv_hi", [P, DC, INNER], F32R)
        wv_lo = t("wv_lo", [P, DC, INNER], F32R)
        wv_abs = t("wv_abs", [P, DC])
        wv_bound = t("wv_bound", [P, DC, P])
        qT = t("qT", [P, INNER // P, S])
        q_hi = t("q_hi", [P, DC, H0, S], F32R)
        q_lo = t("q_lo", [P, DC, H0, S], F32R)
        c_raw = t("c_raw", [P, DC, CH])
        c_hi = t("c_hi", [P, 2, DC, CH], F32R)
        c_lo = t("c_lo", [P, 2, DC, CH], F32R)
        c_abs = t("c_abs", [P, 2, DC])
        v_scale = t("v_scale", [P, 2])
        v_unscale = t("v_unscale", [P, 2])
        v_hi = t("v_hi", [P, TILES, H0, VW], F16)
        v_lo = t("v_lo", [P, TILES, H0, VW], F16)
        p_exp = t("p_exp", [P, 2, CH])
        pT_hi = t("pT_hi", [P, 2, TILES, S], F16)
        pT_lo = t("pT_lo", [P, 2, TILES, S], F16)
        neg_row = t("neg_row", [P, 2])
        neg_max = t("neg_max", [P, 2, H0])
        drop = t("drop", [P, H0])
        decay = t("decay", [P, H0])
        acc = t("acc", [P, H0, DH + 1])
        rec = t("rec", [P, H0])
        tf_raw = {"gate": wq.rearrange("p c n -> p (c n)"), "up": wv.rearrange("p c n -> p (c n)"),
                  "down": wkT.rearrange("p c n -> p (c n)")}
        tf_sum, tf_inv = t("tf_sum", [P, 3]), t("tf_per_mean", [P, 3])
        tf_ones = t("tf_ones", [P, P])
        o, oT = wq[:, 0, :], wv.rearrange("p c (j s) -> p (c j) s", s=S)
        tg = t("tg", [P, 1])
        one = t("one", [P, 1, 1])

        s_scores = [ps[:, 0:2, 0:HCH], ps[:, 2:4, 0:HCH]]
        s_t = [ps[:, 4, :], ps[:, 5, :]]
        s_v = ps[:, 6, :]
        s_pv = ps[:, 7, 0:4 * (DH + 1)].rearrange("p (h e) -> p h e", e=DH + 1)

        raw_loaded = sem("raw_loaded")
        ident_ready = sem("ident_ready")
        q_done, qT_ready = sem("q_done"), sem("qT_ready")
        qk_done, q_hi_ready, q_ready = sem("qk_done"), sem("q_hi_ready"), sem("q_ready")
        wv_hi_ready, wv_ready = sem("wv_hi_ready"), sem("wv_ready")
        bound_w_ready, ones_ready = sem("bound_w_ready"), sem("ones_ready")
        split_done, absmax_done, scale_ready = sem("split_done"), sem("absmax_done"), sem("scale_ready")
        scores_done, neg_max_ready, exp_done = sem("scores_done"), sem("neg_max_ready"), sem("exp_done")
        row_max_done = sem("row_max_done")
        t0_done, t1_done = sem("t0_done"), sem("t1_done")
        pT_hi_ready, pT_lo_ready = sem("pT_hi_ready"), sem("pT_lo_ready")
        v_bank_written, v_bank_free, v_hi_ready = sem("v_bank_written"), sem("v_bank_free"), sem("v_hi_ready")
        pv_done, drop_ready, decay_ready = sem("pv_done"), sem("drop_ready"), sem("decay_ready")
        acc_scaled, acc_num, flushed = sem("acc_scaled"), sem("acc_num"), sem("flushed")
        o_ready, oT_done, oT_ready = sem("o_ready"), sem("oT_done"), sem("oT_ready")
        gate_ready = sem("gate_ready")
        split_hi = sem("split_hi")
        tf_loaded = {n: sem("tf_loaded_" + n) for n in ("gate", "up", "down")}
        tf_summed, tf_total, tf_mean_ready = sem("tf_summed"), sem("tf_total"), sem("tf_mean_ready")
        tf_scaled, tf_rounded, tf_quantised = sem("tf_scaled"), sem("tf_rounded"), sem("tf_quantised")

        ctxT = a["ctxT"].rearrange("(c p) k -> p c k", p=P)
        rows_dram = a["rows"].rearrange("(o r) d -> o r d", o=1)

        def chunk_pairs(engine, two_chunks):
            two_chunks(0, True, False)
            with engine.Fori(1, NCH // 2 - 1) as i:
                two_chunks(i * 2, False, False)
            two_chunks(NCH - 2, False, True)

        def steps(c0, last):
            for par in range(2):
                for h in range(H0):
                    c = c0 + par
                    yield c, par, h, c * H0 + h, last and par == 1

        def four_heads(q, k):
            h = 8 * (k // 4) + k // 2 % 2
            return q[:, k % 2, h:h + 7:2, :]

        def v_use(c, h):
            return c * 15 + (8 + h)

        def v_bank(use, early):
            return ps[:, (6, 5, 4)[use % 3], :] if early else s_v

        def v_tile(c, h):
            return c * 14 + (7 + h if h < 7 else 6 + h)

        with nc.Block() as block:
            @block.sync
            def _(sp):
                sp.dma_start(x[:, :], a["x"]).then_inc(loaded["x"], 16)
                sp.dma_start(rows[:, 0:R_BOUT, :], rows_dram[:, 0:R_BOUT, :].to_broadcast([P, R_BOUT, D])).then_inc(loaded["ln_rows"], 16)
                sp.dma_start(c_raw[:, :, :], ctxT[:, :, 0:CH]).then_inc(raw_loaded, 16)
                sp.dma_start(wkT[:, :, :], a["wkT"].rearrange("(c p) n -> p c n", p=P)).then_inc(loaded["wkT"], 16)
                sp.dma_start(rows[:, R_BOUT:, :], rows_dram[:, R_BOUT:, :].to_broadcast([P, NROWS - R_BOUT, D])).then_inc(loaded["rows"], 16)
                sp.dma_start(gate[:, 0:1], a["gate"].to_broadcast([P, 1])).then_inc(loaded["rows"], 16)
                sp.dma_start(cols[:, :], a["cols"]).then_inc(loaded["rows"], 16)
                sp.dma_start(w_out[:, :, :], a["w_out"].rearrange("(c p) n -> p c n", p=P)).then_inc(loaded["w_out"], 16)

                for n in ("wq", "wk", "wv"):
                    sp.dma_start(ca_w[n][:, :, :], a["ca_" + n].rearrange("(c p) n -> p c n", p=P)).then_inc(loaded["ca"], 16)

                def tf_load(n):
                    w = a["tf_" + n].rearrange("(c p) n -> p c n", p=P)
                    sp.dma_start(tf_raw[n].rearrange("p (c n) -> p c n", c=w.shape[1]), w).then_inc(tf_loaded[n], 16)

                sp.wait_ge(q_done, 2)
                tf_load("gate")
                sp.wait_ge(wv_ready, 1)
                tf_load("up")
                sp.wait_ge(qk_done, 8)
                tf_load("down")

                def two_chunks(c0, first, last):
                    for par in range(2):
                        if last and par == 1:
                            break
                        c = c0 + par
                        sp.wait_ge(split_done, c + 1)
                        sp.wait_ge(absmax_done, c * 2 + 2)
                        sp.dma_start(c_raw[:, :, :], ctxT[:, :, bass.ds((c + 1) * CH, CH)]).then_inc(raw_loaded, 16)

                chunk_pairs(sp, two_chunks)

            @block.gpsimd
            def _(pool):
                link = plink.on(pool)
                link(nc.gpsimd.memset(ident[:, :], 0.0))
                nc.gpsimd.affine_select(out=ident[:, :], in_=ident[:, :], compare_op=ALU.not_equal, fill=1.0, base=0,
                                        pattern=[[-1, P]], channel_multiplier=1).then_inc(ident_ready, 1)
                nc.gpsimd.memset(v_hi[:, :, :, DH:VW], 1.0).then_inc(ones_ready, 1)
                nc.gpsimd.memset(acc[:, :, :], 0.0).then_inc(ones_ready, 1)
                nc.gpsimd.memset(one[:, :, :], 1.0).then_inc(ones_ready, 1)
                nc.gpsimd.memset(tf_ones[:, :], 1.0).then_inc(ones_ready, 1)
                nc.gpsimd.memset(neg_max[:, 1, :], BIG).then_inc(ones_ready, 1)

                def split(c, par):
                    pool.wait_ge(raw_loaded, (c + 1) * 16)
                    at_least(pool, scores_done, (c - 1) * H0)
                    if not (isinstance(c, int) and c == 0):
                        nc.gpsimd.tensor_tensor(c_hi[:, par, :, :], c_raw[:, :, :], one[:, :, :].to_broadcast([P, DC, CH]), ALU.mult).then_inc(split_hi, 1)
                    pool.wait_ge(split_hi, c + 1)
                    nc.gpsimd.tensor_tensor(c_lo[:, par, :, :], c_raw[:, :, :], c_hi[:, par, :, :].bitcast(F32),
                                            ALU.subtract).then_inc(split_done, 1)

                def two_chunks(c0, first, last):
                    for c, par, h, n, end in steps(c0, last):
                        if h == 0 and not end:
                            split(c + 1, 1 - par)
                        if h % 4 == 3:
                            g = h // 4
                            pool.wait_ge(decay_ready, c * 4 + (g + 1))
                            at_least(pool, flushed, (c - 1) * 4 + (g + 1))
                            grp = acc[:, 4 * g:4 * g + 4, :]
                            nc.gpsimd.tensor_tensor(grp, grp, decay[:, 4 * g:4 * g + 4].unsqueeze(2).to_broadcast([P, 4, DH + 1]),
                                                    ALU.mult).then_inc(acc_scaled, 1)
                            if first and par == 1 and g > 0:
                                name = TERNARY[g - 1]
                                pool.wait_ge(tf_rounded, 2 * g)
                                nc.gpsimd.tensor_scalar(tf_wq[name][:, :], tf_raw[name], -1.0, None, ALU.max).then_inc(tf_quantised, 1)

                pool.wait_ge(ones_ready, 5)
                split(0, 0)
                chunk_pairs(pool, two_chunks)

            @block.scalar
            def _(act):
                link = alink.on(act)
                act.dma_start(wq[:, :, :], a["wq"].rearrange("(c p) n -> p c n", p=P)).then_inc(loaded["wq"], 16)
                act.dma_start(wv[:, :, :], a["wv"].rearrange("(c p) n -> p c n", p=P)).then_inc(loaded["wv"], 16)
                act.wait_ge(raw_loaded, 16)
                nc.scalar.activation(c_hi[:, 0, :, :], c_raw[:, :, :], ACT.Copy).then_inc(split_hi, 1)
                act.wait_ge(shared["zT_done"], 1)
                nc.scalar.activation(zT[:, :, :], ps[:, 0, 0:DC * S].rearrange("p (c s) -> p c s", c=DC), ACT.Copy).then_inc(shared["zT_ready"], 1)
                act.wait_ge(loaded["wv"], 16)
                nc.scalar.activation(wv_hi[:, :, :], wv[:, :, :], ACT.Copy).then_inc(wv_hi_ready, 1)

                def v_high(tile, half, par, use, early=False):
                    act.wait_ge(v_bank_written, use + 1)
                    nc.scalar.activation(v_hi[:, tile, 8 * half:8 * half + 8, 0:DH],
                                         v_bank(use, early).rearrange("p (h e) -> p h e", e=DH), ACT.Copy,
                                         scale=v_scale[:, par:par + 1]).then_inc(v_hi_ready, 1)

                def exponent(n, h, par):
                    act.wait_ge(neg_max_ready, n + 1)
                    at_least(act, t1_done, n - 1)
                    nc.scalar.activation(p_exp[:, h % 2, :].rearrange("p (b k) -> p b k", b=2), s_scores[h % 2], ACT.Exp,
                                         bias=neg_max[:, par, h:h + 1]).then_inc(exp_done, 1)

                for k in range(2):
                    act.wait_ge(q_done, k + 1)
                    nc.scalar.activation(qT[:, 4 * k:4 * k + 4, :], ps[:, 1 + k, :].rearrange("p (j s) -> p j s", j=4), ACT.Copy,
                                         scale=DH ** -0.5).then_inc(qT_ready, 1)
                for k in range(8):
                    act.wait_ge(qk_done, k + 1)
                    nc.scalar.activation(four_heads(q_hi, k),
                                         ps[:, k % 4, :].rearrange("p (h s) -> p h s", h=4), ACT.Copy).then_inc(q_hi_ready, 1)
                act.wait_ge(scale_ready, 1)
                for k in range(TILES):
                    if k == 2:
                        exponent(0, 0, 0)
                    v_high(k, 0, 0, 1 + k, True)

                def two_chunks(c0, first, last):
                    for c, par, h, n, end in steps(c0, last):
                        if not (end and h == H0 - 1):
                            exponent(n + 1, (h + 1) % H0, par if h < H0 - 1 else 1 - par)
                        if h < 7:
                            if h == 0:
                                at_least(act, pv_done, c * H0)
                            v_high(h, 1, par, v_use(c, h))
                        elif 8 <= h < 15 and not end:
                            if h == 8:
                                act.wait_ge(pv_done, c * H0 + 8)
                                act.wait_ge(scale_ready, c + 2)
                            v_high(h - 8, 0, 1 - par, v_use(c, h))
                        if h % 4 == 3:
                            g = h // 4
                            act.wait_ge(drop_ready, c * 4 + (g + 1))
                            at_least(act, acc_scaled, (c - 1) * 4 + (g + 1))
                            nc.scalar.activation(decay[:, 4 * g:4 * g + 4], drop[:, 4 * g:4 * g + 4], ACT.Exp).then_inc(decay_ready, 1)
                        at_least(act, pv_done, n - 1)
                        act.wait_ge(t0_done, n + 1)
                        nc.scalar.activation(pT_hi[:, h % 2, 0:T0, :], s_t[0].rearrange("p (t s) -> p t s", t=T0), ACT.Copy).then_inc(pT_hi_ready, 1)
                        act.wait_ge(t1_done, n + 1)
                        nc.scalar.activation(pT_hi[:, h % 2, T0:TILES, :], s_t[1][:, 0:(TILES - T0) * S].rearrange("p (t s) -> p t s", s=S),
                                             ACT.Copy).then_inc(pT_hi_ready, 1)
                        if first and par == 0 and h in (9, 11, 13):
                            k = (h - 9) // 2
                            name = TERNARY[k]
                            act.wait_ge(tf_loaded[name], 16)
                            nc.scalar.activation(tf_wq[name][:, :], tf_raw[name], ACT.Abs, accum_out=tf_sum[:, k:k + 1]).then_inc(tf_summed, 1)
                        if first and par == 1 and h < 12 and h % 4 in (1, 2):
                            k = h // 4
                            w = tf_raw[TERNARY[k]]
                            if h % 4 == 1:
                                act.wait_ge(tf_mean_ready, 1)
                                nc.scalar.activation(w, w, ACT.Copy, scale=tf_inv[:, k:k + 1]).then_inc(tf_scaled, 1)
                            else:
                                act.wait_ge(tf_scaled, 2 * k + 1)
                                nc.scalar.activation(w, w, ACT.Copy, bias=ROUND).then_inc(tf_scaled, 1)

                chunk_pairs(act, two_chunks)
                act.wait_ge(loaded["rows"], 48)
                nc.scalar.activation(tg[:, :], gate[:, 0:1], ACT.Tanh).then_inc(gate_ready, 1)
                for k in range(2):
                    act.wait_ge(oT_done, k + 1)
                    nc.scalar.activation(oT[:, 4 * k:4 * k + 4, :], ps[:, k, :].rearrange("p (j s) -> p j s", j=4), ACT.Copy).then_inc(oT_ready, 1)

            @block.vector
            def _(v):
                link = vlink.on(v)
                v.wait_ge(loaded["x"], 16)
                link(layer_norm(nc.vector, link, z[:, :], x[:, :], st, stats))
                link(layer_norm(nc.vector, link, y[:, :], z[:, :], st, stats))
                v.wait_ge(loaded["ln_rows"], 16)
                link(nc.vector.tensor_tensor(y[:, :], y[:, :], rows[:, R_LN_G, :], ALU.mult))
                nc.vector.tensor_tensor(y[:, :], y[:, :], rows[:, R_LN_B, :], ALU.add).then_inc(shared["z_ready"], 1)

                def absmax(c, par, k):
                    v.wait_ge(raw_loaded, (c + 1) * 16)
                    nc.vector.tensor_reduce(c_abs[:, par, k:k + 1], c_raw[:, k, :], AX.X, ALU.max,
                                            apply_absolute_value=True).then_inc(absmax_done, 1)

                def scale(c, par, use):
                    v.wait_ge(v_bank_written, use + 1)
                    nc.vector.tensor_scalar(v_unscale[:, par:par + 1], s_v[:, 0:1], 1.0 / V_TOP, 1e-30, ALU.mult, ALU.max).then_inc(v_bank_free, 1)
                    v.wait_ge(v_bank_free, use + 1)
                    nc.vector.reciprocal(v_scale[:, par:par + 1], v_unscale[:, par:par + 1]).then_inc(scale_ready, 1)

                def v_low(tile, half, par, use, number, early=False):
                    v.wait_ge(v_hi_ready, number + 1)
                    nc.vector.scalar_tensor_tensor(out=v_lo[:, tile, 8 * half:8 * half + 8, 0:DH],
                                                   in0=v_bank(use, early).rearrange("p (h e) -> p h e", e=DH), scalar=v_scale[:, par:par + 1],
                                                   in1=v_hi[:, tile, 8 * half:8 * half + 8, 0:DH],
                                                   op0=ALU.mult, op1=ALU.subtract).then_inc(v_bank_free, 1)

                def row_max(n, h, par):
                    v.wait_ge(scores_done, n + 1)
                    nc.vector.tensor_reduce(neg_row[:, h % 2:h % 2 + 1], s_scores[h % 2], AX.XY, ALU.max, negate=True).then_inc(row_max_done, 1)
                    v.wait_ge(row_max_done, n + 1)
                    nc.vector.scalar_tensor_tensor(out=neg_max[:, par, h:h + 1], in0=neg_row[:, h % 2:h % 2 + 1], scalar=LN_K,
                                                   in1=neg_max[:, 1 - par, h:h + 1], op0=ALU.add, op1=ALU.min).then_inc(neg_max_ready, 1)

                def flush(f, g, par):
                    v.wait_ge(pv_done, (f + 1) * 4)
                    v.wait_ge(acc_scaled, f + 1)
                    nc.vector.scalar_tensor_tensor(out=acc[:, 4 * g:4 * g + 4, 0:DH], in0=s_pv[:, :, 0:DH],
                                                   scalar=v_unscale[:, par:par + 1], in1=acc[:, 4 * g:4 * g + 4, 0:DH],
                                                   op0=ALU.mult, op1=ALU.add).then_inc(acc_num, 1)
                    nc.vector.tensor_tensor(acc[:, 4 * g:4 * g + 4, DH:DH + 1], acc[:, 4 * g:4 * g + 4, DH:DH + 1],
                                            s_pv[:, :, DH:DH + 1], ALU.add).then_inc(flushed, 1)

                v.wait_ge(loaded["wv"], 16)
                link(nc.vector.tensor_reduce(wv_abs[:, :], wv[:, :, :], AX.X, ALU.max, apply_absolute_value=True))
                absmax(0, 0, 0)
                absmax(0, 0, 1)
                nc.vector.tensor_copy(wv_bound[:, :, :], wv_abs[:, :].unsqueeze(2).to_broadcast([P, DC, P])).then_inc(bound_w_ready, 1)
                v.wait_ge(wv_hi_ready, 1)
                nc.vector.tensor_tensor(wv_lo[:, :, :], wv[:, :, :], wv_hi[:, :, :].bitcast(F32), ALU.subtract).then_inc(wv_ready, 1)
                scale(0, 0, 0)
                for k in range(8):
                    v.wait_ge(q_hi_ready, k + 1)
                    nc.vector.tensor_tensor(four_heads(q_lo, k), ps[:, k % 4, :].rearrange("p (h s) -> p h s", h=4),
                                            four_heads(q_hi, k).bitcast(F32), ALU.subtract).then_inc(q_ready, 1)
                v.wait_ge(ones_ready, 5)
                for k in range(TILES):
                    if k == 2:
                        row_max(0, 0, 0)
                    v_low(k, 0, 0, 1 + k, k, True)

                def two_chunks(c0, first, last):
                    for c, par, h, n, end in steps(c0, last):
                        if not (end and h == H0 - 1):
                            row_max(n + 1, (h + 1) % H0, par if h < H0 - 1 else 1 - par)
                        if h in (2, 4) and not end:
                            absmax(c + 1, 1 - par, h // 2 - 1)
                        if h < 7:
                            v_low(h, 1, par, v_use(c, h), v_tile(c, h))
                        elif h == 7 and not end:
                            scale(c + 1, 1 - par, v_use(c, h))
                        elif h < 15 and not end:
                            v_low(h - 8, 0, 1 - par, v_use(c, h), v_tile(c, h))
                        if h % 4 == 0 and not (first and par == 0 and h == 0):
                            flush(c * 4 + (h // 4 - 1), (h // 4 - 1) % 4, par if h else 1 - par)
                        if first and par == 0 and h == H0 - 1:
                            v.wait_ge(tf_total, 1)
                            link(nc.vector.tensor_scalar(tf_mean[:, :], s_v[:, 0:3], 1.0 / (D * INNER), 1e-5, ALU.mult, ALU.max))
                            nc.vector.reciprocal(tf_inv[:, :], tf_mean[:, :]).then_inc(tf_mean_ready, 1)
                        if first and par == 1 and h in (5, 6, 9, 10, 13, 14):
                            v.wait_ge(tf_scaled, h // 4 * 2)
                            w = tf_raw[TERNARY[h // 4 - 1]][:, (h + 1) % 2 * INNER:((h + 1) % 2 + 1) * INNER]
                            nc.vector.tensor_scalar(w, w, ROUND, 1.0, ALU.subtract, ALU.min).then_inc(tf_rounded, 1)
                        if h % 4 == 3:
                            g = h // 4
                            at_least(v, decay_ready, (c - 1) * 4 + (g + 1))
                            v.wait_ge(neg_max_ready, n + 1)
                            nc.vector.tensor_tensor(drop[:, 4 * g:4 * g + 4], neg_max[:, par, 4 * g:4 * g + 4],
                                                    neg_max[:, 1 - par, 4 * g:4 * g + 4], ALU.subtract).then_inc(drop_ready, 1)
                        for b, (t0, t1) in enumerate(((0, T0), (T0, TILES))):
                            v.wait_ge(pT_hi_ready, n * 2 + (b + 1))
                            nc.vector.tensor_tensor(pT_lo[:, h % 2, t0:t1, :], s_t[b][:, 0:(t1 - t0) * S].rearrange("p (t s) -> p t s", s=S),
                                                    pT_hi[:, h % 2, t0:t1, :], ALU.subtract).then_inc(pT_lo_ready, 1)

                chunk_pairs(v, two_chunks)
                flush(NCH * 4 - 1, 3, 1)
                v.wait_ge(flushed, NCH * 4)
                v.wait_ge(acc_num, NCH * 4)
                link(nc.vector.reciprocal(rec[:, :], acc[:, :, DH]))
                nc.vector.tensor_tensor(o[:, :].rearrange("p (h e) -> p h e", e=DH), acc[:, :, 0:DH],
                                        rec[:, :].unsqueeze(2).to_broadcast([P, H0, DH]), ALU.mult).then_inc(o_ready, 1)
                v.wait_ge(shared["out_done"], 1)
                link(nc.vector.tensor_tensor(y[:, :], ps[:, 2, 0:D], rows[:, R_BOUT, :], ALU.add))
                v.wait_ge(loaded["ca"], 48)
                v.wait_ge(gate_ready, 1)
                link(nc.vector.scalar_tensor_tensor(out=x[:, :], in0=y[:, :], scalar=tg[:, 0:1], in1=x[:, :], op0=ALU.mult, op1=ALU.add))

            @block.tensor
            def _(pe):
                def v_project(tile, half, par, use, early=False):
                    at_least(pe, v_bank_free, use - 2 if early else use)
                    k = 0
                    for c in range(DC):
                        lh = c_hi[:, par, c, tile * P:(tile + 1) * P]
                        ll = c_lo[:, par, c, tile * P:(tile + 1) * P]
                        rh = wv_hi[:, c, 512 * half:512 * half + 512]
                        rl = wv_lo[:, c, 512 * half:512 * half + 512]
                        for lhs, rhs in ((lh, rh), (lh, rl), (ll, rh)):
                            mm = nc.tensor.matmul(v_bank(use, early), lhs, rhs, start=(k == 0), stop=(k == 5))
                            k += 1
                    mm.then_inc(v_bank_written, 1)

                def bound(par, use):
                    at_least(pe, v_bank_free, use)
                    for c in range(DC):
                        mm = nc.tensor.matmul(s_v[:, 0:1], wv_bound[:, c, :], c_abs[:, par, c:c + 1], start=(c == 0), stop=(c == DC - 1))
                    mm.then_inc(v_bank_written, 1)

                def scores(n, h, par):
                    at_least(pe, exp_done, n - 1)
                    k = 0
                    for c in range(DC):
                        for qq, cc in ((q_hi, c_hi), (q_hi, c_lo), (q_lo, c_hi)):
                            for b in range(2):
                                mm = nc.tensor.matmul(s_scores[h % 2][:, b, :], qq[:, c, h, :], cc[:, par, c, b * HCH:(b + 1) * HCH],
                                                      start=(k == 0), stop=(k == 5))
                            k += 1
                    mm.then_inc(scores_done, 1)

                def weigh(n, h):
                    pe.wait_ge(pT_lo_ready, n * 2 + 2)
                    for tile in range(TILES):
                        ph, pl = pT_hi[:, h % 2, tile, :], pT_lo[:, h % 2, tile, :]
                        nc.tensor.matmul(s_pv[:, h % 4, :], ph, v_hi[:, tile, h, 0:DH + 1], start=(tile == 0), stop=False)
                        nc.tensor.matmul(s_pv[:, h % 4, 0:DH], ph, v_lo[:, tile, h, 0:DH], start=False, stop=False)
                        mm = nc.tensor.matmul(s_pv[:, h % 4, :], pl, v_hi[:, tile, h, 0:DH + 1], start=False, stop=(tile == TILES - 1))
                    mm.then_inc(pv_done, 1)

                def transpose_p(n, h):
                    pe.wait_ge(exp_done, n + 1)
                    for tile in range(TILES):
                        b, s = (0, tile) if tile < T0 else (1, tile - T0)
                        mm = nc.tensor.transpose(s_t[b][:, s * S:(s + 1) * S], p_exp[:, h % 2, tile * P:(tile + 1) * P], ident[:, :])
                        if tile == T0 - 1:
                            mm.then_inc(t0_done, 1)
                    mm.then_inc(t1_done, 1)

                pe.wait_ge(ident_ready, 1)
                pe.wait_ge(shared["z_ready"], 1)
                for c in range(DC):
                    mm = nc.tensor.transpose(ps[:, 0, c * S:(c + 1) * S], y[:, c * P:(c + 1) * P], ident[:, :])
                mm.then_inc(shared["zT_done"], 1)
                pe.wait_ge(shared["zT_ready"], 1)
                pe.wait_ge(loaded["wq"], 16)
                for k in range(2):
                    for j in range(4):
                        for c in range(DC):
                            mm = nc.tensor.matmul(ps[:, 1 + k, j * S:(j + 1) * S], wq[:, c, (4 * k + j) * P:(4 * k + j + 1) * P],
                                                  zT[:, c, :], start=(c == 0), stop=(c == DC - 1))
                    mm.then_inc(q_done, 1)
                pe.wait_ge(bound_w_ready, 1)
                pe.wait_ge(absmax_done, 2)
                bound(0, 0)
                pe.wait_ge(loaded["wkT"], 16)
                for k in range(8):
                    if k == 0:
                        pe.wait_ge(qT_ready, 2)
                    at_least(pe, q_ready, k - 3)
                    for i in range(4):
                        r = DH * (k // 2 % 2)
                        j = 4 * (k // 4) + i
                        mm = nc.tensor.matmul(ps[:, k % 4, i * S:(i + 1) * S], wkT[r:r + DH, j, (k % 2) * P:(k % 2 + 1) * P],
                                              qT[r:r + DH, j, :], start=True, stop=True)
                    mm.then_inc(qk_done, 1)
                pe.wait_ge(q_ready, 8)
                pe.wait_ge(split_done, 1)
                scores(0, 0, 0)
                pe.wait_ge(wv_ready, 1)
                for k in range(TILES):
                    v_project(k, 0, 0, 1 + k, True)

                def two_chunks(c0, first, last):
                    for c, par, h, n, end in steps(c0, last):
                        if not (end and h == H0 - 1):
                            if h == H0 - 1:
                                pe.wait_ge(split_done, c + 2)
                            scores(n + 1, (h + 1) % H0, par if h < H0 - 1 else 1 - par)
                        if first and par == 1 and h == 0:
                            pe.wait_ge(tf_mean_ready, 1)
                        if h < 7:
                            v_project(h, 1, par, v_use(c, h))
                        elif h == 7 and not end:
                            pe.wait_ge(absmax_done, c * 2 + 4)
                            bound(1 - par, v_use(c, h))
                        elif h < 15 and not end:
                            if h == 8:
                                pe.wait_ge(split_done, c + 2)
                            v_project(h - 8, 0, 1 - par, v_use(c, h))
                        elif first and par == 0:
                            pe.wait_ge(v_bank_free, v_use(c, h))
                            pe.wait_ge(tf_summed, 3)
                            nc.tensor.matmul(s_v[:, 0:3], tf_ones[:, :], tf_sum[:, :], start=True, stop=True).then_inc(tf_total, 1)
                        if not (first and par == 0 and h == 0):
                            hp = (h - 1) % H0
                            if hp % 4 == 0:
                                at_least(pe, flushed, c * 4 + hp // 4)
                            if hp % 8 == 0:
                                pe.wait_ge(v_bank_free, c * 15 + (8 if hp == 0 else 15))
                            weigh(n - 1, hp)
                        transpose_p(n, h)

                chunk_pairs(pe, two_chunks)
                weigh(NCH * H0 - 1, H0 - 1)
                pe.wait_ge(o_ready, 1)
                for k in range(2):
                    for j in range(4):
                        mm = nc.tensor.transpose(ps[:, k, j * S:(j + 1) * S], o[:, (4 * k + j) * P:(4 * k + j + 1) * P], ident[:, :])
                    mm.then_inc(oT_done, 1)
                pe.wait_ge(loaded["w_out"], 16)
                for k in range(8):
                    if k % 4 == 0:
                        pe.wait_ge(oT_ready, k // 4 + 1)
                    mm = nc.tensor.matmul(ps[:, 2, 0:D], oT[:, k, :], w_out[:, k, :], start=(k == 0), stop=(k == 7))
                mm.then_inc(shared["out_done"], 1)


def transpose_z(nc, pe, ps, z, ident, done):
    for c in range(DC):
        mm = nc.tensor.transpose(ps[:, 0, c * S:(c + 1) * S], z[:, c * P:(c + 1) * P], ident[:, :])
    mm.then_inc(done, 1)


RING = 4


class ContextStream:
    pass


def context_stream(a, scope, sb, sem):
    xa = ContextStream()
    xa.w = {n: sb("xa_" + n, [P, DC, D], F32, scope) for n in ("wq", "wkT", "wv")}
    xa.ct = sb("xa_ct", [P, RING, DC, CH], F32, scope)
    xa.cn = sb("xa_cn", [P, RING, TILES, D], F32, scope)
    xa.w_loaded = sem("xa_w_loaded")
    xa.ct_loaded = [sem("xa_ct_loaded%d" % k) for k in range(RING)]
    xa.cn_loaded = [sem("xa_cn_loaded%d" % k) for k in range(RING)]
    ctxT = a["ctxT"].rearrange("(c p) k -> p c k", p=P)
    ctxN = a["ctx"].rearrange("(n t p) d -> n p t d", t=TILES, p=P)

    def load_weights(sp):
        for n in xa.w:
            sp.dma_start(xa.w[n][:, :, :], a["xa_" + n].rearrange("(c p) n -> p c n", p=P)).then_inc(xa.w_loaded, 16)

    def load_ct(sp, c, slot):
        sp.dma_start(xa.ct[:, slot, :, :], ctxT[:, :, bass.ds(c * CH, CH)]).then_inc(xa.ct_loaded[slot], 16)

    def load_cn(sp, c, slot):
        sp.dma_start(xa.cn[:, slot, :, :], ctxN[bass.ds(c, 1), :, :, :].rearrange("o p t d -> p (o t) d")).then_inc(xa.cn_loaded[slot], 16)

    xa.load_weights, xa.load_ct, xa.load_cn = load_weights, load_ct, load_cn
    return xa


def causal_attention(nc, a, sb, sem, base, links, shared, w, xa):
    x, z, y, zT, ident, st, stats, rows, cols, ps = base
    vlink, alink, plink = links
    with ExitStack() as own:
        def t(name, shape, dt=F32):
            return sb("ca_" + name, shape, dt, own)

        qT, kT, val = t("qT", [P, DC, S]), t("kT", [P, DC, S]), t("val", [P, D])
        sc, p, pT = t("sc", [P, S]), t("p", [P, S]), t("pT", [P, S])
        neg_max, total, rec = t("neg_max", [P, 1]), t("total", [P, 1]), t("rec", [P, 1])
        E = {n: sem("ca_" + n) for n in ("proj_done", "q_ready", "kv_ready",
                                         "copied", "masked", )}
        with nc.Block() as block:
            @block.sync
            def _(sp):
                xa.load_weights(sp)
                for c in range(RING):
                    xa.load_ct(sp, c, c)
                for c in range(RING):
                    xa.load_cn(sp, c, c)

            @block.vector
            def _(v):
                link = vlink.on(v)
                layer_norm(nc.vector, link, z[:, :], x[:, :], st, stats).then_inc(shared["z_ready"], 1)
                v.wait_ge(shared["zT_done"], 2)
                nc.vector.tensor_copy(zT[:, :, :], ps[:, 0, 0:DC * S].rearrange("p (c s) -> p c s", c=DC)).then_inc(shared["zT_ready"], 1)
                v.wait_ge(E["proj_done"], 1)
                nc.vector.tensor_tensor(kT[:, :, :], ps[:, 2, 0:DC * S].rearrange("p (c s) -> p c s", c=DC),
                                        cols[:, C_A_BK:C_A_BK + DC].unsqueeze(2).to_broadcast([P, DC, S]), ALU.add).then_inc(E["kv_ready"], 1)
                nc.vector.tensor_tensor(val[:, :], ps[:, 3, 0:D], rows[:, R_A_BV, :], ALU.add).then_inc(E["kv_ready"], 1)
                v.wait_ge(E["masked"], 1)
                link(nc.vector.tensor_reduce(neg_max[:, :], sc[:, :], AX.X, ALU.max, negate=True))
                nc.vector.tensor_scalar(neg_max[:, :], neg_max[:, :], D ** -0.5, None, ALU.mult).then_inc(shared["max_ready"], 1)
                v.wait_ge(shared["exp_ready"], 1)
                link(nc.vector.reciprocal(rec[:, :], total[:, :]))
                v.wait_ge(shared["out_done"], 2)
                link(nc.vector.scalar_tensor_tensor(out=x[:, :], in0=ps[:, 6, 0:D], scalar=rec[:, 0:1], in1=x[:, :],
                                                    op0=ALU.mult, op1=ALU.add))

            @block.scalar
            def _(act):
                link = alink.on(act)
                act.wait_ge(E["proj_done"], 1)
                for c in range(DC):
                    nc.scalar.activation(qT[:, c, :], ps[:, 1, c * S:(c + 1) * S], ACT.Identity,
                                         bias=cols[:, C_A_BQ + c:C_A_BQ + c + 1]).then_inc(E["q_ready"], 1)
                act.wait_ge(shared["logits_done"], 1)
                nc.scalar.activation(sc[:, :], ps[:, 4, 0:S], ACT.Copy).then_inc(E["copied"], 1)
                act.wait_ge(shared["max_ready"], 1)
                nc.scalar.activation(p[:, :], sc[:, :], ACT.Exp, bias=neg_max[:, 0:1], scale=D ** -0.5,
                                     accum_out=total[:, :]).then_inc(shared["exp_ready"], 1)
                act.wait_ge(shared["turned"], 1)
                nc.scalar.activation(pT[:, :], ps[:, 5, 0:S], ACT.Copy).then_inc(shared["turned_copied"], 1)

            @block.gpsimd
            def _(pool):
                pool.wait_ge(E["copied"], 1)
                nc.gpsimd.affine_select(out=sc[:, :], in_=sc[:, :], compare_op=ALU.is_ge, fill=-BIG, base=0,
                                        pattern=[[-1, S]], channel_multiplier=1).then_inc(E["masked"], 1)

            @block.tensor
            def _(pe):
                pe.wait_ge(shared["z_ready"], 2)
                transpose_z(nc, pe, ps, z, ident, shared["zT_done"])
                pe.wait_ge(shared["zT_ready"], 2)
                for bank, n in ((1, "wq"), (2, "wk")):
                    for e in range(DC):
                        for c in range(DC):
                            nc.tensor.matmul(ps[:, bank, e * S:(e + 1) * S], w[n][:, c, e * P:(e + 1) * P], zT[:, c, :],
                                             start=(c == 0), stop=(c == DC - 1))
                for c in range(DC):
                    mm = nc.tensor.matmul(ps[:, 3, 0:D], zT[:, c, :], w["wv"][:, c, :], start=(c == 0), stop=(c == DC - 1))
                mm.then_inc(E["proj_done"], 1)
                pe.wait_ge(E["q_ready"], 2)
                pe.wait_ge(E["kv_ready"], 2)
                for c in range(DC):
                    mm = nc.tensor.matmul(ps[:, 4, 0:S], qT[:, c, :], kT[:, c, :], start=(c == 0), stop=(c == DC - 1))
                mm.then_inc(shared["logits_done"], 1)
                pe.wait_ge(shared["exp_ready"], 1)
                nc.tensor.transpose(ps[:, 5, 0:S], p[:, :], ident[:, :]).then_inc(shared["turned"], 1)
                pe.wait_ge(shared["turned_copied"], 1)
                nc.tensor.matmul(ps[:, 6, 0:D], pT[:, :], val[:, :], start=True, stop=True).then_inc(shared["out_done"], 1)


def quantise_rows(v, link, q, src, am, inv):
    link(v.tensor_reduce(am[:, 0:1], src, AX.X, ALU.max, apply_absolute_value=True))
    link(v.tensor_scalar(am[:, 0:1], am[:, 0:1], 1e-5, None, ALU.max))
    link(v.reciprocal(am[:, 1:2], am[:, 0:1]))
    link(v.tensor_scalar(am[:, 1:2], am[:, 1:2], 127.0, None, ALU.mult))
    link(v.tensor_scalar(inv, am[:, 0:1], 1.0 / 127.0, None, ALU.mult))
    link(v.tensor_scalar(q, src, am[:, 1:2], ROUND, ALU.mult, ALU.add))
    link(v.tensor_scalar(q, q, ROUND, 127.0, ALU.subtract, ALU.min))
    return v.tensor_scalar(q, q, -128.0, None, ALU.max)


def ternary_ffn(nc, a, sb, sem, base, links, shared, wq, mean, ss):
    x, z, y, zT, ident, st, stats, rows, cols, ps = base
    vlink, alink, plink = links
    F = INNER
    with ExitStack() as own:
        def t(name, shape, dt=F32):
            return sb("tf_" + name, shape, dt, own)

        zqT = t("zqT", [P, DC, S], BF16)
        am, inv, sg = t("am", [P, 2]), t("inv", [P, 2]), t("sg", [P, 4])
        e, h, hqT = t("e", [P, F]), t("h", [P, F]), t("hqT", [P, 8, S], BF16)
        E = {n: sem("tf_" + n) for n in ("gu_done", "sg_ready", "e_ready", "hq_ready", "hT_done", "hT_ready")}
        with nc.Block() as block:
            @block.sync
            def _(sp):
                ss.load(sp)

            @block.scalar
            def _(act):
                act.wait_ge(E["sg_ready"], 1)
                act.wait_ge(E["gu_done"], 1)
                nc.scalar.activation(e[:, :].rearrange("p (b n) -> p b n", b=2), ps[:, 0:2, :], ACT.Tanh, scale=sg[:, 2:3]).then_inc(E["e_ready"], 1)
                for k in range(2):
                    act.wait_ge(E["hT_done"], k + 1)
                    nc.scalar.activation(hqT[:, 4 * k:4 * k + 4, :], ps[:, 5 + k, :].rearrange("p (j s) -> p j s", j=4), ACT.Copy).then_inc(E["hT_ready"], 1)

            @block.vector
            def _(v):
                link = vlink.on(v)
                link(layer_norm(nc.vector, link, z[:, :], x[:, :], st, stats))
                quantise_rows(nc.vector, link, y[:, :], z[:, :], am, inv[:, 0:1]).then_inc(shared["z_ready"], 1)
                link(nc.vector.tensor_tensor(sg[:, 0:2], mean[:, 0:2], inv[:, 0:1].to_broadcast([P, 2]), ALU.mult))
                nc.vector.tensor_scalar(sg[:, 2:3], sg[:, 0:1], 0.5, None, ALU.mult).then_inc(E["sg_ready"], 1)
                v.wait_ge(E["sg_ready"], 1)
                link(nc.vector.tensor_tensor(sg[:, 3:4], sg[:, 2:3], sg[:, 1:2], ALU.mult))
                v.wait_ge(shared["zT_done"], 3)
                nc.vector.tensor_copy(zqT[:, :, :], ps[:, 0, 0:DC * S].rearrange("p (c s) -> p c s", c=DC)).then_inc(shared["zT_ready"], 1)
                v.wait_ge(E["e_ready"], 1)
                gp = ps[:, 0:2, :].rearrange("p b n -> p (b n)")
                up = ps[:, 2:4, :].rearrange("p b n -> p (b n)")
                link(nc.vector.scalar_tensor_tensor(out=e[:, :], in0=e[:, :], scalar=1.0, in1=gp, op0=ALU.add, op1=ALU.mult))
                link(nc.vector.scalar_tensor_tensor(out=h[:, :], in0=up, scalar=sg[:, 3:4], in1=e[:, :], op0=ALU.mult, op1=ALU.mult))
                quantise_rows(nc.vector, link, h[:, :], h[:, :], am, inv[:, 1:2]).then_inc(E["hq_ready"], 1)
                link(nc.vector.tensor_tensor(sg[:, 3:4], mean[:, 2:3], inv[:, 1:2], ALU.mult))
                v.wait_ge(shared["out_done"], 3)
                link(nc.vector.scalar_tensor_tensor(out=x[:, :], in0=ps[:, 4, 0:D], scalar=sg[:, 3:4], in1=x[:, :],
                                                    op0=ALU.mult, op1=ALU.add))

            @block.tensor
            def _(pe):
                pe.wait_ge(shared["z_ready"], 3)
                transpose_z(nc, pe, ps, y, ident, shared["zT_done"])
                pe.wait_ge(shared["zT_ready"], 3)
                for k, n in enumerate(("gate", "up")):
                    for b in range(2):
                        for c in range(DC):
                            mm = nc.tensor.matmul(ps[:, 2 * k + b, :], zqT[:, c, :], wq[n][:, c * F + 512 * b:c * F + 512 * b + 512],
                                                  start=(c == 0), stop=(c == DC - 1))
                mm.then_inc(E["gu_done"], 1)
                pe.wait_ge(E["hq_ready"], 1)
                for k in range(2):
                    for j in range(4):
                        mm = nc.tensor.transpose(ps[:, 5 + k, j * S:(j + 1) * S], h[:, (4 * k + j) * P:(4 * k + j + 1) * P], ident[:, :])
                    mm.then_inc(E["hT_done"], 1)
                for j in range(8):
                    if j % 4 == 0:
                        pe.wait_ge(E["hT_ready"], j // 4 + 1)
                    mm = nc.tensor.matmul(ps[:, 4, 0:D], hqT[:, j, :], wq["down"][:, j * D:(j + 1) * D], start=(j == 0), stop=(j == 7))
                mm.then_inc(shared["out_done"], 1)


def second_cross_attention(nc, a, sb, sem, base, links, shared, xa):
    x, z, y, zT, ident, st, stats, rows, cols, ps = base
    vlink, alink, plink = links
    w, ct, cn, ct_loaded, cn_loaded = xa.w, xa.ct, xa.cn, xa.ct_loaded, xa.cn_loaded
    with ExitStack() as own:
        def t(name, shape, dt=F32):
            return sb("xa_" + name, shape, dt, own)

        qT, q2T = t("qT", [P, DC, S]), t("q2T", [P, DC, S])
        lim = t("lim", [P, 2])
        sc = t("sc", [P, SK])
        chunk_max, top, neg_top = t("chunk_max", [P, NCH]), t("top", [P, 1]), t("neg_top", [P, 1])
        total = t("total", [P, NCH])
        p = t("p", [P, 2, CH])
        pT = t("pT", [P, 2, TILES, S])
        rec, u, uT = t("rec", [P, 1]), t("u", [P, D]), t("uT", [P, DC, S])
        E = {n: sem("xa_" + n) for n in ("q_done", "q_ready", "q2_done", "q2_ready",
                                         "lim_ready", "scores_done", "max_done", "clipped", "top_ready", "p_ready",
                                         "t0_done", "t1_done", "pT0_ready", "pT1_ready", "weighed", "u_ready",
                                         "ones_ready")}
        sc_ps = [ps[:, 2:4, 0:HCH], ps[:, 4:6, 0:HCH]]
        t_ps = [ps[:, 4, :], ps[:, 5, :]]

        def chunks(engine, step, first=0, last=NCH):
            start = first + (last - first) % RING
            for c in range(first, start):
                step(c, c % RING, c // RING)
            with engine.Fori(0, (last - start) // RING) as i:
                for c in range(start, start + RING):
                    step(i * RING + c, c % RING, i + c // RING)

        with nc.Block() as block:
            @block.sync
            def _(sp):
                def transposed(c, slot, turn):
                    sp.wait_ge(E["scores_done"], c - (RING - 1))
                    xa.load_ct(sp, c, slot)

                def context_rows(c, slot, turn):
                    sp.wait_ge(E["weighed"], c - (RING - 1))
                    xa.load_cn(sp, c, slot)

                chunks(sp, transposed, RING)
                chunks(sp, context_rows, RING)

            @block.scalar
            def _(act):
                link = alink.on(act)
                act.wait_ge(shared["zT_done"], 4)
                nc.scalar.activation(zT[:, :, :], ps[:, 0, 0:DC * S].rearrange("p (c s) -> p c s", c=DC), ACT.Copy).then_inc(shared["zT_ready"], 1)
                act.wait_ge(E["q2_done"], 1)
                nc.scalar.activation(q2T[:, :, :], ps[:, 2, 0:DC * S].rearrange("p (c s) -> p c s", c=DC), ACT.Copy).then_inc(E["q2_ready"], 1)
                act.wait_ge(E["top_ready"], 1)

                def exponent(c, par):
                    at_least(act, E["t1_done"], c - 1)
                    nc.scalar.activation(p[:, par, :], sc[:, bass.ds(c * CH, CH)], ACT.Exp, bias=neg_top[:, 0:1],
                                         accum_out=total[:, bass.ds(c, 1)]).then_inc(E["p_ready"], 1)

                def copy_turned(c, par):
                    act.wait_ge(E["t1_done"], c + 1)
                    at_least(act, E["weighed"], c - 1)
                    nc.scalar.activation(pT[:, par, T0:TILES, :], t_ps[1][:, 0:(TILES - T0) * S].rearrange("p (t s) -> p t s", s=S),
                                         ACT.Copy).then_inc(E["pT1_ready"], 1)

                def step(c, slot, turn):
                    exponent(c + 1, (slot + 1) % 2)
                    copy_turned(c, slot % 2)

                exponent(0, 0)
                chunks(act, step, 0, NCH - 1)
                copy_turned(NCH - 1, (NCH - 1) % 2)
                act.wait_ge(shared["turned"], 2)
                nc.scalar.activation(uT[:, :, :], ps[:, 0, 0:DC * S].rearrange("p (c s) -> p c s", c=DC), ACT.Copy).then_inc(shared["turned_copied"], 1)

            @block.vector
            def _(v):
                link = vlink.on(v)
                layer_norm(nc.vector, link, z[:, :], x[:, :], st, stats).then_inc(shared["z_ready"], 1)
                v.wait_ge(E["q_done"], 1)
                link(nc.vector.tensor_tensor(qT[:, :, :], ps[:, 1, 0:DC * S].rearrange("p (c s) -> p c s", c=DC),
                                             cols[:, C_X_BQ:C_X_BQ + DC].unsqueeze(2).to_broadcast([P, DC, S]), ALU.add))
                nc.vector.tensor_scalar(qT[:, :, :], qT[:, :, :], D ** -0.5, None, ALU.mult).then_inc(E["q_ready"], 1)
                v.wait_ge(E["q2_done"], 1)
                nc.vector.tensor_scalar(lim[:, 0:1], ps[:, 6, 0:1], -1.0, -100.0, ALU.mult, ALU.add).then_inc(E["lim_ready"], 1)
                nc.vector.tensor_scalar(lim[:, 1:2], ps[:, 6, 0:1], -1.0, 100.0, ALU.mult, ALU.add).then_inc(E["lim_ready"], 1)
                v.wait_ge(E["lim_ready"], 2)

                def measure_and_clip(c, slot, turn):
                    v.wait_ge(E["scores_done"], c + 1)
                    nc.vector.tensor_reduce(chunk_max[:, bass.ds(c, 1)], sc_ps[slot % 2], AX.XY, ALU.max).then_inc(E["max_done"], 1)
                    nc.vector.tensor_scalar(sc[:, bass.ds(c * CH, CH)].rearrange("p (b k) -> p b k", b=2), sc_ps[slot % 2],
                                            lim[:, 0:1], lim[:, 1:2], ALU.max, ALU.min).then_inc(E["clipped"], 1)

                chunks(v, measure_and_clip)
                v.wait_ge(E["max_done"], NCH)
                link(nc.vector.tensor_reduce(top[:, :], chunk_max[:, :], AX.X, ALU.max))
                link(nc.vector.tensor_scalar(top[:, :], top[:, :], lim[:, 0:1], lim[:, 1:2], ALU.max, ALU.min))
                v.wait_ge(E["clipped"], NCH)
                nc.vector.tensor_scalar(neg_top[:, :], top[:, :], -1.0, None, ALU.mult).then_inc(E["top_ready"], 1)

                def copy_turned(c, slot, turn):
                    v.wait_ge(E["t0_done"], c + 1)
                    at_least(v, E["weighed"], c - 1)
                    nc.vector.tensor_copy(pT[:, slot % 2, 0:T0, :], t_ps[0].rearrange("p (t s) -> p t s", s=S)).then_inc(E["pT0_ready"], 1)

                chunks(v, copy_turned)
                v.wait_ge(E["p_ready"], NCH)
                link(nc.vector.tensor_reduce(rec[:, :], total[:, :], AX.X, ALU.add))
                link(nc.vector.reciprocal(rec[:, :], rec[:, :]))
                v.wait_ge(E["weighed"], NCH)
                nc.vector.tensor_scalar(u[:, :], ps[:, 7, 0:D], rec[:, 0:1], None, ALU.mult).then_inc(E["u_ready"], 1)
                link(nc.vector.tensor_tensor(x[:, :], x[:, :], rows[:, R_X_BV, :], ALU.add))
                v.wait_ge(shared["out_done"], 4)
                link(nc.vector.tensor_tensor(x[:, :], ps[:, 1, 0:D], x[:, :], ALU.add))

            @block.tensor
            def _(pe):
                pe.wait_ge(shared["z_ready"], 4)
                transpose_z(nc, pe, ps, z, ident, shared["zT_done"])
                pe.wait_ge(shared["zT_ready"], 4)
                pe.wait_ge(xa.w_loaded, 48)
                for e in range(DC):
                    for c in range(DC):
                        mm = nc.tensor.matmul(ps[:, 1, e * S:(e + 1) * S], w["wq"][:, c, e * P:(e + 1) * P], zT[:, c, :],
                                              start=(c == 0), stop=(c == DC - 1))
                mm.then_inc(E["q_done"], 1)
                pe.wait_ge(E["q_ready"], 1)
                for c in range(DC):
                    nc.tensor.matmul(ps[:, 6, 0:1], qT[:, c, :], cols[:, C_X_BK + c:C_X_BK + c + 1], start=(c == 0), stop=(c == DC - 1))
                for e in range(DC):
                    for c in range(DC):
                        mm = nc.tensor.matmul(ps[:, 2, e * S:(e + 1) * S], w["wkT"][:, c, e * P:(e + 1) * P], qT[:, c, :],
                                              start=(c == 0), stop=(c == DC - 1))
                mm.then_inc(E["q2_done"], 1)
                pe.wait_ge(E["q2_ready"], 1)

                def scores(c, slot, turn):
                    pe.wait_ge(ct_loaded[slot], turn * 16 + 16)
                    at_least(pe, E["clipped"], c - 1)
                    for k in range(DC):
                        for b in range(2):
                            mm = nc.tensor.matmul(sc_ps[slot % 2][:, b, :], q2T[:, k, :], ct[:, slot, k, b * HCH:(b + 1) * HCH],
                                                  start=(k == 0), stop=(k == DC - 1))
                    mm.then_inc(E["scores_done"], 1)

                chunks(pe, scores)
                pe.wait_ge(E["clipped"], NCH)

                def turn_p(c, par):
                    pe.wait_ge(E["p_ready"], c + 1)
                    at_least(pe, E["pT0_ready"], c)
                    at_least(pe, E["pT1_ready"], c)
                    for tile in range(TILES):
                        b, s = (0, tile) if tile < T0 else (1, tile - T0)
                        mm = nc.tensor.transpose(t_ps[b][:, s * S:(s + 1) * S], p[:, par, tile * P:(tile + 1) * P], ident[:, :])
                        if tile == T0 - 1:
                            mm.then_inc(E["t0_done"], 1)
                    mm.then_inc(E["t1_done"], 1)

                def weigh(c, slot, turn):
                    pe.wait_ge(cn_loaded[slot], turn * 16 + 16)
                    pe.wait_ge(E["pT0_ready"], c + 1)
                    pe.wait_ge(E["pT1_ready"], c + 1)
                    for tile in range(TILES):
                        mm = nc.tensor.matmul(ps[:, 7, 0:D], pT[:, slot % 2, tile, :], cn[:, slot, tile, :],
                                              start=(isinstance(c, int) and c == 0 and tile == 0), stop=True, skip_group_check=True)
                    mm.then_inc(E["weighed"], 1)

                def step(c, slot, turn):
                    turn_p(c + 1, (slot + 1) % 2)
                    weigh(c, slot, turn)

                turn_p(0, 0)
                chunks(pe, step, 0, NCH - 1)
                weigh(NCH - 1, (NCH - 1) % RING, (NCH - 1) // RING)
                pe.wait_ge(E["u_ready"], 1)
                for c in range(DC):
                    mm = nc.tensor.transpose(ps[:, 0, c * S:(c + 1) * S], u[:, c * P:(c + 1) * P], ident[:, :])
                mm.then_inc(shared["turned"], 1)
                pe.wait_ge(shared["turned_copied"], 2)
                for c in range(DC):
                    mm = nc.tensor.matmul(ps[:, 1, 0:D], uT[:, c, :], w["wv"][:, c, :], start=(c == 0), stop=(c == DC - 1))
                mm.then_inc(shared["out_done"], 1)


NS = 32
RANK = 16
CI = 512
CT = CI // P
TAPS = 4
HALF_N = NS // 2
HALF_READ = 12


class ScanWeights:
    pass


def scan_weights(a, scope, sb, sem):
    ss = ScanWeights()
    ss.ip = sb("ss_in_proj", [P, DC, 2 * CI], F32, scope)
    ss.op = sb("ss_out_proj", [P, CT, D], F32, scope)
    ss.xp = sb("ss_x_proj", [P, CT, RANK + 2 * NS], F32, scope)
    ss.dp = sb("ss_dt_proj", [RANK, CI], F32, scope)
    ss.cw, ss.al = sb("ss_conv_w", [P, CT, TAPS], F32, scope), sb("ss_a_log", [P, CT, NS], F32, scope)
    ss.loaded = sem("ss_loaded")

    def load(sp):
        sp.dma_start(ss.ip[:, :, :], a["ss_in"].rearrange("(c p) n -> p c n", p=P)).then_inc(ss.loaded, 16)
        sp.dma_start(ss.cw[:, :, :], a["ss_conv"].rearrange("(j p) k -> p j k", p=P)).then_inc(ss.loaded, 16)
        sp.dma_start(ss.xp[:, :, :], a["ss_x"].rearrange("(j p) k -> p j k", p=P)).then_inc(ss.loaded, 16)
        sp.dma_start(ss.dp[:, :], a["ss_dt"]).then_inc(ss.loaded, 16)
        sp.dma_start(ss.al[:, :, :], a["ss_alog"].rearrange("(j p) k -> p j k", p=P)).then_inc(ss.loaded, 16)
        sp.dma_start(ss.op[:, :, :], a["ss_out"].rearrange("(j p) n -> p j n", p=P)).then_inc(ss.loaded, 16)

    ss.load = load
    return ss


SS_LOADED = 6 * 16


def selective_scan(nc, a, sb, sem, base, links, shared, ss, me):
    x, z, y, zT, ident, st, stats, rows, cols, ps = base
    vlink, alink, plink = links
    ip, op, xp, dp, cw, al = ss.ip, ss.op, ss.xp, ss.dp, ss.cw, ss.al
    with ExitStack() as own:
        def t(name, shape, dt=F32):
            return sb("ss_" + name, shape, dt, own)

        up = t("up", [P, CT, TAPS - 1 + S])
        u, th, zg = t("u", [P, CT, S]), t("th", [P, CT, S]), t("zg", [P, CT, S])
        dbl = t("dbl", [RANK + 2 * NS, S])
        dt_, e, r, r2, du = (t(n, [P, CT, S]) for n in ("dt", "e", "r", "r2", "du"))
        b_all, c_all = t("b_all", [P, NS, S]), t("c_all", [P, NS, S])
        decay = t("decay", [P, 2, NS, S])
        h = t("h", [P, 2, NS, S])
        bc_dram = nc.dram_tensor("ss_bc", [2 * NS, S], F32).ap()
        ys = t("ys", [P, CT, S])
        E = {n: sem("ss_" + n) for n in ("uz_done", "up_ready", "zero_ready", "conv", "conv_done", "th_ready", "u_ready", "dbl_done",
                                         "dbl_ready", "dt_done", "abs_ready", "e_ready", "dt_ready", "bc_stored",
                                         "b_loaded", "c_loaded", "decay_ready", "zero_col", "driven", "scanned", "read", "pool_read",
                                         "summed", "zth_ready", "sum_copied", "y_ready")}

        def halves():
            for j in range(CT):
                for g in range(2):
                    yield j, j % 2, g, 2 * j + g

        with nc.Block() as block:
            @block.sync
            def _(sp):
                sp.wait_ge(E["dbl_ready"], 1)
                sp.dma_start(bc_dram, dbl[RANK:, :]).then_inc(E["bc_stored"], 16)
                sp.wait_ge(E["bc_stored"], 16)
                for k, (to, loaded) in enumerate(((b_all, E["b_loaded"]), (c_all, E["c_loaded"]))):
                    sp.dma_start(to[:, :, :], bc_dram[k * NS:(k + 1) * NS, :].rearrange("(o n) s -> o n s", o=1).to_broadcast([P, NS, S])).then_inc(loaded, 16)
                me.load_first(sp)

            @block.gpsimd
            def _(pool):
                link = plink.on(pool)
                nc.gpsimd.memset(up[:, :, 0:TAPS - 1], 0.0).then_inc(E["zero_ready"], 1)
                nc.gpsimd.memset(decay[:, :, :, 0:1], 0.0).then_inc(E["zero_col"], 1)
                pool.wait_ge(E["b_loaded"], 16)

                def drive(j, par, g, n):
                    pool.wait_ge(E["dt_ready"], j + 1)
                    at_least(pool, E["summed"], n - 3)
                    lo = g * HALF_N
                    nc.gpsimd.tensor_tensor(h[:, par, lo:lo + HALF_N, :], du[:, j, :].unsqueeze(1).to_broadcast([P, HALF_N, S]),
                                            b_all[:, lo:lo + HALF_N, :], ALU.mult).then_inc(E["driven"], 1)

                def read(j, par, g, n):
                    pool.wait_ge(E["scanned"], n + 1)
                    lo, hi = g * HALF_N + HALF_READ, (g + 1) * HALF_N
                    nc.gpsimd.tensor_tensor(h[:, par, lo:hi, :], h[:, par, lo:hi, :], c_all[:, lo:hi, :], ALU.mult).then_inc(E["pool_read"], 1)

                order = list(halves())
                drive(*order[0])
                pool.wait_ge(E["c_loaded"], 16)
                for n, half in enumerate(order):
                    if n + 1 < len(order):
                        drive(*order[n + 1])
                    read(*half)

            @block.scalar
            def _(act):
                link = alink.on(act)
                act.wait_ge(shared["zT_done"], 5)
                nc.scalar.activation(zT[:, :, :], ps[:, 0, 0:DC * S].rearrange("p (c s) -> p c s", c=DC), ACT.Copy).then_inc(shared["zT_ready"], 1)
                act.wait_ge(ss.loaded, SS_LOADED)
                link(nc.scalar.activation(al[:, :, :], al[:, :, :], ACT.Exp))
                link(nc.scalar.activation(al[:, :, :], al[:, :, :], ACT.Copy, scale=-1.0))
                act.wait_ge(E["uz_done"], 1)
                nc.scalar.activation(up[:, :, TAPS - 1:], ps[:, 1, :].rearrange("p (j s) -> p j s", j=CT), ACT.Copy).then_inc(E["up_ready"], 1)
                nc.scalar.activation(zg[:, :, :], ps[:, 2, :].rearrange("p (j s) -> p j s", j=CT), ACT.Tanh, scale=0.5).then_inc(E["zth_ready"], 1)
                act.wait_ge(E["conv_done"], CT)
                nc.scalar.activation(th[:, :, :], u[:, :, :], ACT.Tanh, scale=0.5).then_inc(E["th_ready"], 1)
                act.wait_ge(E["dbl_done"], 1)
                nc.scalar.activation(dbl[:, :], ps[0:RANK + 2 * NS, 3, 0:S], ACT.Copy).then_inc(E["dbl_ready"], 1)
                act.wait_ge(E["abs_ready"], 1)
                link(nc.scalar.activation(e[:, :, :], r[:, :, :], ACT.Abs))
                nc.scalar.activation(e[:, :, :], e[:, :, :], ACT.Exp, scale=-1.0).then_inc(E["e_ready"], 1)
                act.wait_ge(E["zero_col"], 1)
                for j, par, g, n in halves():
                    act.wait_ge(E["dt_ready"], j + 1)
                    at_least(act, E["scanned"], n - 3)
                    for k in range(g * HALF_N, (g + 1) * HALF_N):
                        ins = nc.scalar.activation(decay[:, par, k, 1:S], dt_[:, j, 1:S], ACT.Exp, scale=al[:, j, k:k + 1])
                    ins.then_inc(E["decay_ready"], 1)

            @block.vector
            def _(v):
                link = vlink.on(v)
                link(layer_norm(nc.vector, link, z[:, :], x[:, :], st, stats))
                link(nc.vector.bn_stats(stats[:, :], z[:, :]))
                link(nc.vector.bn_aggr(st[:, 0:2], stats[:, :]))
                link(nc.vector.scalar_tensor_tensor(out=st[:, 1:2], in0=st[:, 0:1], scalar=st[:, 0:1], in1=st[:, 1:2], op0=ALU.mult, op1=ALU.add))
                layer_norm_scale(nc.vector, link, st, 1e-6)
                nc.vector.scalar_tensor_tensor(out=y[:, :], in0=z[:, :], scalar=st[:, 3:4], in1=rows[:, R_RMS_W, :],
                                               op0=ALU.mult, op1=ALU.mult).then_inc(shared["z_ready"], 1)
                link(nc.vector.tensor_tensor(x[:, :], x[:, :], z[:, :], ALU.add))
                v.wait_ge(E["up_ready"], 1)
                v.wait_ge(E["zero_ready"], 1)
                for k in range(TAPS):
                    for j in range(CT):
                        src, wk = up[:, j, k:k + S], cw[:, j, k:k + 1]
                        if k == 0:
                            nc.vector.tensor_scalar(u[:, j, :], src, wk, cols[:, C_CONVB + j:C_CONVB + j + 1], ALU.mult, ALU.add).then_inc(E["conv"], 1)
                        else:
                            v.wait_ge(E["conv"], (k - 1) * CT + j + 1)
                            nc.vector.scalar_tensor_tensor(out=u[:, j, :], in0=src, scalar=wk, in1=u[:, j, :], op0=ALU.mult,
                                                           op1=ALU.add).then_inc(E["conv_done" if k == TAPS - 1 else "conv"], 1)
                v.wait_ge(E["th_ready"], 1)
                link(nc.vector.scalar_tensor_tensor(out=u[:, :, :], in0=th[:, :, :], scalar=1.0, in1=u[:, :, :], op0=ALU.add, op1=ALU.mult))
                nc.vector.tensor_scalar(u[:, :, :], u[:, :, :], 0.5, None, ALU.mult).then_inc(E["u_ready"], 1)
                v.wait_ge(E["dt_done"], 1)
                nc.vector.tensor_tensor(r[:, :, :], ps[:, 4, :].rearrange("p (j s) -> p j s", j=CT),
                                        cols[:, C_DTB:C_DTB + CT].unsqueeze(2).to_broadcast([P, CT, S]), ALU.add).then_inc(E["abs_ready"], 1)
                v.wait_ge(E["e_ready"], 1)

                def step_size(j):
                    d, q, q2, w = dt_[:, j, :], e[:, j, :], r2[:, j, :], r[:, j, :]
                    link(nc.vector.tensor_scalar(d, q, 2.0, None, ALU.add))
                    link(nc.vector.reciprocal(d, d))
                    link(nc.vector.tensor_tensor(q, q, d, ALU.mult))
                    link(nc.vector.tensor_tensor(q2, q, q, ALU.mult))
                    link(nc.vector.tensor_scalar(d, q2, 1.0 / 15, 1.0 / 13, ALU.mult, ALU.add))
                    link(nc.vector.tensor_tensor(d, d, q2, ALU.mult))
                    for k in (11, 9, 7, 5, 3):
                        link(nc.vector.scalar_tensor_tensor(out=d, in0=d, scalar=1.0 / k, in1=q2, op0=ALU.add, op1=ALU.mult))
                    link(nc.vector.scalar_tensor_tensor(out=d, in0=d, scalar=1.0, in1=q, op0=ALU.add, op1=ALU.mult))
                    link(nc.vector.tensor_scalar(w, w, 0.0, None, ALU.max))
                    link(nc.vector.scalar_tensor_tensor(out=d, in0=d, scalar=2.0, in1=w, op0=ALU.mult, op1=ALU.add))
                    nc.vector.tensor_tensor(du[:, j, :], d, u[:, j, :], ALU.mult).then_inc(E["dt_ready"], 1)

                def total(j):
                    v.wait_ge(E["summed"], 2 * j + 2)
                    nc.vector.tensor_reduce(ys[:, j, :], ps[:, 3 + j % 2, :].rearrange("p (n s) -> p s n", n=4), AX.X, ALU.add).then_inc(E["sum_copied"], 1)

                step_size(0)
                step_size(1)
                for j, par, g, n in halves():
                    lo = g * HALF_N
                    flat = "p n s -> p (n s)"
                    v.wait_ge(E["decay_ready"], n + 1)
                    v.wait_ge(E["driven"], n + 1)
                    hs = h[:, par, lo:lo + HALF_N, :].rearrange(flat)
                    nc.vector.tensor_tensor_scan(hs, decay[:, par, lo:lo + HALF_N, :].rearrange(flat), hs,
                                                 0.0, ALU.mult, ALU.add).then_inc(E["scanned"], 1)
                    if n == 0:
                        v.wait_ge(E["c_loaded"], 16)
                    v.wait_ge(E["scanned"], n + 1)
                    hi = lo + HALF_READ
                    nc.vector.tensor_tensor(h[:, par, lo:hi, :], h[:, par, lo:hi, :], c_all[:, lo:hi, :], ALU.mult).then_inc(E["read"], 1)
                    if g == 0 and j + 2 < CT:
                        step_size(j + 2)
                    if g == 1 and j > 0:
                        total(j - 1)
                total(CT - 1)
                v.wait_ge(E["sum_copied"], CT)
                link(nc.vector.tensor_tensor(u[:, :, :], u[:, :, :], cols[:, C_DPAR:C_DPAR + CT].unsqueeze(2).to_broadcast([P, CT, S]), ALU.mult))
                v.wait_ge(E["zth_ready"], 1)
                link(nc.vector.scalar_tensor_tensor(out=zg[:, :, :], in0=zg[:, :, :], scalar=1.0, in1=ps[:, 2, :].rearrange("p (j s) -> p j s", j=CT),
                                                    op0=ALU.add, op1=ALU.mult))
                link(nc.vector.tensor_tensor(ys[:, :, :], ys[:, :, :], u[:, :, :], ALU.add))
                nc.vector.scalar_tensor_tensor(out=ys[:, :, :], in0=ys[:, :, :], scalar=0.5, in1=zg[:, :, :], op0=ALU.mult,
                                               op1=ALU.mult).then_inc(E["y_ready"], 1)
                v.wait_ge(shared["out_done"], 5)
                link(nc.vector.tensor_tensor(x[:, :], ps[:, 0, 0:D], x[:, :], ALU.add))

            @block.tensor
            def _(pe):
                pe.wait_ge(shared["z_ready"], 5)
                transpose_z(nc, pe, ps, y, ident, shared["zT_done"])
                pe.wait_ge(shared["zT_ready"], 5)
                pe.wait_ge(ss.loaded, SS_LOADED)
                for half in range(2):
                    for j in range(CT):
                        for c in range(DC):
                            col = half * CI + j * P
                            mm = nc.tensor.matmul(ps[:, 1 + half, j * S:(j + 1) * S], ip[:, c, col:col + P], zT[:, c, :],
                                                  start=(c == 0), stop=(c == DC - 1))
                mm.then_inc(E["uz_done"], 1)
                pe.wait_ge(E["u_ready"], 1)
                for j in range(CT):
                    mm = nc.tensor.matmul(ps[0:RANK + 2 * NS, 3, 0:S], xp[:, j, :], u[:, j, :], start=(j == 0), stop=(j == CT - 1))
                mm.then_inc(E["dbl_done"], 1)
                pe.wait_ge(E["dbl_ready"], 1)
                for j in range(CT):
                    mm = nc.tensor.matmul(ps[:, 4, j * S:(j + 1) * S], dp[:, j * P:(j + 1) * P], dbl[0:RANK, :], start=True, stop=True)
                mm.then_inc(E["dt_done"], 1)
                pe.wait_ge(E["abs_ready"], 1)
                for j, par, g, n in halves():
                    if g == 0:
                        at_least(pe, E["sum_copied"], j - 1)
                    for k in range(HALF_N // 4):
                        if k == 0:
                            pe.wait_ge(E["read"], n + 1)
                        if k == HALF_READ // 4:
                            pe.wait_ge(E["pool_read"], n + 1)
                        lo = g * HALF_N + 4 * k
                        mm = nc.tensor.matmul(ps[:, 3 + j % 2, :], ident[:, :], h[:, par, lo:lo + 4, :].rearrange("p n s -> p (n s)"),
                                              start=(lo == 0), stop=(lo == NS - 4))
                    mm.then_inc(E["summed"], 1)
                pe.wait_ge(E["y_ready"], 1)
                for j in range(CT):
                    mm = nc.tensor.matmul(ps[:, 0, 0:D], ys[:, j, :], op[:, j, :], start=(j == 0), stop=(j == CT - 1))
                mm.then_inc(shared["out_done"], 1)


NE = 8
FE, FS = 768, 256


class ExpertWeights:
    pass


def expert_weights(a, scope, sb, sem):
    me = ExpertWeights()
    me.router = sb("me_router", [P, DC, NE], F32, scope)
    me.s1, me.s2 = sb("me_s1", [P, DC, 2 * FS], F32, scope), sb("me_s2", [P, FS // P, D], F32, scope)
    me.w1, me.w2 = [sb("me_w1_0", [P, DC, 2 * FE], F32, scope)], [sb("me_w2_0", [P, FE // P, D], F32, scope)]
    me.shared_loaded = sem("me_shared_loaded")
    me.w1_loaded = [sem("me_w1_loaded0"), sem("me_w1_loaded1")]
    me.w2_loaded = [sem("me_w2_loaded0"), sem("me_w2_loaded1")]
    w1 = a["me_w1"].rearrange("e (c p) n -> p e c n", p=P)
    w2 = a["me_w2"].rearrange("e (c p) n -> p e c n", p=P)

    def load_w1(sp, e, par):
        sp.dma_start(me.w1[par][:, :, :], w1[:, bass.ds(e, 1), :, :].rearrange("p o c n -> p (o c) n")).then_inc(me.w1_loaded[par], 16)

    def load_w2(sp, e, par):
        sp.dma_start(me.w2[par][:, :, :], w2[:, bass.ds(e, 1), :, :].rearrange("p o c n -> p (o c) n")).then_inc(me.w2_loaded[par], 16)

    def load_first(sp):
        sp.dma_start(me.router[:, :, :], a["me_router"].rearrange("(c p) n -> p c n", p=P)).then_inc(me.shared_loaded, 16)
        sp.dma_start(me.s1[:, :, :], a["me_s1"].rearrange("(c p) n -> p c n", p=P)).then_inc(me.shared_loaded, 16)
        sp.dma_start(me.s2[:, :, :], a["me_s2"].rearrange("(c p) n -> p c n", p=P)).then_inc(me.shared_loaded, 16)
        load_w1(sp, 0, 0)
        load_w2(sp, 0, 0)

    me.load_w1, me.load_w2, me.load_first = load_w1, load_w2, load_first
    return me


def expert_ffn(nc, a, sb, sem, base, links, shared, me):
    x, z, y, zT, ident, st, stats, rows, cols, ps = base
    vlink, alink, plink = links
    with ExitStack() as own:
        def t(name, shape, dt=F32):
            return sb("me_" + name, shape, dt, own)

        me.w1.append(t("w1_1", [P, DC, 2 * FE]))
        me.w2.append(t("w2_1", [P, FE // P, D]))
        router, s1, s2, w1, w2, w1_loaded, w2_loaded = me.router, me.s1, me.s2, me.w1, me.w2, me.w1_loaded, me.w2_loaded
        pr, total, rec = t("pr", [P, NE]), t("total", [P, 1]), t("rec", [P, 4])
        cmp, eq = t("cmp", [P, NE, NE]), t("eq", [P, NE, NE])
        before = t("before", [P, NE, NE])
        rank, pick, comb = t("rank", [P, NE]), t("pick", [P, 2, NE]), t("comb", [P, NE])
        best = t("best", [P, 2])
        th, hT = t("th", [P, 2, FE]), t("hT", [P, 2, FE])
        E = {n: sem("me_" + n) for n in ("before_ready", "best_ready", "ex_ready", "comb_ready", "up_done", "th_ready", "h_ready",
                                         "down_done", "added", "silu")}
        gu = [ps[:, 0:3, :].rearrange("p b n -> p (b n)"), ps[:, 3:6, :].rearrange("p b n -> p (b n)")]

        with nc.Block() as block:
            @block.sync
            def _(sp):
                me.load_w1(sp, 1, 1)
                me.load_w2(sp, 1, 1)
                with sp.Fori(1, NE // 2) as i:
                    for par in range(2):
                        sp.wait_ge(E["up_done"], i * 2 + par)
                        me.load_w1(sp, i * 2 + par, par)
                        sp.wait_ge(E["down_done"], i * 2 + par)
                        me.load_w2(sp, i * 2 + par, par)

            @block.gpsimd
            def _(pool):
                link = plink.on(pool)
                link(nc.gpsimd.memset(before[:, :, :], 1.0))
                nc.gpsimd.affine_select(out=before[:, :, :], in_=before[:, :, :], compare_op=ALU.is_gt, fill=0.0, base=0,
                                        pattern=[[1, NE], [-1, NE]], channel_multiplier=0).then_inc(E["before_ready"], 1)

            @block.scalar
            def _(act):
                link = alink.on(act)
                act.wait_ge(shared["zT_done"], 6)
                nc.scalar.activation(zT[:, :, :], ps[:, 6, 0:DC * S].rearrange("p (c s) -> p c s", c=DC), ACT.Copy).then_inc(shared["zT_ready"], 1)
                act.wait_ge(shared["max_ready"], 2)
                nc.scalar.activation(pr[:, :], ps[:, 7, 0:NE], ACT.Exp, bias=rec[:, 0:1], accum_out=total[:, :]).then_inc(shared["exp_ready"], 1)

                def half_tanh(n, par, width):
                    act.wait_ge(E["up_done"], n + 1)
                    at_least(act, E["h_ready"], n - 1)
                    nc.scalar.activation(th[:, par, 0:width], gu[par][:, 0:width], ACT.Tanh, scale=0.5).then_inc(E["th_ready"], 1)

                half_tanh(0, 1, FS)
                act.wait_ge(E["best_ready"], 1)
                nc.scalar.activation(rec[:, 2:3], best[:, 1:2], ACT.Exp, bias=rec[:, 1:2]).then_inc(E["ex_ready"], 1)

                def pair(i):
                    for par in range(2):
                        half_tanh(i * 2 + (par + 1), par, FE)

                with act.Fori(0, NE // 2) as i:
                    pair(i)

            @block.vector
            def _(v):
                link = vlink.on(v)
                link(layer_norm(nc.vector, link, z[:, :], x[:, :], st, stats))
                link(layer_norm(nc.vector, link, y[:, :], z[:, :], st, stats))
                link(nc.vector.tensor_tensor(y[:, :], y[:, :], rows[:, R_F_G, :], ALU.mult))
                nc.vector.tensor_tensor(y[:, :], y[:, :], rows[:, R_F_B, :], ALU.add).then_inc(shared["z_ready"], 1)
                v.wait_ge(shared["logits_done"], 2)
                nc.vector.tensor_reduce(rec[:, 0:1], ps[:, 7, 0:NE], AX.X, ALU.max, negate=True).then_inc(shared["max_ready"], 1)
                v.wait_ge(shared["exp_ready"], 2)
                link(nc.vector.reciprocal(total[:, :], total[:, :]))
                link(nc.vector.tensor_scalar(pr[:, :], pr[:, :], total[:, 0:1], None, ALU.mult))
                mine = pr[:, :].unsqueeze(2).to_broadcast([P, NE, NE])
                other = pr[:, :].unsqueeze(1).to_broadcast([P, NE, NE])
                link(nc.vector.tensor_tensor(cmp[:, :, :], other, mine, ALU.is_gt))
                link(nc.vector.tensor_tensor(eq[:, :, :], other, mine, ALU.is_equal))
                v.wait_ge(E["before_ready"], 1)
                link(nc.vector.tensor_tensor(eq[:, :, :], eq[:, :, :], before[:, :, :], ALU.mult))
                link(nc.vector.tensor_tensor(cmp[:, :, :], cmp[:, :, :], eq[:, :, :], ALU.add))
                link(nc.vector.tensor_reduce(rank[:, :], cmp[:, :, :], AX.X, ALU.add))
                for k in range(2):
                    link(nc.vector.tensor_scalar(pick[:, k, :], rank[:, :], float(k), None, ALU.is_equal))
                    link(nc.vector.tensor_tensor(comb[:, :], pick[:, k, :], pr[:, :], ALU.mult))
                    link(nc.vector.tensor_reduce(best[:, k:k + 1], comb[:, :], AX.X, ALU.add))
                nc.vector.tensor_scalar(rec[:, 1:2], best[:, 0:1], -1.0, None, ALU.mult).then_inc(E["best_ready"], 1)
                v.wait_ge(E["ex_ready"], 1)
                link(nc.vector.tensor_scalar(rec[:, 3:4], rec[:, 2:3], 1.0, None, ALU.add))
                link(nc.vector.reciprocal(rec[:, 3:4], rec[:, 3:4]))
                link(nc.vector.tensor_tensor(rec[:, 2:3], rec[:, 2:3], rec[:, 3:4], ALU.mult))
                link(nc.vector.tensor_scalar(comb[:, :], pick[:, 0, :], rec[:, 3:4], None, ALU.mult))
                link(nc.vector.scalar_tensor_tensor(out=comb[:, :], in0=pick[:, 1, :], scalar=rec[:, 2:3], in1=comb[:, :], op0=ALU.mult, op1=ALU.add))

                def hidden(n, par, width):
                    v.wait_ge(E["th_ready"], n + 1)
                    nc.vector.scalar_tensor_tensor(out=th[:, par, 0:width], in0=th[:, par, 0:width], scalar=1.0, in1=gu[par][:, 0:width],
                                                   op0=ALU.add, op1=ALU.mult).then_inc(E["silu"], 1)
                    v.wait_ge(E["silu"], n + 1)
                    at_least(v, E["down_done"], n - 1)
                    nc.vector.scalar_tensor_tensor(out=hT[:, par, 0:width], in0=th[:, par, 0:width], scalar=0.5, in1=gu[par][:, width:2 * width],
                                                   op0=ALU.mult, op1=ALU.mult).then_inc(E["h_ready"], 1)

                def weigh(n, bank, scalar):
                    v.wait_ge(E["down_done"], n + 1)
                    at_least(v, E["added"], n)
                    nc.vector.scalar_tensor_tensor(out=x[:, :], in0=ps[:, bank, 0:D], scalar=scalar, in1=x[:, :],
                                                   op0=ALU.mult, op1=ALU.add).then_inc(E["added"], 1)

                hidden(0, 1, FS)
                hidden(1, 0, FE)
                weigh(0, 7, 1.0)

                def pair(i, peeled):
                    hidden(i * 2 + 2, 1, FE)
                    weigh(i * 2 + 1, 6, comb[:, bass.ds(i * 2, 1)])
                    if not peeled:
                        hidden(i * 2 + 3, 0, FE)
                    weigh(i * 2 + 2, 7, comb[:, bass.ds(i * 2 + 1, 1)])

                with v.Fori(0, NE // 2 - 1) as i:
                    pair(i, False)
                pair(NE // 2 - 1, True)
                v.wait_ge(E["added"], NE + 1)

            @block.tensor
            def _(pe):
                pe.wait_ge(shared["z_ready"], 6)
                for c in range(DC):
                    mm = nc.tensor.transpose(ps[:, 6, c * S:(c + 1) * S], y[:, c * P:(c + 1) * P], ident[:, :])
                mm.then_inc(shared["zT_done"], 1)
                pe.wait_ge(shared["zT_ready"], 6)
                pe.wait_ge(me.shared_loaded, 48)
                for c in range(DC):
                    mm = nc.tensor.matmul(ps[:, 7, 0:NE], zT[:, c, :], router[:, c, :], start=(c == 0), stop=(c == DC - 1))
                mm.then_inc(shared["logits_done"], 1)

                def first_product(n, par, w, width):
                    at_least(pe, E["h_ready"], n - 1)
                    for j in range(2 * width // P):
                        for c in range(DC):
                            mm = nc.tensor.matmul(gu[par][:, j * P:(j + 1) * P], w[:, c, j * P:(j + 1) * P], zT[:, c, :],
                                                  start=(c == 0), stop=(c == DC - 1))
                    mm.then_inc(E["up_done"], 1)

                def second_product(n, par, w, width):
                    pe.wait_ge(E["h_ready"], n + 1)
                    at_least(pe, E["added"], n - 1)
                    for j in range(width // P):
                        mm = nc.tensor.matmul(ps[:, 7 - (1 - par), 0:D], hT[:, par, j * P:(j + 1) * P], w[:, j, :],
                                              start=(j == 0), stop=(j == width // P - 1))
                    mm.then_inc(E["down_done"], 1)

                first_product(0, 1, s1, FS)
                pe.wait_ge(w1_loaded[0], 16)
                first_product(1, 0, w1[0], FE)
                pe.wait_ge(shared["exp_ready"], 2)
                second_product(0, 1, s2, FS)

                def pair(i, peeled):
                    pe.wait_ge(w1_loaded[1], i * 16 + 16)
                    first_product(i * 2 + 2, 1, w1[1], FE)
                    pe.wait_ge(w2_loaded[0], i * 16 + 16)
                    second_product(i * 2 + 1, 0, w2[0], FE)
                    if not peeled:
                        pe.wait_ge(w1_loaded[0], i * 16 + 32)
                        first_product(i * 2 + 3, 0, w1[0], FE)
                    pe.wait_ge(w2_loaded[1], i * 16 + 16)
                    second_product(i * 2 + 2, 1, w2[1], FE)

                with pe.Fori(0, NE // 2 - 1) as i:
                    pair(i, False)
                pair(NE // 2 - 1, True)


_INS = {
    "ss_in": lambda i: i["L1_attn_in_proj_w"].T,
    "ss_conv": lambda i: i["L1_attn_conv_w"],
    "ss_x": lambda i: i["L1_attn_x_proj_w"].T,
    "ss_dt": lambda i: i["L1_attn_dt_proj_w"].T,
    "ss_alog": lambda i: i["L1_attn_A_log"],
    "ss_out": lambda i: i["L1_attn_out_proj_w"].T,
    "me_router": lambda i: i["L1_ffn_router_w"].T,
    "me_w1": lambda i: i["L1_ffn_gate_up_w"].transpose(0, 2, 1),
    "me_w2": lambda i: i["L1_ffn_down_w"].transpose(0, 2, 1),
    "me_s1": lambda i: i["L1_ffn_shared_gate_up_w"].T,
    "me_s2": lambda i: i["L1_ffn_shared_down_w"].T,
    "ctx": lambda i: i["ctx_1024"][0],
    "ca_wq": lambda i: i["L0_attn_Wq"].T,
    "ca_wk": lambda i: i["L0_attn_Wk"].T,
    "ca_wv": lambda i: i["L0_attn_Wv"].T,
    "tf_gate": lambda i: i["L0_ffn_w_gate"].T,
    "tf_up": lambda i: i["L0_ffn_w_up"].T,
    "tf_down": lambda i: i["L0_ffn_w_down"].T,
    "xa_wq": lambda i: i["L1_xattn_Wq"],
    "xa_wkT": lambda i: i["L1_xattn_Wk"].T,
    "xa_wv": lambda i: i["L1_xattn_Wv"],
    "x": lambda i: i["x"][0],
    "ctxT": lambda i: i["ctx_1024"][0].T,
    "wq": lambda i: i["L0_xattn_w_q"],
    "wkT": lambda i: i["L0_xattn_w_kv"][:, :INNER].T,
    "wv": lambda i: i["L0_xattn_w_kv"][:, INNER:],
    "w_out": lambda i: i["L0_xattn_w_out"],
    "gate": lambda i: i["L0_xattn_gate"].reshape(1, 1),
}


def kernel(**inputs):
    import numpy as np
    import concourse.bacc as bacc
    from concourse.bass_utils import run_bass_kernel_spmd

    given = {k: np.asarray(v) for k, v in inputs.items()}
    rows = np.stack([given["L0_xattn_ln_gamma"], given["L0_xattn_ln_beta"], given["L0_xattn_b_out"], given["L0_attn_bv"],
                     given["L1_xattn_bv"], given["L1_attn_norm_w"], given["L1_ffn_ln_gamma"], given["L1_ffn_ln_beta"]])
    cols = np.concatenate([given[n].reshape(-1, P).T for n in
                           ("L0_attn_bq", "L0_attn_bk", "L1_xattn_bq", "L1_xattn_bk", "L1_attn_conv_b",
                            "L1_attn_dt_proj_b", "L1_attn_D_param")], axis=1)
    arrays = {n: f(given) for n, f in _INS.items()}
    arrays["rows"], arrays["cols"] = rows, cols
    nc = bacc.Bacc("TRN2", target_bir_lowering=False, num_devices=1)
    feed, aps = {}, {}
    for n, v in arrays.items():
        feed["in_" + n] = np.ascontiguousarray(v)
        aps[n] = nc.dram_tensor("in_" + n, v.shape, mybir.dt.from_np(v.dtype), kind="ExternalInput").ap()
    out = nc.dram_tensor("out", (S, D), F32, kind="ExternalOutput").ap()
    perceiver(nc, aps, out)
    r = run_bass_kernel_spmd(nc, [feed], core_ids=[0])
    return r.results[0]["out"].reshape(1, S, D)
```

```python
from contextlib import ExitStack

import concourse.bass as bass
from concourse import mybir

ALU = mybir.AluOpType
ACT = mybir.ActivationFunctionType
AX = mybir.AxisListType
F32 = mybir.dt.float32
F32R = mybir.dt.float32r
F16 = mybir.dt.float16
BF16 = mybir.dt.bfloat16
I32 = mybir.dt.int32

P = 128
D = 256
DC = D // P
S = 128
SK = 12544
TILES = 7
CH = TILES * P
NCH = SK // CH
HCH = CH // 2
H0, DH = 16, 64
INNER = H0 * DH
VW = DH + 2
T0 = 4
K_AHEAD = 4
LN_K = 14 * 0.6931471805599453
V_TOP = 32768.0
BIG = 3.0e38
LN_EPS = 1e-5
ROUND = 12582912.0

R_LN_G, R_LN_B, R_BOUT, R_A_BV, R_X_BV, R_RMS_W, R_F_G, R_F_B = range(8)
NROWS = 8
TERNARY = ("gate", "up", "down")
TF_SUM_STEPS = (5, 6, 8, 9, 10, 12)
C_A_BQ, C_A_BK, C_X_BQ, C_X_BK = 0, 2, 4, 6
C_CONVB, C_DTB, C_DPAR = 8, 12, 16
NCOLS = 20


def at_least(engine, sem, value):
    if isinstance(value, int) and value <= 0:
        return
    engine.wait_ge(sem, value)


class Linker:

    def __init__(self, engine, sem):
        self.engine, self.sem, self.count = engine, sem, 0

    def on(self, engine):
        self.engine = engine
        return self

    def __call__(self, ins):
        self.count += 1
        ins.then_inc(self.sem, 1)
        self.engine.wait_ge(self.sem, self.count)


def layer_norm_scale(v, link, st, eps):
    t, y, a, b = st[:, 2:3], st[:, 3:4], st[:, 4:5], st[:, 5:6]
    link(v.tensor_scalar(t, st[:, 1:2], eps, None, ALU.add))
    link(v.tensor_scalar(y.bitcast(I32), t.bitcast(I32), 1, None, ALU.logical_shift_right))
    link(v.tensor_scalar(y.bitcast(I32), y.bitcast(I32), -1.0, float(0x5F3759DF), ALU.mult, ALU.add))
    link(v.tensor_scalar(a, y, y, t, ALU.mult, ALU.mult))
    link(v.tensor_scalar(b, a, 0.375, -1.25, ALU.mult, ALU.add))
    link(v.tensor_scalar(a, a, b, 1.875, ALU.mult, ALU.add))
    link(v.tensor_tensor(y, y, a, ALU.mult))
    link(v.tensor_scalar(a, y, y, t, ALU.mult, ALU.mult))
    link(v.tensor_scalar(a, a, -0.5, 1.5, ALU.mult, ALU.add))
    link(v.tensor_tensor(y, y, a, ALU.mult))


def layer_norm(v, link, out, x, st, stats, eps=LN_EPS):
    link(v.bn_stats(stats[:, :], x))
    link(v.bn_aggr(st[:, 0:2], stats[:, :]))
    layer_norm_scale(v, link, st, eps)
    return v.tensor_scalar(out, x, st[:, 0:1], st[:, 3:4], ALU.subtract, ALU.mult)


def perceiver(nc, a, out):
    with ExitStack() as ctx:
        def sb(name, shape, dt=F32, scope=ctx):
            return scope.enter_context(nc.sbuf_tensor(name, shape, dt))

        def sem(name):
            return ctx.enter_context(nc.semaphore(name))

        x = sb("x", [P, D])
        z = sb("z", [P, D])
        y = sb("y", [P, D])
        zT = sb("zT", [P, DC, S])
        ident = sb("ident", [P, P])
        st = sb("st", [P, 8])
        stats = sb("stats", [P, 6])
        rows = sb("rows", [P, NROWS, D])
        cols = sb("cols", [P, NCOLS])
        gate = sb("gate", [P, 2])
        ca_w = {n: sb("ca_" + n, [P, DC, D]) for n in ("wq", "wk", "wv")}
        tf_wq = {n: sb("tf_" + n, [P, 2 * INNER], BF16) for n in ("gate", "up", "down")}
        tf_mean = sb("tf_mean", [P, 3])
        ps = ctx.enter_context(nc.psum_tensor("ps", [P, 8, 512], F32))

        vlink = Linker(None, sem("vector_chain"))
        alink = Linker(None, sem("scalar_chain"))
        plink = Linker(None, sem("pool_chain"))
        links = (vlink, alink, plink)
        stored = sem("stored")
        shared = {n: sem(n) for n in ("z_ready", "zT_done", "zT_ready", "out_done", "logits_done", "max_ready",
                                      "exp_ready", "turned", "turned_copied")}
        loaded = {n: sem("loaded_" + n) for n in ("x", "ln_rows", "rows", "wq", "wk", "wv", "w_out", "ca")}
        base = (x, z, y, zT, ident, st, stats, rows, cols, ps)

        first_cross_attention(nc, ctx, a, sb, sem, *base[:9], gate, ps, *links, shared, loaded, ca_w, tf_wq, tf_mean)
        with ExitStack() as late:
            ss = scan_weights(a, late, sb, sem)
            with ExitStack() as mid:
                xa = context_stream(a, mid, sb, sem)
                causal_attention(nc, a, sb, sem, base, links, shared, ca_w, xa)
                ternary_ffn(nc, a, sb, sem, base, links, shared, tf_wq, tf_mean, ss)
                second_cross_attention(nc, a, sb, sem, base, links, shared, xa)
            me = expert_weights(a, late, sb, sem)
            selective_scan(nc, a, sb, sem, base, links, shared, ss, me)
            expert_ffn(nc, a, sb, sem, base, links, shared, me)

        with nc.Block() as block:
            @block.sync
            def _(sp):
                sp.dma_start(out, x[:, :]).then_inc(stored, 16)
                sp.wait_ge(stored, 16)


def first_cross_attention(nc, ctx, a, sb, sem, x, z, y, zT, ident, st, stats, rows, cols, gate, ps,
                          vlink, alink, plink, shared, loaded, ca_w, tf_wq, tf_mean):
    with ExitStack() as own:
        def t(name, shape, dt=F32):
            return sb(name, shape, dt, own)

        wq = t("wq", [P, DC, INNER])
        wk = t("wk", [P, DC, INNER])
        wv = t("wv", [P, DC, INNER])
        wk_hi = t("wk_hi", [P, DC, INNER], F32R)
        wk_lo = t("wk_lo", [P, DC, INNER], F32R)
        wv_hi = t("wv_hi", [P, DC, INNER], F32R)
        wv_lo = t("wv_lo", [P, DC, INNER], F32R)
        wv_abs = t("wv_abs", [P, DC])
        wv_bound = t("wv_bound", [P, DC, P])
        q_hi = t("q_hi", [P, H0, S], F32R)
        q_lo = t("q_lo", [P, H0, S], F32R)
        k_st = t("k_st", [P, 2, 2, CH], F32R)
        k_raw = t("k_raw", [P, 2, HCH])
        c_raw = t("c_raw", [P, DC, CH])
        c_hi = t("c_hi", [P, 2, DC, CH], F32R)
        c_lo = t("c_lo", [P, 2, DC, CH], F32R)
        c_abs = t("c_abs", [P, 2, DC])
        v_scale = t("v_scale", [P, 2])
        v_unscale = t("v_unscale", [P, 2])
        v_hi = t("v_hi", [P, TILES, H0, VW], F16)
        v_lo = t("v_lo", [P, TILES, H0, VW], F16)
        p_exp = t("p_exp", [P, 2, CH])
        pT_hi = t("pT_hi", [P, 2, TILES, S], F16)
        pT_lo = t("pT_lo", [P, 2, TILES, S], F16)
        neg_row = t("neg_row", [P, 2])
        neg_max = t("neg_max", [P, 2, H0])
        drop = t("drop", [P, H0])
        decay = t("decay", [P, H0])
        acc = t("acc", [P, H0, DH + 1])
        rec = t("rec", [P, H0])
        tf_raw = {"gate": wq.rearrange("p c n -> p (c n)"), "up": wv.rearrange("p c n -> p (c n)"),
                  "down": wk.rearrange("p c n -> p (c n)")}
        tf_sum, tf_inv = t("tf_sum", [P, 6]), t("tf_per_mean", [P, 3])
        tf_ones = t("tf_ones", [P, P])

        def tf_half(w, k, half):
            return w[TERNARY[k]][:, half * INNER:(half + 1) * INNER]

        o, oT = wq[:, 0, :], wv.rearrange("p c (j s) -> p (c j) s", s=S)
        w_out = wk.rearrange("p c (j n) -> p (c j) n", n=D)
        tg = t("tg", [P, 1])
        one = t("one", [P, 1, 1])

        q_twice = [tf_wq[n].bitcast(F32).rearrange("p (h t e) -> p h t e", t=2, e=DH) for n in ("gate", "up")]

        s_scores = ps[:, 0:2, 0:HCH]
        s_k = ps[:, 2, 0:HCH]
        s_t = [ps[:, 4, :], ps[:, 5, :]]
        s_v = ps[:, 6, :]
        s_pv = [ps[:, b, 0:4 * (DH + 1)].rearrange("p (h e) -> p h e", e=DH + 1) for b in (7, 3)]

        raw_loaded = sem("raw_loaded")
        ident_ready = sem("ident_ready")
        qn_done, q_twice_ready = sem("qn_done"), [sem("q_twice_ready0"), sem("q_twice_ready1")]
        q_done, q_hi_ready, q_ready = sem("q_done"), sem("q_hi_ready"), sem("q_ready")
        wk_hi_ready, wk_ready = sem("wk_hi_ready"), sem("wk_ready")
        k_written, k_raw_ready, k_even_high = sem("k_written"), sem("k_raw_ready"), sem("k_even_high")
        k_odd_high, k_ready = sem("k_odd_high"), sem("k_ready")
        wv_hi_ready, wv_ready = sem("wv_hi_ready"), sem("wv_ready")
        bound_w_ready, ones_ready = sem("bound_w_ready"), sem("ones_ready")
        split_done, absmax_done, scale_ready = sem("split_done"), sem("absmax_done"), sem("scale_ready")
        scores_done, neg_max_ready, exp_done = sem("scores_done"), sem("neg_max_ready"), sem("exp_done")
        row_max_done = sem("row_max_done")
        t0_done, t1_done = sem("t0_done"), sem("t1_done")
        pT_hi_ready, pT_lo_ready = sem("pT_hi_ready"), sem("pT_lo_ready")
        v_bank_written, v_bank_free, v_hi_ready = sem("v_bank_written"), sem("v_bank_free"), sem("v_hi_ready")
        pv_done, drop_ready, decay_ready = sem("pv_done"), sem("drop_ready"), sem("decay_ready")
        acc_scaled, acc_num, flushed = sem("acc_scaled"), sem("acc_num"), sem("flushed")
        o_ready, oT_done, oT_ready = sem("o_ready"), sem("oT_done"), sem("oT_ready")
        gate_ready, table_loaded = sem("gate_ready"), sem("table_loaded")
        split_hi = sem("split_hi")
        tf_loaded = {n: sem("tf_loaded_" + n) for n in ("gate", "up", "down")}
        tf_summed, tf_total, tf_mean_ready = sem("tf_summed"), sem("tf_total"), sem("tf_mean_ready")
        tf_scaled, tf_rounded, tf_quantised = sem("tf_scaled"), sem("tf_rounded"), sem("tf_quantised")

        ctxT = a["ctxT"].rearrange("(c p) k -> p c k", p=P)
        rows_dram = a["rows"].rearrange("(o r) d -> o r d", o=1)

        def chunk_pairs(engine, two_chunks):
            two_chunks(0, True, False)
            with engine.Fori(1, NCH // 2 - 1) as i:
                two_chunks(i * 2, False, False)
            two_chunks(NCH - 2, False, True)

        def steps(c0, last):
            for par in range(2):
                for h in range(H0):
                    c = c0 + par
                    yield c, par, h, c * H0 + h, last and par == 1

        def q_bank(g):
            return ps[:, (1, 7, 0, 4)[g], :].rearrange("p (h s) -> p h s", h=4)

        def k_bank(u, early):
            return ps[:, 2 + u % 2, 0:HCH] if early else s_k

        def k_keys(u):
            return slice(u % 2 * HCH, (u % 2 + 1) * HCH)

        def k_step(c, par, h):
            u = h + K_AHEAD
            return (par, u) if u < H0 else (1 - par, u - H0)

        def v_use(c, h):
            return c * 15 + (7 + h)

        def v_bank(use, early):
            return ps[:, (6, 5, 4)[use % 3], :] if early else s_v

        def v_tile(c, h):
            return c * 14 + (6 + h if h < 8 else 5 + h)

        with nc.Block() as block:
            @block.sync
            def _(sp):
                sp.dma_start(x[:, :], a["x"]).then_inc(loaded["x"], 16)
                sp.dma_start(rows[:, 0:R_BOUT, :], rows_dram[:, 0:R_BOUT, :].to_broadcast([P, R_BOUT, D])).then_inc(loaded["ln_rows"], 16)
                sp.dma_start(c_raw[:, :, :], ctxT[:, :, 0:CH]).then_inc(raw_loaded, 16)
                sp.dma_start(rows[:, R_BOUT:, :], rows_dram[:, R_BOUT:, :].to_broadcast([P, NROWS - R_BOUT, D])).then_inc(loaded["rows"], 16)
                sp.dma_start(gate[:, 0:1], a["gate"].to_broadcast([P, 1])).then_inc(loaded["rows"], 16)
                sp.dma_start(cols[:, :], a["cols"]).then_inc(loaded["rows"], 16)
                for n in ("wq", "wk", "wv"):
                    sp.dma_start(ca_w[n][:, :, :], a["ca_" + n].rearrange("(c p) n -> p c n", p=P)).then_inc(loaded["ca"], 16)

                def tf_load(n):
                    w = a["tf_" + n].rearrange("(c p) n -> p c n", p=P)
                    sp.dma_start(tf_raw[n].rearrange("p (c n) -> p c n", c=w.shape[1]), w).then_inc(tf_loaded[n], 16)

                sp.wait_ge(qn_done, 2)
                tf_load("gate")
                sp.wait_ge(wv_ready, 1)
                sp.wait_ge(bound_w_ready, 1)
                tf_load("up")
                sp.wait_ge(wk_ready, 1)
                tf_load("down")

                def two_chunks(c0, first, last):
                    for par in range(2):
                        if last and par == 1:
                            break
                        c = c0 + par
                        sp.wait_ge(split_done, c * 4 + 4)
                        sp.wait_ge(absmax_done, c * 2 + 2)
                        sp.dma_start(c_raw[:, :, :], ctxT[:, :, bass.ds((c + 1) * CH, CH)]).then_inc(raw_loaded, 16)

                chunk_pairs(sp, two_chunks)
                sp.wait_ge(tf_quantised, 6)
                sp.dma_start(w_out, a["w_out"].rearrange("(c p) n -> p c n", p=P)).then_inc(loaded["w_out"], 16)

            @block.gpsimd
            def _(pool):
                link = plink.on(pool)
                link(nc.gpsimd.memset(ident[:, :], 0.0))
                nc.gpsimd.affine_select(out=ident[:, :], in_=ident[:, :], compare_op=ALU.not_equal, fill=1.0, base=0,
                                        pattern=[[-1, P]], channel_multiplier=1).then_inc(ident_ready, 1)
                nc.gpsimd.memset(v_hi[:, :, :, DH:VW], 1.0).then_inc(ones_ready, 1)
                nc.gpsimd.memset(acc[:, :, :], 0.0).then_inc(ones_ready, 1)
                nc.gpsimd.memset(one[:, :, :], 1.0).then_inc(ones_ready, 1)
                nc.gpsimd.memset(tf_ones[:, :], 1.0).then_inc(ones_ready, 1)
                nc.gpsimd.memset(neg_max[:, 1, :], BIG).then_inc(ones_ready, 1)

                def split(c, par, k):
                    part = (slice(None), par, k // 2 % 2, k_keys(k))
                    raw = c_raw[:, k // 2 % 2, k_keys(k)]
                    if k == 0:
                        pool.wait_ge(k_written, (c - 1) * H0)
                        pool.wait_ge(raw_loaded, (c + 1) * 16)
                    if k < 4:
                        nc.gpsimd.tensor_tensor(c_hi[part], raw, one[:, 0, :].to_broadcast([P, HCH]), ALU.mult).then_inc(split_hi, 1)
                        pool.wait_ge(split_hi, c * 4 + (k + 1))
                    else:
                        nc.gpsimd.tensor_tensor(c_lo[part], raw, c_hi[part].bitcast(F32), ALU.subtract).then_inc(split_done, 1)
                        pool.wait_ge(split_done, c * 4 + (k - 3))

                def k_split(number, u):
                    keys, tile = k_keys(u), u // 2 % 2
                    pool.wait_ge(k_raw_ready, number - (K_AHEAD - 1))
                    nc.gpsimd.tensor_tensor(k_st[DH:P, tile, 1, keys], k_raw[DH:P, u % 2, :], one[DH:P, 0, :].to_broadcast([DH, HCH]),
                                            ALU.mult).then_inc(k_odd_high, 1)
                    pool.wait_ge(k_even_high, number + 1)
                    pool.wait_ge(k_odd_high, number + 1)
                    nc.gpsimd.tensor_tensor(k_st[DH:P, tile, 0, keys], k_raw[0:DH, u % 2, :], k_st[0:DH, tile, 0, keys].bitcast(F32),
                                            ALU.subtract).then_inc(k_ready, 1)
                    pool.wait_ge(k_ready, number * 2 + 1)
                    nc.gpsimd.tensor_tensor(k_st[0:DH, tile, 1, keys], k_raw[DH:P, u % 2, :], k_st[DH:P, tile, 1, keys].bitcast(F32),
                                            ALU.subtract).then_inc(k_ready, 1)
                    pool.wait_ge(k_ready, number * 2 + 2)

                def two_chunks(c0, first, last):
                    for c, par, h, n, end in steps(c0, last):
                        if not (end and h + K_AHEAD >= H0):
                            k_split(n + K_AHEAD, k_step(c, par, h)[1])
                        if h < 8 and not end:
                            split(c + 1, 1 - par, h)
                        if h % 4 == 3:
                            g = h // 4
                            pool.wait_ge(decay_ready, c * 4 + (g + 1))
                            at_least(pool, flushed, (c - 1) * 4 + (g + 1))
                            grp = acc[:, 4 * g:4 * g + 4, :]
                            nc.gpsimd.tensor_tensor(grp, grp, decay[:, 4 * g:4 * g + 4].unsqueeze(2).to_broadcast([P, 4, DH + 1]),
                                                    ALU.mult).then_inc(acc_scaled, 1)
                            pool.wait_ge(acc_scaled, c * 4 + (g + 1))

                pool.wait_ge(ones_ready, 5)
                pool.wait_ge(split_hi, 4)
                nc.gpsimd.tensor_tensor(c_lo[:, 0, :, :], c_raw[:, :, :], c_hi[:, 0, :, :].bitcast(F32), ALU.subtract).then_inc(split_done, 4)
                pool.wait_ge(loaded["wv"], 16)
                pool.wait_ge(wv_hi_ready, 1)
                nc.gpsimd.tensor_tensor(wv_lo[:, :, :], wv[:, :, :], wv_hi[:, :, :].bitcast(F32), ALU.subtract).then_inc(wv_ready, 1)
                pool.wait_ge(wv_ready, 1)
                chunk_pairs(pool, two_chunks)

            @block.scalar
            def _(act):
                act.dma_start(wk[:, :, :], a["wk"].rearrange("(c p) n -> p c n", p=P)).then_inc(loaded["wk"], 16)
                act.dma_start(wq[:, :, :], a["wq"].rearrange("(c p) n -> p c n", p=P)).then_inc(loaded["wq"], 16)
                act.dma_start(wv[:, :, :], a["wv"].rearrange("(c p) n -> p c n", p=P)).then_inc(loaded["wv"], 16)
                act.wait_ge(ones_ready, 5)
                nc.scalar.activation(tg[:, :], one[:, 0, :], ACT.Exp).then_inc(table_loaded, 1)
                act.wait_ge(loaded["wk"], 16)
                nc.scalar.activation(wk_hi[:, :, :], wk[:, :, :], ACT.Copy).then_inc(wk_hi_ready, 1)
                act.wait_ge(raw_loaded, 16)
                nc.scalar.activation(c_hi[:, 0, :, :], c_raw[:, :, :], ACT.Copy).then_inc(split_hi, 4)
                act.wait_ge(shared["zT_done"], 1)
                nc.scalar.activation(zT[:, :, :], ps[:, 0, 0:DC * S].rearrange("p (c s) -> p c s", c=DC), ACT.Copy).then_inc(shared["zT_ready"], 1)
                act.wait_ge(loaded["wv"], 16)
                nc.scalar.activation(wv_hi[:, :, :], wv[:, :, :], ACT.Copy).then_inc(wv_hi_ready, 1)

                def v_high(tile, half, par, use, early=False):
                    act.wait_ge(v_bank_written, use + 1)
                    nc.scalar.activation(v_hi[:, tile, 8 * half:8 * half + 8, 0:DH],
                                         v_bank(use, early).rearrange("p (h e) -> p h e", e=DH), ACT.Copy,
                                         scale=v_scale[:, par:par + 1]).then_inc(v_hi_ready, 1)

                def exponent(n, h, par):
                    act.wait_ge(neg_max_ready, n + 1)
                    at_least(act, t1_done, n - 1)
                    nc.scalar.activation(p_exp[:, h % 2, :].rearrange("p (b k) -> p b k", b=2), s_scores, ACT.Exp,
                                         bias=neg_max[:, par, h:h + 1]).then_inc(exp_done, 1)

                def k_copy(number, u):
                    act.wait_ge(k_written, number + 1)
                    act.wait_ge(k_ready, number * 2 - 2)
                    nc.scalar.activation(k_raw[:, u % 2, :], s_k, ACT.Copy).then_inc(k_raw_ready, 1)
                    nc.scalar.activation(k_st[0:DH, u // 2 % 2, 0, k_keys(u)], s_k[0:DH, :], ACT.Copy).then_inc(k_even_high, 1)

                act.wait_ge(qn_done, 1)
                nc.scalar.activation(q_twice[0], ps[:, 4, :].rearrange("p (h o e) -> p h o e", o=1, e=DH).to_broadcast([P, 8, 2, DH]),
                                     ACT.Copy).then_inc(q_twice_ready[0], 1)
                for g in range(4):
                    act.wait_ge(q_done, g + 1)
                    nc.scalar.activation(q_hi[:, 4 * g:4 * g + 4, :], q_bank(g), ACT.Copy, scale=DH ** -0.5).then_inc(q_hi_ready, 1)
                for u in range(K_AHEAD):
                    act.wait_ge(k_written, u + 1)
                    for side, high in ((0, k_even_high), (1, k_odd_high)):
                        r = DH * side
                        nc.scalar.activation(k_st[r:r + DH, u // 2 % 2, side, k_keys(u)], k_bank(u, True)[r:r + DH, :], ACT.Copy).then_inc(high, 1)
                act.wait_ge(scale_ready, 1)
                for k in range(TILES):
                    if k == 2:
                        exponent(0, 0, 0)
                    v_high(k, 0, 0, 1 + k, True)

                def two_chunks(c0, first, last):
                    for c, par, h, n, end in steps(c0, last):
                        if not (end and h + K_AHEAD >= H0):
                            k_copy(n + K_AHEAD, k_step(c, par, h)[1])
                        if not (end and h == H0 - 1):
                            exponent(n + 1, (h + 1) % H0, par if h < H0 - 1 else 1 - par)
                        if 0 < h < 8:
                            if h == 1:
                                at_least(act, pv_done, c * H0)
                            v_high(h - 1, 1, par, v_use(c, h))
                        elif h > 8 and not end:
                            if h == 9:
                                act.wait_ge(pv_done, c * H0 + 8)
                                act.wait_ge(scale_ready, c + 2)
                            v_high(h - 9, 0, 1 - par, v_use(c, h))
                        if h % 4 == 3:
                            g = h // 4
                            act.wait_ge(drop_ready, c * 4 + (g + 1))
                            at_least(act, acc_scaled, (c - 1) * 4 + (g + 1))
                            nc.scalar.activation(decay[:, 4 * g:4 * g + 4], drop[:, 4 * g:4 * g + 4], ACT.Exp).then_inc(decay_ready, 1)
                        at_least(act, pv_done, n - 1)
                        act.wait_ge(t0_done, n + 1)
                        nc.scalar.activation(pT_hi[:, h % 2, 0:T0, :], s_t[0].rearrange("p (t s) -> p t s", t=T0), ACT.Copy).then_inc(pT_hi_ready, 1)
                        act.wait_ge(t1_done, n + 1)
                        nc.scalar.activation(pT_hi[:, h % 2, T0:TILES, :], s_t[1][:, 0:(TILES - T0) * S].rearrange("p (t s) -> p t s", s=S),
                                             ACT.Copy).then_inc(pT_hi_ready, 1)
                        if first and par == 0 and h in TF_SUM_STEPS:
                            k = TF_SUM_STEPS.index(h)
                            w, name = tf_half(tf_raw, k // 2, k % 2), TERNARY[k // 2]
                            act.wait_ge(tf_loaded[name], 16)
                            nc.scalar.activation(tf_half(tf_wq, k // 2, k % 2), w, ACT.Abs, accum_out=tf_sum[:, k:k + 1]).then_inc(tf_summed, 1)
                        if last and par == 0 and 1 <= h <= 12:
                            j = h - 1
                            w = tf_half(tf_raw, j // 4, j % 2)
                            if j % 4 < 2:
                                nc.scalar.activation(w, w, ACT.Copy, scale=tf_inv[:, j // 4:j // 4 + 1]).then_inc(tf_scaled, 1)
                            else:
                                act.wait_ge(tf_scaled, j - 1)
                                nc.scalar.activation(w, w, ACT.Copy, bias=ROUND).then_inc(tf_scaled, 1)

                chunk_pairs(act, two_chunks)
                act.wait_ge(loaded["rows"], 48)
                act.wait_ge(table_loaded, 1)
                nc.scalar.activation(tg[:, :], gate[:, 0:1], ACT.Tanh).then_inc(gate_ready, 1)
                for k in range(2):
                    act.wait_ge(oT_done, k + 1)
                    nc.scalar.activation(oT[:, 4 * k:4 * k + 4, :], ps[:, k, :].rearrange("p (j s) -> p j s", j=4), ACT.Copy).then_inc(oT_ready, 1)

            @block.vector
            def _(v):
                link = vlink.on(v)
                v.wait_ge(loaded["x"], 16)
                link(layer_norm(nc.vector, link, z[:, :], x[:, :], st, stats))
                link(layer_norm(nc.vector, link, y[:, :], z[:, :], st, stats))
                v.wait_ge(loaded["ln_rows"], 16)
                link(nc.vector.tensor_tensor(y[:, :], y[:, :], rows[:, R_LN_G, :], ALU.mult))
                nc.vector.tensor_tensor(y[:, :], y[:, :], rows[:, R_LN_B, :], ALU.add).then_inc(shared["z_ready"], 1)

                def absmax(c, par, k):
                    v.wait_ge(raw_loaded, (c + 1) * 16)
                    nc.vector.tensor_reduce(c_abs[:, par, k:k + 1], c_raw[:, k, :], AX.X, ALU.max,
                                            apply_absolute_value=True).then_inc(absmax_done, 1)

                def scale(c, par, use):
                    v.wait_ge(v_bank_written, use + 1)
                    nc.vector.tensor_scalar(v_unscale[:, par:par + 1], s_v[:, 0:1], 1.0 / V_TOP, 1e-30, ALU.mult, ALU.max).then_inc(v_bank_free, 1)
                    v.wait_ge(v_bank_free, use + 1)
                    nc.vector.reciprocal(v_scale[:, par:par + 1], v_unscale[:, par:par + 1]).then_inc(scale_ready, 1)

                def v_low(tile, half, par, use, number, early=False):
                    v.wait_ge(v_hi_ready, number + 1)
                    nc.vector.scalar_tensor_tensor(out=v_lo[:, tile, 8 * half:8 * half + 8, 0:DH],
                                                   in0=v_bank(use, early).rearrange("p (h e) -> p h e", e=DH), scalar=v_scale[:, par:par + 1],
                                                   in1=v_hi[:, tile, 8 * half:8 * half + 8, 0:DH],
                                                   op0=ALU.mult, op1=ALU.subtract).then_inc(v_bank_free, 1)

                def row_max(n, h, par):
                    v.wait_ge(scores_done, n + 1)
                    nc.vector.tensor_reduce(neg_row[:, h % 2:h % 2 + 1], s_scores, AX.XY, ALU.max, negate=True).then_inc(row_max_done, 1)
                    v.wait_ge(row_max_done, n + 1)
                    nc.vector.scalar_tensor_tensor(out=neg_max[:, par, h:h + 1], in0=neg_row[:, h % 2:h % 2 + 1], scalar=LN_K,
                                                   in1=neg_max[:, 1 - par, h:h + 1], op0=ALU.add, op1=ALU.min).then_inc(neg_max_ready, 1)

                def p_low(n, h):
                    for b, (t0, t1) in enumerate(((0, T0), (T0, TILES))):
                        v.wait_ge(pT_hi_ready, n * 2 + (b + 1))
                        nc.vector.tensor_tensor(pT_lo[:, h % 2, t0:t1, :], s_t[b][:, 0:(t1 - t0) * S].rearrange("p (t s) -> p t s", s=S),
                                                pT_hi[:, h % 2, t0:t1, :], ALU.subtract).then_inc(pT_lo_ready, 1)

                def flush(f, g, par):
                    v.wait_ge(pv_done, (f + 1) * 4)
                    v.wait_ge(acc_scaled, f + 1)
                    nc.vector.scalar_tensor_tensor(out=acc[:, 4 * g:4 * g + 4, 0:DH], in0=s_pv[g % 2][:, :, 0:DH],
                                                   scalar=v_unscale[:, par:par + 1], in1=acc[:, 4 * g:4 * g + 4, 0:DH],
                                                   op0=ALU.mult, op1=ALU.add).then_inc(acc_num, 1)
                    nc.vector.tensor_tensor(acc[:, 4 * g:4 * g + 4, DH:DH + 1], acc[:, 4 * g:4 * g + 4, DH:DH + 1],
                                            s_pv[g % 2][:, :, DH:DH + 1], ALU.add).then_inc(flushed, 1)

                v.wait_ge(loaded["wk"], 16)
                v.wait_ge(wk_hi_ready, 1)
                nc.vector.tensor_tensor(wk_lo[:, :, :], wk[:, :, :], wk_hi[:, :, :].bitcast(F32), ALU.subtract).then_inc(wk_ready, 1)

                absmax(0, 0, 0)
                absmax(0, 0, 1)
                v.wait_ge(qn_done, 2)
                nc.vector.tensor_copy(q_twice[1], ps[:, 5, :].rearrange("p (h o e) -> p h o e", o=1, e=DH).to_broadcast([P, 8, 2, DH])).then_inc(q_twice_ready[1], 1)

                for g in range(4):
                    v.wait_ge(q_hi_ready, g + 1)
                    nc.vector.scalar_tensor_tensor(out=q_lo[:, 4 * g:4 * g + 4, :], in0=q_bank(g), scalar=DH ** -0.5,
                                                   in1=q_hi[:, 4 * g:4 * g + 4, :].bitcast(F32), op0=ALU.mult, op1=ALU.subtract).then_inc(q_ready, 1)
                v.wait_ge(loaded["wv"], 16)
                link(nc.vector.tensor_reduce(wv_abs[:, :], wv[:, :, :], AX.X, ALU.max, apply_absolute_value=True))
                nc.vector.tensor_copy(wv_bound[:, :, :], wv_abs[:, :].unsqueeze(2).to_broadcast([P, DC, P])).then_inc(bound_w_ready, 1)
                for u in range(K_AHEAD):
                    for side, high in ((0, k_even_high), (1, k_odd_high)):
                        r, other = DH * side, DH * (1 - side)
                        v.wait_ge(high, u + 1)
                        nc.vector.tensor_tensor(k_st[other:other + DH, u // 2 % 2, side, k_keys(u)], k_bank(u, True)[r:r + DH, :],
                                                k_st[r:r + DH, u // 2 % 2, side, k_keys(u)].bitcast(F32), ALU.subtract).then_inc(k_ready, 1)
                scale(0, 0, 0)
                v.wait_ge(ones_ready, 5)
                for k in range(TILES):
                    if k == 2:
                        row_max(0, 0, 0)
                    v_low(k, 0, 0, 1 + k, k, True)

                def two_chunks(c0, first, last):
                    for c, par, h, n, end in steps(c0, last):
                        if h % 4 == 3:
                            g = h // 4
                            at_least(v, decay_ready, (c - 1) * 4 + (g + 1))
                            v.wait_ge(neg_max_ready, n + 1)
                            nc.vector.tensor_tensor(drop[:, 4 * g:4 * g + 4], neg_max[:, par, 4 * g:4 * g + 4],
                                                    neg_max[:, 1 - par, 4 * g:4 * g + 4], ALU.subtract).then_inc(drop_ready, 1)
                        if not (first and par == 0 and h == 0):
                            p_low(n - 1, (h - 1) % H0)
                        if not (end and h == H0 - 1):
                            row_max(n + 1, (h + 1) % H0, par if h < H0 - 1 else 1 - par)
                        if h % 4 == 1 and not (first and par == 0 and h == 1):
                            flush(c * 4 + (h // 4 - 1), (h // 4 - 1) % 4, par if h > 1 else 1 - par)
                        if last and par == 0 and h in (5, 6, 9, 10, 13, 14):
                            k, half = h // 4 - 1, h % 4 - 1
                            v.wait_ge(tf_scaled, 4 * k + 3 + half)
                            w = tf_half(tf_raw, k, half)
                            nc.vector.tensor_scalar(w, w, ROUND, 1.0, ALU.subtract, ALU.min).then_inc(tf_rounded, 1)
                        if last and par == 1 and 1 <= h <= 6:
                            k, half = (h - 1) // 2, (h - 1) % 2
                            v.wait_ge(tf_rounded, h)
                            nc.vector.tensor_scalar(tf_half(tf_wq, k, half), tf_half(tf_raw, k, half), -1.0, None,
                                                    ALU.max).then_inc(tf_quantised, 1)
                        if h in (2, 4) and not end:
                            absmax(c + 1, 1 - par, h // 2 - 1)
                        if 0 < h < 8:
                            v_low(h - 1, 1, par, v_use(c, h), v_tile(c, h))
                        elif h == 8 and not end:
                            scale(c + 1, 1 - par, v_use(c, h))
                        elif h > 8 and not end:
                            v_low(h - 9, 0, 1 - par, v_use(c, h), v_tile(c, h))
                        if first and par == 1 and h == 0:
                            v.wait_ge(tf_total, 1)
                            link(nc.vector.tensor_reduce(tf_mean[:, :], s_v[:, 0:6].rearrange("p (k b) -> p k b", b=2), AX.X, ALU.add))
                            link(nc.vector.tensor_scalar(tf_mean[:, :], tf_mean[:, :], 1.0 / (D * INNER), 1e-5, ALU.mult, ALU.max))
                            nc.vector.reciprocal(tf_inv[:, :], tf_mean[:, :]).then_inc(tf_mean_ready, 1)

                chunk_pairs(v, two_chunks)
                p_low(NCH * H0 - 1, H0 - 1)
                flush(NCH * 4 - 1, 3, 1)
                v.wait_ge(flushed, NCH * 4)
                v.wait_ge(acc_num, NCH * 4)
                link(nc.vector.reciprocal(rec[:, :], acc[:, :, DH]))
                nc.vector.tensor_tensor(o[:, :].rearrange("p (h e) -> p h e", e=DH), acc[:, :, 0:DH],
                                        rec[:, :].unsqueeze(2).to_broadcast([P, H0, DH]), ALU.mult).then_inc(o_ready, 1)
                v.wait_ge(shared["out_done"], 1)
                link(nc.vector.tensor_tensor(y[:, :], ps[:, 2, 0:D], rows[:, R_BOUT, :], ALU.add))
                v.wait_ge(loaded["ca"], 48)
                v.wait_ge(gate_ready, 1)
                link(nc.vector.scalar_tensor_tensor(out=x[:, :], in0=y[:, :], scalar=tg[:, 0:1], in1=x[:, :], op0=ALU.mult, op1=ALU.add))

            @block.tensor
            def _(pe):
                def v_project(tile, half, par, use, early=False):
                    at_least(pe, v_bank_free, use - 2 if early else use)
                    k = 0
                    for c in range(DC):
                        lh = c_hi[:, par, c, tile * P:(tile + 1) * P]
                        ll = c_lo[:, par, c, tile * P:(tile + 1) * P]
                        rh = wv_hi[:, c, 512 * half:512 * half + 512]
                        rl = wv_lo[:, c, 512 * half:512 * half + 512]
                        for lhs, rhs in ((lh, rh), (lh, rl), (ll, rh)):
                            mm = nc.tensor.matmul(v_bank(use, early), lhs, rhs, start=(k == 0), stop=(k == 5))
                            k += 1
                    mm.then_inc(v_bank_written, 1)

                def bound(par, use):
                    at_least(pe, v_bank_free, use)
                    for c in range(DC):
                        mm = nc.tensor.matmul(s_v[:, 0:1], wv_bound[:, c, :], c_abs[:, par, c:c + 1], start=(c == 0), stop=(c == DC - 1))
                    mm.then_inc(v_bank_written, 1)

                def k_project(number, par, u, early=False):
                    if early:
                        at_least(pe, k_ready, number * 2 - 2)
                    else:
                        pe.wait_ge(k_even_high, number)
                    m, b = u // 2, u % 2
                    k = 0
                    for c in range(DC):
                        lh, ll = wk_hi[:, c, m * P:(m + 1) * P], wk_lo[:, c, m * P:(m + 1) * P]
                        rh, rl = c_hi[:, par, c, b * HCH:(b + 1) * HCH], c_lo[:, par, c, b * HCH:(b + 1) * HCH]
                        for lhs, rhs in ((lh, rh), (lh, rl), (ll, rh)):
                            mm = nc.tensor.matmul(k_bank(u, early), lhs, rhs, start=(k == 0), stop=(k == 5))
                            k += 1
                    mm.then_inc(k_written, 1)

                def scores(n, h):
                    pe.wait_ge(k_ready, n * 2 + (4 if h % 2 == 0 else 2))
                    at_least(pe, exp_done, n)
                    for k, q in enumerate((q_hi, q_lo)):
                        for b in range(2):
                            mm = nc.tensor.matmul(s_scores[:, b, :], q[:, h, :], k_st[:, h // 2 % 2, h % 2, b * HCH:(b + 1) * HCH],
                                                  start=(k == 0), stop=(k == 1))
                    mm.then_inc(scores_done, 1)

                def weigh(n, h):
                    pe.wait_ge(pT_lo_ready, n * 2 + 2)
                    for tile in range(TILES):
                        ph, pl = pT_hi[:, h % 2, tile, :], pT_lo[:, h % 2, tile, :]
                        nc.tensor.matmul(s_pv[h // 4 % 2][:, h % 4, :], ph, v_hi[:, tile, h, 0:DH + 1], start=(tile == 0), stop=False)
                        nc.tensor.matmul(s_pv[h // 4 % 2][:, h % 4, 0:DH], ph, v_lo[:, tile, h, 0:DH], start=False, stop=False)
                        mm = nc.tensor.matmul(s_pv[h // 4 % 2][:, h % 4, :], pl, v_hi[:, tile, h, 0:DH + 1], start=False, stop=(tile == TILES - 1))
                    mm.then_inc(pv_done, 1)

                def transpose_p(n, h):
                    pe.wait_ge(exp_done, n + 1)
                    for tile in range(TILES):
                        b, s = (0, tile) if tile < T0 else (1, tile - T0)
                        mm = nc.tensor.transpose(s_t[b][:, s * S:(s + 1) * S], p_exp[:, h % 2, tile * P:(tile + 1) * P], ident[:, :])
                        if tile == T0 - 1:
                            mm.then_inc(t0_done, 1)
                    mm.then_inc(t1_done, 1)

                pe.wait_ge(ident_ready, 1)
                pe.wait_ge(shared["z_ready"], 1)
                for c in range(DC):
                    mm = nc.tensor.transpose(ps[:, 0, c * S:(c + 1) * S], y[:, c * P:(c + 1) * P], ident[:, :])
                mm.then_inc(shared["zT_done"], 1)
                pe.wait_ge(shared["zT_ready"], 1)
                pe.wait_ge(loaded["wq"], 16)
                for k in range(2):
                    for c in range(DC):
                        mm = nc.tensor.matmul(ps[:, 4 + k, :], zT[:, c, :], wq[:, c, 512 * k:512 * k + 512], start=(c == 0), stop=(c == DC - 1))
                    mm.then_inc(qn_done, 1)
                for g in range(4):
                    pe.wait_ge(q_twice_ready[g // 2], 1)
                    for i in range(4):
                        mm = nc.tensor.transpose(q_bank(g)[:, i, :], q_twice[g // 2][:, 4 * (g % 2) + i, :, :].rearrange("p t e -> p (t e)"), ident[:, :])
                    mm.then_inc(q_done, 1)
                pe.wait_ge(split_done, 4)
                pe.wait_ge(wk_ready, 1)
                for u in range(K_AHEAD):
                    k_project(u, 0, u, True)
                pe.wait_ge(bound_w_ready, 1)
                pe.wait_ge(absmax_done, 2)
                bound(0, 0)
                pe.wait_ge(q_ready, 4)
                scores(0, 0)
                pe.wait_ge(wv_ready, 1)
                for k in range(TILES):
                    v_project(k, 0, 0, 1 + k, True)

                def two_chunks(c0, first, last):
                    for c, par, h, n, end in steps(c0, last):
                        if not (end and h == H0 - 1):
                            scores(n + 1, (h + 1) % H0)
                        if first and par == 0 and h == 0:
                            pe.wait_ge(k_ready, K_AHEAD * 2)
                        if not (end and h + K_AHEAD >= H0):
                            k_project(n + K_AHEAD, *k_step(c, par, h))
                        if first and par == 1 and h == 1:
                            pe.wait_ge(tf_mean_ready, 1)
                        if 0 < h < 8:
                            v_project(h - 1, 1, par, v_use(c, h))
                        elif h == 8 and not end:
                            pe.wait_ge(absmax_done, c * 2 + 4)
                            bound(1 - par, v_use(c, h))
                        elif h > 8 and not end:
                            if h == 9:
                                pe.wait_ge(split_done, c * 4 + 8)
                            v_project(h - 9, 0, 1 - par, v_use(c, h))
                        elif first and par == 1 and h == 0:
                            pe.wait_ge(v_bank_free, v_use(c, 1))
                            pe.wait_ge(tf_summed, 6)
                            nc.tensor.matmul(s_v[:, 0:6], tf_ones[:, :], tf_sum[:, :], start=True, stop=True).then_inc(tf_total, 1)
                        if not (first and par == 0 and h == 0):
                            hp = (h - 1) % H0
                            if hp % 4 == 0:
                                at_least(pe, flushed, c * 4 + hp // 4 - 1)
                            if hp % 8 == 0:
                                pe.wait_ge(v_bank_free, c * 15 + (8 if hp == 0 else 15))
                            weigh(n - 1, hp)
                        if first and par == 0 and h == 0:
                            pe.wait_ge(v_bank_free, 8)
                        transpose_p(n, h)

                chunk_pairs(pe, two_chunks)
                weigh(NCH * H0 - 1, H0 - 1)
                pe.wait_ge(o_ready, 1)
                for k in range(2):
                    for j in range(4):
                        mm = nc.tensor.transpose(ps[:, k, j * S:(j + 1) * S], o[:, (4 * k + j) * P:(4 * k + j + 1) * P], ident[:, :])
                    mm.then_inc(oT_done, 1)
                pe.wait_ge(loaded["w_out"], 16)
                for k in range(8):
                    if k % 4 == 0:
                        pe.wait_ge(oT_ready, k // 4 + 1)
                    mm = nc.tensor.matmul(ps[:, 2, 0:D], oT[:, k, :], w_out[:, k, :], start=(k == 0), stop=(k == 7))
                mm.then_inc(shared["out_done"], 1)


def transpose_z(nc, pe, ps, z, ident, done):
    for c in range(DC):
        mm = nc.tensor.transpose(ps[:, 0, c * S:(c + 1) * S], z[:, c * P:(c + 1) * P], ident[:, :])
    mm.then_inc(done, 1)


RING = 4


class ContextStream:
    pass


def context_stream(a, scope, sb, sem):
    xa = ContextStream()
    xa.w = {n: sb("xa_" + n, [P, DC, D], F32, scope) for n in ("wq", "wkT", "wv")}
    xa.ct = sb("xa_ct", [P, RING, DC, CH], F32, scope)
    xa.cn = sb("xa_cn", [P, RING, TILES, D], F32, scope)
    xa.w_loaded = sem("xa_w_loaded")
    xa.ct_loaded = [sem("xa_ct_loaded%d" % k) for k in range(RING)]
    xa.cn_loaded = [sem("xa_cn_loaded%d" % k) for k in range(RING)]
    ctxT = a["ctxT"].rearrange("(c p) k -> p c k", p=P)
    ctxN = a["ctx"].rearrange("(n t p) d -> n p t d", t=TILES, p=P)

    def load_weights(sp):
        for n in xa.w:
            sp.dma_start(xa.w[n][:, :, :], a["xa_" + n].rearrange("(c p) n -> p c n", p=P)).then_inc(xa.w_loaded, 16)

    def load_ct(sp, c, slot):
        sp.dma_start(xa.ct[:, slot, :, :], ctxT[:, :, bass.ds(c * CH, CH)]).then_inc(xa.ct_loaded[slot], 16)

    def load_cn(sp, c, slot):
        sp.dma_start(xa.cn[:, slot, :, :], ctxN[bass.ds(c, 1), :, :, :].rearrange("o p t d -> p (o t) d")).then_inc(xa.cn_loaded[slot], 16)

    xa.load_weights, xa.load_ct, xa.load_cn = load_weights, load_ct, load_cn
    return xa


def causal_attention(nc, a, sb, sem, base, links, shared, w, xa):
    x, z, y, zT, ident, st, stats, rows, cols, ps = base
    vlink, alink, plink = links
    with ExitStack() as own:
        def t(name, shape, dt=F32):
            return sb("ca_" + name, shape, dt, own)

        qT, kT, val = t("qT", [P, DC, S]), t("kT", [P, DC, S]), t("val", [P, D])
        sc, p, pT = t("sc", [P, S]), t("p", [P, S]), t("pT", [P, S])
        neg_max, total, rec = t("neg_max", [P, 1]), t("total", [P, 1]), t("rec", [P, 1])
        E = {n: sem("ca_" + n) for n in ("proj_done", "q_ready", "kv_ready",
                                         "copied", "masked", )}
        with nc.Block() as block:
            @block.sync
            def _(sp):
                xa.load_weights(sp)
                for c in range(RING):
                    xa.load_ct(sp, c, c)
                for c in range(RING):
                    xa.load_cn(sp, c, c)

            @block.vector
            def _(v):
                link = vlink.on(v)
                layer_norm(nc.vector, link, z[:, :], x[:, :], st, stats).then_inc(shared["z_ready"], 1)
                v.wait_ge(shared["zT_done"], 2)
                nc.vector.tensor_copy(zT[:, :, :], ps[:, 0, 0:DC * S].rearrange("p (c s) -> p c s", c=DC)).then_inc(shared["zT_ready"], 1)
                v.wait_ge(E["proj_done"], 1)
                nc.vector.tensor_tensor(kT[:, :, :], ps[:, 2, 0:DC * S].rearrange("p (c s) -> p c s", c=DC),
                                        cols[:, C_A_BK:C_A_BK + DC].unsqueeze(2).to_broadcast([P, DC, S]), ALU.add).then_inc(E["kv_ready"], 1)
                nc.vector.tensor_tensor(val[:, :], ps[:, 3, 0:D], rows[:, R_A_BV, :], ALU.add).then_inc(E["kv_ready"], 1)
                v.wait_ge(E["masked"], 1)
                link(nc.vector.tensor_reduce(neg_max[:, :], sc[:, :], AX.X, ALU.max, negate=True))
                nc.vector.tensor_scalar(neg_max[:, :], neg_max[:, :], D ** -0.5, None, ALU.mult).then_inc(shared["max_ready"], 1)
                v.wait_ge(shared["exp_ready"], 1)
                link(nc.vector.reciprocal(rec[:, :], total[:, :]))
                v.wait_ge(shared["out_done"], 2)
                link(nc.vector.scalar_tensor_tensor(out=x[:, :], in0=ps[:, 6, 0:D], scalar=rec[:, 0:1], in1=x[:, :],
                                                    op0=ALU.mult, op1=ALU.add))

            @block.scalar
            def _(act):
                act.wait_ge(E["proj_done"], 1)
                for c in range(DC):
                    nc.scalar.activation(qT[:, c, :], ps[:, 1, c * S:(c + 1) * S], ACT.Identity,
                                         bias=cols[:, C_A_BQ + c:C_A_BQ + c + 1]).then_inc(E["q_ready"], 1)
                act.wait_ge(shared["logits_done"], 1)
                nc.scalar.activation(sc[:, :], ps[:, 4, 0:S], ACT.Copy).then_inc(E["copied"], 1)
                act.wait_ge(shared["max_ready"], 1)
                nc.scalar.activation(p[:, :], sc[:, :], ACT.Exp, bias=neg_max[:, 0:1], scale=D ** -0.5,
                                     accum_out=total[:, :]).then_inc(shared["exp_ready"], 1)
                act.wait_ge(shared["turned"], 1)
                nc.scalar.activation(pT[:, :], ps[:, 5, 0:S], ACT.Copy).then_inc(shared["turned_copied"], 1)

            @block.gpsimd
            def _(pool):
                pool.wait_ge(E["copied"], 1)
                nc.gpsimd.affine_select(out=sc[:, :], in_=sc[:, :], compare_op=ALU.is_ge, fill=-BIG, base=0,
                                        pattern=[[-1, S]], channel_multiplier=1).then_inc(E["masked"], 1)

            @block.tensor
            def _(pe):
                pe.wait_ge(shared["z_ready"], 2)
                transpose_z(nc, pe, ps, z, ident, shared["zT_done"])
                pe.wait_ge(shared["zT_ready"], 2)
                for bank, n in ((1, "wq"), (2, "wk")):
                    for e in range(DC):
                        for c in range(DC):
                            nc.tensor.matmul(ps[:, bank, e * S:(e + 1) * S], w[n][:, c, e * P:(e + 1) * P], zT[:, c, :],
                                             start=(c == 0), stop=(c == DC - 1))
                for c in range(DC):
                    mm = nc.tensor.matmul(ps[:, 3, 0:D], zT[:, c, :], w["wv"][:, c, :], start=(c == 0), stop=(c == DC - 1))
                mm.then_inc(E["proj_done"], 1)
                pe.wait_ge(E["q_ready"], 2)
                pe.wait_ge(E["kv_ready"], 2)
                for c in range(DC):
                    mm = nc.tensor.matmul(ps[:, 4, 0:S], qT[:, c, :], kT[:, c, :], start=(c == 0), stop=(c == DC - 1))
                mm.then_inc(shared["logits_done"], 1)
                pe.wait_ge(shared["exp_ready"], 1)
                nc.tensor.transpose(ps[:, 5, 0:S], p[:, :], ident[:, :]).then_inc(shared["turned"], 1)
                pe.wait_ge(shared["turned_copied"], 1)
                nc.tensor.matmul(ps[:, 6, 0:D], pT[:, :], val[:, :], start=True, stop=True).then_inc(shared["out_done"], 1)


def quantise_rows(v, link, q, src, am, inv):
    link(v.tensor_reduce(am[:, 0:1], src, AX.X, ALU.max, apply_absolute_value=True))
    link(v.tensor_scalar(am[:, 0:1], am[:, 0:1], 1e-5, None, ALU.max))
    link(v.reciprocal(am[:, 1:2], am[:, 0:1]))
    link(v.tensor_scalar(am[:, 1:2], am[:, 1:2], 127.0, None, ALU.mult))
    link(v.tensor_scalar(inv, am[:, 0:1], 1.0 / 127.0, None, ALU.mult))
    link(v.tensor_scalar(q, src, am[:, 1:2], ROUND, ALU.mult, ALU.add))
    link(v.tensor_scalar(q, q, ROUND, 127.0, ALU.subtract, ALU.min))
    return v.tensor_scalar(q, q, -128.0, None, ALU.max)


def ternary_ffn(nc, a, sb, sem, base, links, shared, wq, mean, ss):
    x, z, y, zT, ident, st, stats, rows, cols, ps = base
    vlink, alink, plink = links
    F = INNER
    with ExitStack() as own:
        def t(name, shape, dt=F32):
            return sb("tf_" + name, shape, dt, own)

        zqT = t("zqT", [P, DC, S], BF16)
        am, inv, sg = t("am", [P, 2]), t("inv", [P, 2]), t("sg", [P, 4])
        e, h, hqT = t("e", [P, F]), t("h", [P, F]), t("hqT", [P, 8, S], BF16)
        E = {n: sem("tf_" + n) for n in ("gu_done", "sg_ready", "e_ready", "hq_ready", "hT_done", "hT_ready")}
        with nc.Block() as block:
            @block.sync
            def _(sp):
                ss.load(sp)

            @block.scalar
            def _(act):
                act.wait_ge(E["sg_ready"], 1)
                act.wait_ge(E["gu_done"], 1)
                nc.scalar.activation(e[:, :].rearrange("p (b n) -> p b n", b=2), ps[:, 0:2, :], ACT.Tanh, scale=sg[:, 2:3]).then_inc(E["e_ready"], 1)
                for k in range(2):
                    act.wait_ge(E["hT_done"], k + 1)
                    nc.scalar.activation(hqT[:, 4 * k:4 * k + 4, :], ps[:, 5 + k, :].rearrange("p (j s) -> p j s", j=4), ACT.Copy).then_inc(E["hT_ready"], 1)

            @block.vector
            def _(v):
                link = vlink.on(v)
                link(layer_norm(nc.vector, link, z[:, :], x[:, :], st, stats))
                quantise_rows(nc.vector, link, y[:, :], z[:, :], am, inv[:, 0:1]).then_inc(shared["z_ready"], 1)
                link(nc.vector.tensor_tensor(sg[:, 0:2], mean[:, 0:2], inv[:, 0:1].to_broadcast([P, 2]), ALU.mult))
                nc.vector.tensor_scalar(sg[:, 2:3], sg[:, 0:1], 0.5, None, ALU.mult).then_inc(E["sg_ready"], 1)
                v.wait_ge(E["sg_ready"], 1)
                link(nc.vector.tensor_tensor(sg[:, 3:4], sg[:, 2:3], sg[:, 1:2], ALU.mult))
                v.wait_ge(shared["zT_done"], 3)
                nc.vector.tensor_copy(zqT[:, :, :], ps[:, 0, 0:DC * S].rearrange("p (c s) -> p c s", c=DC)).then_inc(shared["zT_ready"], 1)
                v.wait_ge(E["e_ready"], 1)
                gp = ps[:, 0:2, :].rearrange("p b n -> p (b n)")
                up = ps[:, 2:4, :].rearrange("p b n -> p (b n)")
                link(nc.vector.scalar_tensor_tensor(out=e[:, :], in0=e[:, :], scalar=1.0, in1=gp, op0=ALU.add, op1=ALU.mult))
                link(nc.vector.scalar_tensor_tensor(out=h[:, :], in0=up, scalar=sg[:, 3:4], in1=e[:, :], op0=ALU.mult, op1=ALU.mult))
                quantise_rows(nc.vector, link, h[:, :], h[:, :], am, inv[:, 1:2]).then_inc(E["hq_ready"], 1)
                link(nc.vector.tensor_tensor(sg[:, 3:4], mean[:, 2:3], inv[:, 1:2], ALU.mult))
                v.wait_ge(shared["out_done"], 3)
                link(nc.vector.scalar_tensor_tensor(out=x[:, :], in0=ps[:, 4, 0:D], scalar=sg[:, 3:4], in1=x[:, :],
                                                    op0=ALU.mult, op1=ALU.add))

            @block.tensor
            def _(pe):
                pe.wait_ge(shared["z_ready"], 3)
                transpose_z(nc, pe, ps, y, ident, shared["zT_done"])
                pe.wait_ge(shared["zT_ready"], 3)
                for k, n in enumerate(("gate", "up")):
                    for b in range(2):
                        for c in range(DC):
                            mm = nc.tensor.matmul(ps[:, 2 * k + b, :], zqT[:, c, :], wq[n][:, c * F + 512 * b:c * F + 512 * b + 512],
                                                  start=(c == 0), stop=(c == DC - 1))
                mm.then_inc(E["gu_done"], 1)
                pe.wait_ge(E["hq_ready"], 1)
                for k in range(2):
                    for j in range(4):
                        mm = nc.tensor.transpose(ps[:, 5 + k, j * S:(j + 1) * S], h[:, (4 * k + j) * P:(4 * k + j + 1) * P], ident[:, :])
                    mm.then_inc(E["hT_done"], 1)
                for j in range(8):
                    if j % 4 == 0:
                        pe.wait_ge(E["hT_ready"], j // 4 + 1)
                    mm = nc.tensor.matmul(ps[:, 4, 0:D], hqT[:, j, :], wq["down"][:, j * D:(j + 1) * D], start=(j == 0), stop=(j == 7))
                mm.then_inc(shared["out_done"], 1)


def second_cross_attention(nc, a, sb, sem, base, links, shared, xa):
    x, z, y, zT, ident, st, stats, rows, cols, ps = base
    vlink, alink, plink = links
    w, ct, cn, ct_loaded, cn_loaded = xa.w, xa.ct, xa.cn, xa.ct_loaded, xa.cn_loaded
    with ExitStack() as own:
        def t(name, shape, dt=F32):
            return sb("xa_" + name, shape, dt, own)

        qT, q2T = t("qT", [P, DC, S]), t("q2T", [P, DC, S])
        lim = t("lim", [P, 2])
        sc = t("sc", [P, SK])
        chunk_max, top, neg_top = t("chunk_max", [P, NCH]), t("top", [P, 1]), t("neg_top", [P, 1])
        total = t("total", [P, NCH])
        p = t("p", [P, 2, CH])
        pT = t("pT", [P, 2, TILES, S])
        rec, u, uT = t("rec", [P, 1]), t("u", [P, D]), t("uT", [P, DC, S])
        E = {n: sem("xa_" + n) for n in ("q_done", "q_ready", "q2_done", "q2_ready",
                                         "lim_ready", "scores_done", "max_done", "clipped", "top_ready", "p_ready",
                                         "t0_done", "t1_done", "pT0_ready", "pT1_ready", "weighed", "u_ready")}
        sc_ps = [ps[:, 2:4, 0:HCH], ps[:, 4:6, 0:HCH]]
        t_ps = [ps[:, 4, :], ps[:, 5, :]]

        def chunks(engine, step, first=0, last=NCH):
            start = first + (last - first) % RING
            for c in range(first, start):
                step(c, c % RING, c // RING)
            with engine.Fori(0, (last - start) // RING) as i:
                for c in range(start, start + RING):
                    step(i * RING + c, c % RING, i + c // RING)

        with nc.Block() as block:
            @block.sync
            def _(sp):
                def transposed(c, slot, turn):
                    sp.wait_ge(E["scores_done"], c - (RING - 1))
                    xa.load_ct(sp, c, slot)

                def context_rows(c, slot, turn):
                    sp.wait_ge(E["weighed"], c - (RING - 1))
                    xa.load_cn(sp, c, slot)

                chunks(sp, transposed, RING)
                chunks(sp, context_rows, RING)

            @block.scalar
            def _(act):
                act.wait_ge(shared["zT_done"], 4)
                nc.scalar.activation(zT[:, :, :], ps[:, 0, 0:DC * S].rearrange("p (c s) -> p c s", c=DC), ACT.Copy).then_inc(shared["zT_ready"], 1)
                act.wait_ge(E["q2_done"], 1)
                nc.scalar.activation(q2T[:, :, :], ps[:, 2, 0:DC * S].rearrange("p (c s) -> p c s", c=DC), ACT.Copy).then_inc(E["q2_ready"], 1)
                act.wait_ge(E["top_ready"], 1)

                def exponent(c, par):
                    at_least(act, E["t1_done"], c - 1)
                    nc.scalar.activation(p[:, par, :], sc[:, bass.ds(c * CH, CH)], ACT.Exp, bias=neg_top[:, 0:1],
                                         accum_out=total[:, bass.ds(c, 1)]).then_inc(E["p_ready"], 1)

                def copy_turned(c, par):
                    act.wait_ge(E["t1_done"], c + 1)
                    at_least(act, E["weighed"], c - 1)
                    nc.scalar.activation(pT[:, par, T0:TILES, :], t_ps[1][:, 0:(TILES - T0) * S].rearrange("p (t s) -> p t s", s=S),
                                         ACT.Copy).then_inc(E["pT1_ready"], 1)

                def step(c, slot, turn):
                    exponent(c + 1, (slot + 1) % 2)
                    copy_turned(c, slot % 2)

                exponent(0, 0)
                chunks(act, step, 0, NCH - 1)
                copy_turned(NCH - 1, (NCH - 1) % 2)
                act.wait_ge(shared["turned"], 2)
                nc.scalar.activation(uT[:, :, :], ps[:, 0, 0:DC * S].rearrange("p (c s) -> p c s", c=DC), ACT.Copy).then_inc(shared["turned_copied"], 1)

            @block.vector
            def _(v):
                link = vlink.on(v)
                layer_norm(nc.vector, link, z[:, :], x[:, :], st, stats).then_inc(shared["z_ready"], 1)
                v.wait_ge(E["q_done"], 1)
                link(nc.vector.tensor_tensor(qT[:, :, :], ps[:, 1, 0:DC * S].rearrange("p (c s) -> p c s", c=DC),
                                             cols[:, C_X_BQ:C_X_BQ + DC].unsqueeze(2).to_broadcast([P, DC, S]), ALU.add))
                nc.vector.tensor_scalar(qT[:, :, :], qT[:, :, :], D ** -0.5, None, ALU.mult).then_inc(E["q_ready"], 1)
                v.wait_ge(E["q2_done"], 1)
                nc.vector.tensor_scalar(lim[:, 0:1], ps[:, 6, 0:1], -1.0, -100.0, ALU.mult, ALU.add).then_inc(E["lim_ready"], 1)
                nc.vector.tensor_scalar(lim[:, 1:2], ps[:, 6, 0:1], -1.0, 100.0, ALU.mult, ALU.add).then_inc(E["lim_ready"], 1)
                v.wait_ge(E["lim_ready"], 2)

                def measure_and_clip(c, slot, turn):
                    v.wait_ge(E["scores_done"], c + 1)
                    nc.vector.tensor_reduce(chunk_max[:, bass.ds(c, 1)], sc_ps[slot % 2], AX.XY, ALU.max).then_inc(E["max_done"], 1)
                    nc.vector.tensor_scalar(sc[:, bass.ds(c * CH, CH)].rearrange("p (b k) -> p b k", b=2), sc_ps[slot % 2],
                                            lim[:, 0:1], lim[:, 1:2], ALU.max, ALU.min).then_inc(E["clipped"], 1)

                chunks(v, measure_and_clip)
                v.wait_ge(E["max_done"], NCH)
                link(nc.vector.tensor_reduce(top[:, :], chunk_max[:, :], AX.X, ALU.max))
                link(nc.vector.tensor_scalar(top[:, :], top[:, :], lim[:, 0:1], lim[:, 1:2], ALU.max, ALU.min))
                v.wait_ge(E["clipped"], NCH)
                nc.vector.tensor_scalar(neg_top[:, :], top[:, :], -1.0, None, ALU.mult).then_inc(E["top_ready"], 1)

                def copy_turned(c, slot, turn):
                    v.wait_ge(E["t0_done"], c + 1)
                    at_least(v, E["weighed"], c - 1)
                    nc.vector.tensor_copy(pT[:, slot % 2, 0:T0, :], t_ps[0].rearrange("p (t s) -> p t s", s=S)).then_inc(E["pT0_ready"], 1)

                chunks(v, copy_turned)
                v.wait_ge(E["p_ready"], NCH)
                link(nc.vector.tensor_reduce(rec[:, :], total[:, :], AX.X, ALU.add))
                link(nc.vector.reciprocal(rec[:, :], rec[:, :]))
                v.wait_ge(E["weighed"], NCH)
                nc.vector.tensor_scalar(u[:, :], ps[:, 7, 0:D], rec[:, 0:1], None, ALU.mult).then_inc(E["u_ready"], 1)
                link(nc.vector.tensor_tensor(x[:, :], x[:, :], rows[:, R_X_BV, :], ALU.add))
                v.wait_ge(shared["out_done"], 4)
                link(nc.vector.tensor_tensor(x[:, :], ps[:, 1, 0:D], x[:, :], ALU.add))

            @block.tensor
            def _(pe):
                pe.wait_ge(shared["z_ready"], 4)
                transpose_z(nc, pe, ps, z, ident, shared["zT_done"])
                pe.wait_ge(shared["zT_ready"], 4)
                pe.wait_ge(xa.w_loaded, 48)
                for e in range(DC):
                    for c in range(DC):
                        mm = nc.tensor.matmul(ps[:, 1, e * S:(e + 1) * S], w["wq"][:, c, e * P:(e + 1) * P], zT[:, c, :],
                                              start=(c == 0), stop=(c == DC - 1))
                mm.then_inc(E["q_done"], 1)
                pe.wait_ge(E["q_ready"], 1)
                for c in range(DC):
                    nc.tensor.matmul(ps[:, 6, 0:1], qT[:, c, :], cols[:, C_X_BK + c:C_X_BK + c + 1], start=(c == 0), stop=(c == DC - 1))
                for e in range(DC):
                    for c in range(DC):
                        mm = nc.tensor.matmul(ps[:, 2, e * S:(e + 1) * S], w["wkT"][:, c, e * P:(e + 1) * P], qT[:, c, :],
                                              start=(c == 0), stop=(c == DC - 1))
                mm.then_inc(E["q2_done"], 1)
                pe.wait_ge(E["q2_ready"], 1)

                def scores(c, slot, turn):
                    pe.wait_ge(ct_loaded[slot], turn * 16 + 16)
                    at_least(pe, E["clipped"], c - 1)
                    for k in range(DC):
                        for b in range(2):
                            mm = nc.tensor.matmul(sc_ps[slot % 2][:, b, :], q2T[:, k, :], ct[:, slot, k, b * HCH:(b + 1) * HCH],
                                                  start=(k == 0), stop=(k == DC - 1))
                    mm.then_inc(E["scores_done"], 1)

                chunks(pe, scores)
                pe.wait_ge(E["clipped"], NCH)

                def turn_p(c, par):
                    pe.wait_ge(E["p_ready"], c + 1)
                    at_least(pe, E["pT0_ready"], c)
                    at_least(pe, E["pT1_ready"], c)
                    for tile in range(TILES):
                        b, s = (0, tile) if tile < T0 else (1, tile - T0)
                        mm = nc.tensor.transpose(t_ps[b][:, s * S:(s + 1) * S], p[:, par, tile * P:(tile + 1) * P], ident[:, :])
                        if tile == T0 - 1:
                            mm.then_inc(E["t0_done"], 1)
                    mm.then_inc(E["t1_done"], 1)

                def weigh(c, slot, turn):
                    pe.wait_ge(cn_loaded[slot], turn * 16 + 16)
                    pe.wait_ge(E["pT0_ready"], c + 1)
                    pe.wait_ge(E["pT1_ready"], c + 1)
                    for tile in range(TILES):
                        mm = nc.tensor.matmul(ps[:, 7, 0:D], pT[:, slot % 2, tile, :], cn[:, slot, tile, :],
                                              start=(isinstance(c, int) and c == 0 and tile == 0), stop=True, skip_group_check=True)
                    mm.then_inc(E["weighed"], 1)

                def step(c, slot, turn):
                    turn_p(c + 1, (slot + 1) % 2)
                    weigh(c, slot, turn)

                turn_p(0, 0)
                chunks(pe, step, 0, NCH - 1)
                weigh(NCH - 1, (NCH - 1) % RING, (NCH - 1) // RING)
                pe.wait_ge(E["u_ready"], 1)
                for c in range(DC):
                    mm = nc.tensor.transpose(ps[:, 0, c * S:(c + 1) * S], u[:, c * P:(c + 1) * P], ident[:, :])
                mm.then_inc(shared["turned"], 1)
                pe.wait_ge(shared["turned_copied"], 2)
                for c in range(DC):
                    mm = nc.tensor.matmul(ps[:, 1, 0:D], uT[:, c, :], w["wv"][:, c, :], start=(c == 0), stop=(c == DC - 1))
                mm.then_inc(shared["out_done"], 1)


NS = 32
RANK = 16
CI = 512
CT = CI // P
TAPS = 4
HALF_N = NS // 2
HALF_READ = (12, 16)


class ScanWeights:
    pass


def scan_weights(a, scope, sb, sem):
    ss = ScanWeights()
    ss.ip = sb("ss_in_proj", [P, DC, 2 * CI], F32, scope)
    ss.op = sb("ss_out_proj", [P, CT, D], F32, scope)
    ss.xp = sb("ss_x_proj", [P, CT, RANK + 2 * NS], F32, scope)
    ss.dp = sb("ss_dt_proj", [RANK, CI], F32, scope)
    ss.cw, ss.al = sb("ss_conv_w", [P, CT, TAPS], F32, scope), sb("ss_a_log", [P, CT, NS], F32, scope)
    ss.loaded = sem("ss_loaded")

    def load(sp):
        sp.dma_start(ss.ip[:, :, :], a["ss_in"].rearrange("(c p) n -> p c n", p=P)).then_inc(ss.loaded, 16)
        sp.dma_start(ss.cw[:, :, :], a["ss_conv"].rearrange("(j p) k -> p j k", p=P)).then_inc(ss.loaded, 16)
        sp.dma_start(ss.xp[:, :, :], a["ss_x"].rearrange("(j p) k -> p j k", p=P)).then_inc(ss.loaded, 16)
        sp.dma_start(ss.dp[:, :], a["ss_dt"]).then_inc(ss.loaded, 16)
        sp.dma_start(ss.al[:, :, :], a["ss_alog"].rearrange("(j p) k -> p j k", p=P)).then_inc(ss.loaded, 16)
        sp.dma_start(ss.op[:, :, :], a["ss_out"].rearrange("(j p) n -> p j n", p=P)).then_inc(ss.loaded, 16)

    ss.load = load
    return ss


SS_LOADED = 6 * 16


def selective_scan(nc, a, sb, sem, base, links, shared, ss, me):
    x, z, y, zT, ident, st, stats, rows, cols, ps = base
    vlink, alink, plink = links
    ip, op, xp, dp, cw, al = ss.ip, ss.op, ss.xp, ss.dp, ss.cw, ss.al
    with ExitStack() as own:
        def t(name, shape, dt=F32):
            return sb("ss_" + name, shape, dt, own)

        up = t("up", [P, CT, TAPS - 1 + S])
        u, th, zg = t("u", [P, CT, S]), t("th", [P, CT, S]), t("zg", [P, CT, S])
        dbl = t("dbl", [RANK + 2 * NS, S])
        dt_, e, r, r2, du = (t(n, [P, CT, S]) for n in ("dt", "e", "r", "r2", "du"))
        b_all, c_all = t("b_all", [P, NS, S]), t("c_all", [P, NS, S])
        decay = t("decay", [P, 2, NS, S])
        h = t("h", [P, 2, NS, S])
        bc_dram = nc.dram_tensor("ss_bc", [2 * NS, S], F32).ap()
        ys = t("ys", [P, CT, S])
        E = {n: sem("ss_" + n) for n in ("uz_done", "up_ready", "zero_ready", "conv", "conv_done", "th_ready", "u_ready", "dbl_done",
                                         "dbl_ready", "dt_done", "abs_ready", "e_ready", "dt_ready", "bc_stored",
                                         "b_loaded", "c_loaded", "decay_ready", "zero_col", "driven", "scanned", "read", "pool_read",
                                         "summed", "zth_ready", "sum_copied", "y_ready")}

        def halves():
            for j in range(CT):
                for g in range(2):
                    yield j, j % 2, g, 2 * j + g

        with nc.Block() as block:
            @block.sync
            def _(sp):
                sp.wait_ge(E["dbl_ready"], 1)
                sp.dma_start(bc_dram, dbl[RANK:, :]).then_inc(E["bc_stored"], 16)
                sp.wait_ge(E["bc_stored"], 16)
                for k, (to, loaded) in enumerate(((b_all, E["b_loaded"]), (c_all, E["c_loaded"]))):
                    sp.dma_start(to[:, :, :], bc_dram[k * NS:(k + 1) * NS, :].rearrange("(o n) s -> o n s", o=1).to_broadcast([P, NS, S])).then_inc(loaded, 16)
                me.load_first(sp)

            @block.gpsimd
            def _(pool):
                nc.gpsimd.memset(up[:, :, 0:TAPS - 1], 0.0).then_inc(E["zero_ready"], 1)
                nc.gpsimd.memset(decay[:, :, :, 0:1], 0.0).then_inc(E["zero_col"], 1)
                pool.wait_ge(E["b_loaded"], 16)

                def drive(j, par, g, n):
                    pool.wait_ge(E["dt_ready"], j + 1)
                    at_least(pool, E["summed"], n - 3)
                    lo = g * HALF_N
                    nc.gpsimd.tensor_tensor(h[:, par, lo:lo + HALF_N, :], du[:, j, :].unsqueeze(1).to_broadcast([P, HALF_N, S]),
                                            b_all[:, lo:lo + HALF_N, :], ALU.mult).then_inc(E["driven"], 1)

                def read(j, par, g, n):
                    lo, hi = g * HALF_N + HALF_READ[g], (g + 1) * HALF_N
                    if lo == hi:
                        return
                    pool.wait_ge(E["scanned"], n + 1)
                    nc.gpsimd.tensor_tensor(h[:, par, lo:hi, :], h[:, par, lo:hi, :], c_all[:, lo:hi, :], ALU.mult).then_inc(E["pool_read"], 1)

                order = list(halves())
                drive(*order[0])
                pool.wait_ge(E["c_loaded"], 16)
                for n, half in enumerate(order):
                    if n + 1 < len(order):
                        drive(*order[n + 1])
                    read(*half)

            @block.scalar
            def _(act):
                link = alink.on(act)
                act.wait_ge(shared["zT_done"], 5)
                nc.scalar.activation(zT[:, :, :], ps[:, 0, 0:DC * S].rearrange("p (c s) -> p c s", c=DC), ACT.Copy).then_inc(shared["zT_ready"], 1)
                act.wait_ge(ss.loaded, SS_LOADED)
                link(nc.scalar.activation(al[:, :, :], al[:, :, :], ACT.Exp))
                link(nc.scalar.activation(al[:, :, :], al[:, :, :], ACT.Copy, scale=-1.0))
                act.wait_ge(E["uz_done"], 1)
                nc.scalar.activation(up[:, :, TAPS - 1:], ps[:, 1, :].rearrange("p (j s) -> p j s", j=CT), ACT.Copy).then_inc(E["up_ready"], 1)
                act.wait_ge(E["uz_done"], 2)
                nc.scalar.activation(zg[:, :, :], ps[:, 2, :].rearrange("p (j s) -> p j s", j=CT), ACT.Tanh, scale=0.5).then_inc(E["zth_ready"], 1)
                act.wait_ge(E["conv_done"], CT)
                nc.scalar.activation(th[:, :, :], u[:, :, :], ACT.Tanh, scale=0.5).then_inc(E["th_ready"], 1)
                act.wait_ge(E["dbl_done"], 1)
                nc.scalar.activation(dbl[:, :], ps[0:RANK + 2 * NS, 3, 0:S], ACT.Copy).then_inc(E["dbl_ready"], 1)
                act.wait_ge(E["abs_ready"], 1)
                link(nc.scalar.activation(e[:, :, :], r[:, :, :], ACT.Abs))
                nc.scalar.activation(e[:, :, :], e[:, :, :], ACT.Exp, scale=-1.0).then_inc(E["e_ready"], 1)
                act.wait_ge(E["zero_col"], 1)
                for j, par, g, n in halves():
                    act.wait_ge(E["dt_ready"], j + 1)
                    at_least(act, E["scanned"], n - 3)
                    for k in range(g * HALF_N, (g + 1) * HALF_N):
                        ins = nc.scalar.activation(decay[:, par, k, 1:S], dt_[:, j, 1:S], ACT.Exp, scale=al[:, j, k:k + 1])
                    ins.then_inc(E["decay_ready"], 1)

            @block.vector
            def _(v):
                link = vlink.on(v)
                link(layer_norm(nc.vector, link, z[:, :], x[:, :], st, stats))
                link(nc.vector.bn_stats(stats[:, :], z[:, :]))
                link(nc.vector.bn_aggr(st[:, 0:2], stats[:, :]))
                link(nc.vector.scalar_tensor_tensor(out=st[:, 1:2], in0=st[:, 0:1], scalar=st[:, 0:1], in1=st[:, 1:2], op0=ALU.mult, op1=ALU.add))
                layer_norm_scale(nc.vector, link, st, 1e-6)
                nc.vector.scalar_tensor_tensor(out=y[:, :], in0=z[:, :], scalar=st[:, 3:4], in1=rows[:, R_RMS_W, :],
                                               op0=ALU.mult, op1=ALU.mult).then_inc(shared["z_ready"], 1)
                link(nc.vector.tensor_tensor(x[:, :], x[:, :], z[:, :], ALU.add))
                v.wait_ge(E["up_ready"], 1)
                v.wait_ge(E["zero_ready"], 1)
                for k in range(TAPS):
                    for j in range(CT):
                        src, wk = up[:, j, k:k + S], cw[:, j, k:k + 1]
                        if k == 0:
                            nc.vector.tensor_scalar(u[:, j, :], src, wk, cols[:, C_CONVB + j:C_CONVB + j + 1], ALU.mult, ALU.add).then_inc(E["conv"], 1)
                        else:
                            v.wait_ge(E["conv"], (k - 1) * CT + j + 1)
                            nc.vector.scalar_tensor_tensor(out=u[:, j, :], in0=src, scalar=wk, in1=u[:, j, :], op0=ALU.mult,
                                                           op1=ALU.add).then_inc(E["conv_done" if k == TAPS - 1 else "conv"], 1)
                v.wait_ge(E["th_ready"], 1)
                link(nc.vector.scalar_tensor_tensor(out=u[:, :, :], in0=th[:, :, :], scalar=1.0, in1=u[:, :, :], op0=ALU.add, op1=ALU.mult))
                nc.vector.tensor_scalar(u[:, :, :], u[:, :, :], 0.5, None, ALU.mult).then_inc(E["u_ready"], 1)
                v.wait_ge(E["dt_done"], 1)
                nc.vector.tensor_tensor(r[:, :, :], ps[:, 4, :].rearrange("p (j s) -> p j s", j=CT),
                                        cols[:, C_DTB:C_DTB + CT].unsqueeze(2).to_broadcast([P, CT, S]), ALU.add).then_inc(E["abs_ready"], 1)
                v.wait_ge(E["e_ready"], 1)

                def step_size(lo, hi):
                    d, q, q2, w = dt_[:, lo:hi, :], e[:, lo:hi, :], r2[:, lo:hi, :], r[:, lo:hi, :]
                    link(nc.vector.tensor_scalar(d, q, 2.0, None, ALU.add))
                    link(nc.vector.reciprocal(d, d))
                    link(nc.vector.tensor_tensor(q, q, d, ALU.mult))
                    link(nc.vector.tensor_tensor(q2, q, q, ALU.mult))
                    link(nc.vector.tensor_scalar(d, q2, 1.0 / 15, 1.0 / 13, ALU.mult, ALU.add))
                    link(nc.vector.tensor_tensor(d, d, q2, ALU.mult))
                    for k in (11, 9, 7, 5, 3):
                        link(nc.vector.scalar_tensor_tensor(out=d, in0=d, scalar=1.0 / k, in1=q2, op0=ALU.add, op1=ALU.mult))
                    link(nc.vector.scalar_tensor_tensor(out=d, in0=d, scalar=1.0, in1=q, op0=ALU.add, op1=ALU.mult))
                    link(nc.vector.tensor_scalar(w, w, 0.0, None, ALU.max))
                    link(nc.vector.scalar_tensor_tensor(out=d, in0=d, scalar=2.0, in1=w, op0=ALU.mult, op1=ALU.add))
                    nc.vector.tensor_tensor(du[:, lo:hi, :], d, u[:, lo:hi, :], ALU.mult).then_inc(E["dt_ready"], hi - lo)

                def total(j):
                    v.wait_ge(E["summed"], 2 * j + 2)
                    nc.vector.tensor_reduce(ys[:, j, :], ps[:, 3 + j % 2, :].rearrange("p (n s) -> p s n", n=4), AX.X, ALU.add).then_inc(E["sum_copied"], 1)

                step_size(0, 1)
                step_size(1, 2)
                for j, par, g, n in halves():
                    lo = g * HALF_N
                    flat = "p n s -> p (n s)"
                    v.wait_ge(E["decay_ready"], n + 1)
                    v.wait_ge(E["driven"], n + 1)
                    hs = h[:, par, lo:lo + HALF_N, :].rearrange(flat)
                    nc.vector.tensor_tensor_scan(hs, decay[:, par, lo:lo + HALF_N, :].rearrange(flat), hs,
                                                 0.0, ALU.mult, ALU.add).then_inc(E["scanned"], 1)
                    if n == 0:
                        v.wait_ge(E["c_loaded"], 16)
                    v.wait_ge(E["scanned"], n + 1)
                    hi = lo + HALF_READ[g]
                    nc.vector.tensor_tensor(h[:, par, lo:hi, :], h[:, par, lo:hi, :], c_all[:, lo:hi, :], ALU.mult).then_inc(E["read"], 1)
                    if n == 0:
                        step_size(2, CT)
                    if g == 1 and j > 0:
                        total(j - 1)
                total(CT - 1)
                v.wait_ge(E["sum_copied"], CT)
                link(nc.vector.tensor_tensor(u[:, :, :], u[:, :, :], cols[:, C_DPAR:C_DPAR + CT].unsqueeze(2).to_broadcast([P, CT, S]), ALU.mult))
                v.wait_ge(E["zth_ready"], 1)
                link(nc.vector.scalar_tensor_tensor(out=zg[:, :, :], in0=zg[:, :, :], scalar=1.0, in1=ps[:, 2, :].rearrange("p (j s) -> p j s", j=CT),
                                                    op0=ALU.add, op1=ALU.mult))
                link(nc.vector.tensor_tensor(ys[:, :, :], ys[:, :, :], u[:, :, :], ALU.add))
                nc.vector.scalar_tensor_tensor(out=ys[:, :, :], in0=ys[:, :, :], scalar=0.5, in1=zg[:, :, :], op0=ALU.mult,
                                               op1=ALU.mult).then_inc(E["y_ready"], 1)
                v.wait_ge(shared["out_done"], 5)
                link(nc.vector.tensor_tensor(x[:, :], ps[:, 0, 0:D], x[:, :], ALU.add))

            @block.tensor
            def _(pe):
                pe.wait_ge(shared["z_ready"], 5)
                transpose_z(nc, pe, ps, y, ident, shared["zT_done"])
                pe.wait_ge(shared["zT_ready"], 5)
                pe.wait_ge(ss.loaded, SS_LOADED)
                for half in range(2):
                    for j in range(CT):
                        for c in range(DC):
                            col = half * CI + j * P
                            mm = nc.tensor.matmul(ps[:, 1 + half, j * S:(j + 1) * S], ip[:, c, col:col + P], zT[:, c, :],
                                                  start=(c == 0), stop=(c == DC - 1))
                    mm.then_inc(E["uz_done"], 1)
                pe.wait_ge(E["u_ready"], 1)
                for j in range(CT):
                    mm = nc.tensor.matmul(ps[0:RANK + 2 * NS, 3, 0:S], xp[:, j, :], u[:, j, :], start=(j == 0), stop=(j == CT - 1))
                mm.then_inc(E["dbl_done"], 1)
                pe.wait_ge(E["dbl_ready"], 1)
                for j in range(CT):
                    mm = nc.tensor.matmul(ps[:, 4, j * S:(j + 1) * S], dp[:, j * P:(j + 1) * P], dbl[0:RANK, :], start=True, stop=True)
                mm.then_inc(E["dt_done"], 1)
                pe.wait_ge(E["abs_ready"], 1)
                for j, par, g, n in halves():
                    if g == 0:
                        at_least(pe, E["sum_copied"], j - 1)
                    for k in range(HALF_N // 4):
                        if k == 0:
                            pe.wait_ge(E["read"], n + 1)
                        if k == HALF_READ[g] // 4:
                            pe.wait_ge(E["pool_read"], j + 1)
                        lo = g * HALF_N + 4 * k
                        mm = nc.tensor.matmul(ps[:, 3 + j % 2, :], ident[:, :], h[:, par, lo:lo + 4, :].rearrange("p n s -> p (n s)"),
                                              start=(lo == 0), stop=(lo == NS - 4))
                    mm.then_inc(E["summed"], 1)
                pe.wait_ge(E["y_ready"], 1)
                for j in range(CT):
                    mm = nc.tensor.matmul(ps[:, 0, 0:D], ys[:, j, :], op[:, j, :], start=(j == 0), stop=(j == CT - 1))
                mm.then_inc(shared["out_done"], 1)


NE = 8
FE, FS = 768, 256


class ExpertWeights:
    pass


def expert_weights(a, scope, sb, sem):
    me = ExpertWeights()
    me.router = sb("me_router", [P, DC, NE], F32, scope)
    me.s1, me.s2 = sb("me_s1", [P, DC, 2 * FS], F32, scope), sb("me_s2", [P, FS // P, D], F32, scope)
    me.w1, me.w2 = [sb("me_w1_0", [P, DC, 2 * FE], F32, scope)], [sb("me_w2_0", [P, FE // P, D], F32, scope)]
    me.shared_loaded = sem("me_shared_loaded")
    me.w1_loaded = [sem("me_w1_loaded0"), sem("me_w1_loaded1")]
    me.w2_loaded = [sem("me_w2_loaded0"), sem("me_w2_loaded1")]
    w1 = a["me_w1"].rearrange("e (c p) n -> p e c n", p=P)
    w2 = a["me_w2"].rearrange("e (c p) n -> p e c n", p=P)

    def load_w1(sp, e, par):
        sp.dma_start(me.w1[par][:, :, :], w1[:, bass.ds(e, 1), :, :].rearrange("p o c n -> p (o c) n")).then_inc(me.w1_loaded[par], 16)

    def load_w2(sp, e, par):
        sp.dma_start(me.w2[par][:, :, :], w2[:, bass.ds(e, 1), :, :].rearrange("p o c n -> p (o c) n")).then_inc(me.w2_loaded[par], 16)

    def load_first(sp):
        sp.dma_start(me.router[:, :, :], a["me_router"].rearrange("(c p) n -> p c n", p=P)).then_inc(me.shared_loaded, 16)
        sp.dma_start(me.s1[:, :, :], a["me_s1"].rearrange("(c p) n -> p c n", p=P)).then_inc(me.shared_loaded, 16)
        sp.dma_start(me.s2[:, :, :], a["me_s2"].rearrange("(c p) n -> p c n", p=P)).then_inc(me.shared_loaded, 16)
        load_w1(sp, 0, 0)
        load_w2(sp, 0, 0)

    me.load_w1, me.load_w2, me.load_first = load_w1, load_w2, load_first
    return me


def expert_ffn(nc, a, sb, sem, base, links, shared, me):
    x, z, y, zT, ident, st, stats, rows, cols, ps = base
    vlink, alink, plink = links
    with ExitStack() as own:
        def t(name, shape, dt=F32):
            return sb("me_" + name, shape, dt, own)

        me.w1.append(t("w1_1", [P, DC, 2 * FE]))
        me.w2.append(t("w2_1", [P, FE // P, D]))
        router, s1, s2, w1, w2, w1_loaded, w2_loaded = me.router, me.s1, me.s2, me.w1, me.w2, me.w1_loaded, me.w2_loaded
        pr, total, rec = t("pr", [P, NE]), t("total", [P, 1]), t("rec", [P, 4])
        cmp, eq = t("cmp", [P, NE, NE]), t("eq", [P, NE, NE])
        before = t("before", [P, NE, NE])
        rank, pick, comb = t("rank", [P, NE]), t("pick", [P, 2, NE]), t("comb", [P, NE])
        best = t("best", [P, 2])
        th, hT = t("th", [P, 2, FE]), t("hT", [P, 2, FE])
        E = {n: sem("me_" + n) for n in ("before_ready", "best_ready", "ex_ready", "up_done", "th_ready", "h_ready",
                                         "down_done", "added", "silu")}
        gu = [ps[:, 0:3, :].rearrange("p b n -> p (b n)"), ps[:, 3:6, :].rearrange("p b n -> p (b n)")]

        with nc.Block() as block:
            @block.sync
            def _(sp):
                me.load_w1(sp, 1, 1)
                me.load_w2(sp, 1, 1)
                with sp.Fori(1, NE // 2) as i:
                    for par in range(2):
                        sp.wait_ge(E["up_done"], i * 2 + par)
                        me.load_w1(sp, i * 2 + par, par)
                        sp.wait_ge(E["down_done"], i * 2 + par)
                        me.load_w2(sp, i * 2 + par, par)

            @block.gpsimd
            def _(pool):
                link = plink.on(pool)
                link(nc.gpsimd.memset(before[:, :, :], 1.0))
                nc.gpsimd.affine_select(out=before[:, :, :], in_=before[:, :, :], compare_op=ALU.is_gt, fill=0.0, base=0,
                                        pattern=[[1, NE], [-1, NE]], channel_multiplier=0).then_inc(E["before_ready"], 1)

            @block.scalar
            def _(act):
                act.wait_ge(shared["zT_done"], 6)
                nc.scalar.activation(zT[:, :, :], ps[:, 6, 0:DC * S].rearrange("p (c s) -> p c s", c=DC), ACT.Copy).then_inc(shared["zT_ready"], 1)
                act.wait_ge(shared["max_ready"], 2)
                nc.scalar.activation(pr[:, :], ps[:, 7, 0:NE], ACT.Exp, bias=rec[:, 0:1], accum_out=total[:, :]).then_inc(shared["exp_ready"], 1)

                def half_tanh(n, par, width):
                    act.wait_ge(E["up_done"], n + 1)
                    at_least(act, E["h_ready"], n - 1)
                    nc.scalar.activation(th[:, par, 0:width], gu[par][:, 0:width], ACT.Tanh, scale=0.5).then_inc(E["th_ready"], 1)

                half_tanh(0, 1, FS)
                act.wait_ge(E["best_ready"], 1)
                nc.scalar.activation(rec[:, 2:3], best[:, 1:2], ACT.Exp, bias=rec[:, 1:2]).then_inc(E["ex_ready"], 1)

                def pair(i):
                    for par in range(2):
                        half_tanh(i * 2 + (par + 1), par, FE)

                with act.Fori(0, NE // 2) as i:
                    pair(i)

            @block.vector
            def _(v):
                link = vlink.on(v)
                link(layer_norm(nc.vector, link, z[:, :], x[:, :], st, stats))
                link(layer_norm(nc.vector, link, y[:, :], z[:, :], st, stats))
                link(nc.vector.tensor_tensor(y[:, :], y[:, :], rows[:, R_F_G, :], ALU.mult))
                nc.vector.tensor_tensor(y[:, :], y[:, :], rows[:, R_F_B, :], ALU.add).then_inc(shared["z_ready"], 1)
                v.wait_ge(shared["logits_done"], 2)
                nc.vector.tensor_reduce(rec[:, 0:1], ps[:, 7, 0:NE], AX.X, ALU.max, negate=True).then_inc(shared["max_ready"], 1)
                v.wait_ge(shared["exp_ready"], 2)
                link(nc.vector.reciprocal(total[:, :], total[:, :]))
                link(nc.vector.tensor_scalar(pr[:, :], pr[:, :], total[:, 0:1], None, ALU.mult))
                mine = pr[:, :].unsqueeze(2).to_broadcast([P, NE, NE])
                other = pr[:, :].unsqueeze(1).to_broadcast([P, NE, NE])
                link(nc.vector.tensor_tensor(cmp[:, :, :], other, mine, ALU.is_gt))
                link(nc.vector.tensor_tensor(eq[:, :, :], other, mine, ALU.is_equal))
                v.wait_ge(E["before_ready"], 1)
                link(nc.vector.tensor_tensor(eq[:, :, :], eq[:, :, :], before[:, :, :], ALU.mult))
                link(nc.vector.tensor_tensor(cmp[:, :, :], cmp[:, :, :], eq[:, :, :], ALU.add))
                link(nc.vector.tensor_reduce(rank[:, :], cmp[:, :, :], AX.X, ALU.add))
                for k in range(2):
                    link(nc.vector.tensor_scalar(pick[:, k, :], rank[:, :], float(k), None, ALU.is_equal))
                    link(nc.vector.tensor_tensor(comb[:, :], pick[:, k, :], pr[:, :], ALU.mult))
                    link(nc.vector.tensor_reduce(best[:, k:k + 1], comb[:, :], AX.X, ALU.add))
                nc.vector.tensor_scalar(rec[:, 1:2], best[:, 0:1], -1.0, None, ALU.mult).then_inc(E["best_ready"], 1)
                v.wait_ge(E["ex_ready"], 1)
                link(nc.vector.tensor_scalar(rec[:, 3:4], rec[:, 2:3], 1.0, None, ALU.add))
                link(nc.vector.reciprocal(rec[:, 3:4], rec[:, 3:4]))
                link(nc.vector.tensor_tensor(rec[:, 2:3], rec[:, 2:3], rec[:, 3:4], ALU.mult))
                link(nc.vector.tensor_scalar(comb[:, :], pick[:, 0, :], rec[:, 3:4], None, ALU.mult))
                link(nc.vector.scalar_tensor_tensor(out=comb[:, :], in0=pick[:, 1, :], scalar=rec[:, 2:3], in1=comb[:, :], op0=ALU.mult, op1=ALU.add))

                def hidden(n, par, width):
                    v.wait_ge(E["th_ready"], n + 1)
                    nc.vector.scalar_tensor_tensor(out=th[:, par, 0:width], in0=th[:, par, 0:width], scalar=1.0, in1=gu[par][:, 0:width],
                                                   op0=ALU.add, op1=ALU.mult).then_inc(E["silu"], 1)
                    v.wait_ge(E["silu"], n + 1)
                    at_least(v, E["down_done"], n - 1)
                    nc.vector.scalar_tensor_tensor(out=hT[:, par, 0:width], in0=th[:, par, 0:width], scalar=0.5, in1=gu[par][:, width:2 * width],
                                                   op0=ALU.mult, op1=ALU.mult).then_inc(E["h_ready"], 1)

                def weigh(n, bank, scalar):
                    v.wait_ge(E["down_done"], n + 1)
                    at_least(v, E["added"], n)
                    nc.vector.scalar_tensor_tensor(out=x[:, :], in0=ps[:, bank, 0:D], scalar=scalar, in1=x[:, :],
                                                   op0=ALU.mult, op1=ALU.add).then_inc(E["added"], 1)

                hidden(0, 1, FS)
                hidden(1, 0, FE)
                weigh(0, 7, 1.0)

                def pair(i, peeled):
                    hidden(i * 2 + 2, 1, FE)
                    weigh(i * 2 + 1, 6, comb[:, bass.ds(i * 2, 1)])
                    if not peeled:
                        hidden(i * 2 + 3, 0, FE)
                    weigh(i * 2 + 2, 7, comb[:, bass.ds(i * 2 + 1, 1)])

                with v.Fori(0, NE // 2 - 1) as i:
                    pair(i, False)
                pair(NE // 2 - 1, True)
                v.wait_ge(E["added"], NE + 1)

            @block.tensor
            def _(pe):
                pe.wait_ge(shared["z_ready"], 6)
                for c in range(DC):
                    mm = nc.tensor.transpose(ps[:, 6, c * S:(c + 1) * S], y[:, c * P:(c + 1) * P], ident[:, :])
                mm.then_inc(shared["zT_done"], 1)
                pe.wait_ge(shared["zT_ready"], 6)
                pe.wait_ge(me.shared_loaded, 48)
                for c in range(DC):
                    mm = nc.tensor.matmul(ps[:, 7, 0:NE], zT[:, c, :], router[:, c, :], start=(c == 0), stop=(c == DC - 1))
                mm.then_inc(shared["logits_done"], 1)

                def first_product(n, par, w, width):
                    at_least(pe, E["h_ready"], n - 1)
                    for j in range(2 * width // P):
                        for c in range(DC):
                            mm = nc.tensor.matmul(gu[par][:, j * P:(j + 1) * P], w[:, c, j * P:(j + 1) * P], zT[:, c, :],
                                                  start=(c == 0), stop=(c == DC - 1))
                    mm.then_inc(E["up_done"], 1)

                def second_product(n, par, w, width):
                    pe.wait_ge(E["h_ready"], n + 1)
                    at_least(pe, E["added"], n - 1)
                    for j in range(width // P):
                        mm = nc.tensor.matmul(ps[:, 7 - (1 - par), 0:D], hT[:, par, j * P:(j + 1) * P], w[:, j, :],
                                              start=(j == 0), stop=(j == width // P - 1))
                    mm.then_inc(E["down_done"], 1)

                first_product(0, 1, s1, FS)
                pe.wait_ge(w1_loaded[0], 16)
                first_product(1, 0, w1[0], FE)
                pe.wait_ge(shared["exp_ready"], 2)
                second_product(0, 1, s2, FS)

                def pair(i, peeled):
                    pe.wait_ge(w1_loaded[1], i * 16 + 16)
                    first_product(i * 2 + 2, 1, w1[1], FE)
                    pe.wait_ge(w2_loaded[0], i * 16 + 16)
                    second_product(i * 2 + 1, 0, w2[0], FE)
                    if not peeled:
                        pe.wait_ge(w1_loaded[0], i * 16 + 32)
                        first_product(i * 2 + 3, 0, w1[0], FE)
                    pe.wait_ge(w2_loaded[1], i * 16 + 16)
                    second_product(i * 2 + 2, 1, w2[1], FE)

                with pe.Fori(0, NE // 2 - 1) as i:
                    pair(i, False)
                pair(NE // 2 - 1, True)


_INS = {
    "ss_in": lambda i: i["L1_attn_in_proj_w"].T,
    "ss_conv": lambda i: i["L1_attn_conv_w"],
    "ss_x": lambda i: i["L1_attn_x_proj_w"].T,
    "ss_dt": lambda i: i["L1_attn_dt_proj_w"].T,
    "ss_alog": lambda i: i["L1_attn_A_log"],
    "ss_out": lambda i: i["L1_attn_out_proj_w"].T,
    "me_router": lambda i: i["L1_ffn_router_w"].T,
    "me_w1": lambda i: i["L1_ffn_gate_up_w"].transpose(0, 2, 1),
    "me_w2": lambda i: i["L1_ffn_down_w"].transpose(0, 2, 1),
    "me_s1": lambda i: i["L1_ffn_shared_gate_up_w"].T,
    "me_s2": lambda i: i["L1_ffn_shared_down_w"].T,
    "ctx": lambda i: i["ctx_1024"][0],
    "ca_wq": lambda i: i["L0_attn_Wq"].T,
    "ca_wk": lambda i: i["L0_attn_Wk"].T,
    "ca_wv": lambda i: i["L0_attn_Wv"].T,
    "tf_gate": lambda i: i["L0_ffn_w_gate"].T,
    "tf_up": lambda i: i["L0_ffn_w_up"].T,
    "tf_down": lambda i: i["L0_ffn_w_down"].T,
    "xa_wq": lambda i: i["L1_xattn_Wq"],
    "xa_wkT": lambda i: i["L1_xattn_Wk"].T,
    "xa_wv": lambda i: i["L1_xattn_Wv"],
    "x": lambda i: i["x"][0],
    "ctxT": lambda i: i["ctx_1024"][0].T,
    "wq": lambda i: i["L0_xattn_w_q"],
    "wk": lambda i: i["L0_xattn_w_kv"][:, :INNER],
    "wv": lambda i: i["L0_xattn_w_kv"][:, INNER:],
    "w_out": lambda i: i["L0_xattn_w_out"],
    "gate": lambda i: i["L0_xattn_gate"].reshape(1, 1),
}


def kernel(**inputs):
    import numpy as np
    import concourse.bacc as bacc
    from concourse.bass_utils import run_bass_kernel_spmd

    given = {k: np.asarray(v) for k, v in inputs.items()}
    rows = np.stack([given["L0_xattn_ln_gamma"], given["L0_xattn_ln_beta"], given["L0_xattn_b_out"], given["L0_attn_bv"],
                     given["L1_xattn_bv"], given["L1_attn_norm_w"], given["L1_ffn_ln_gamma"], given["L1_ffn_ln_beta"]])
    cols = np.concatenate([given[n].reshape(-1, P).T for n in
                           ("L0_attn_bq", "L0_attn_bk", "L1_xattn_bq", "L1_xattn_bk", "L1_attn_conv_b",
                            "L1_attn_dt_proj_b", "L1_attn_D_param")], axis=1)
    arrays = {n: f(given) for n, f in _INS.items()}
    arrays["rows"], arrays["cols"] = rows, cols
    nc = bacc.Bacc("TRN2", target_bir_lowering=False, num_devices=1)
    feed, aps = {}, {}
    for n, v in arrays.items():
        feed["in_" + n] = np.ascontiguousarray(v)
        aps[n] = nc.dram_tensor("in_" + n, v.shape, mybir.dt.from_np(v.dtype), kind="ExternalInput").ap()
    out = nc.dram_tensor("out", (S, D), F32, kind="ExternalOutput").ap()
    perceiver(nc, aps, out)
    r = run_bass_kernel_spmd(nc, [feed], core_ids=[0])
    return r.results[0]["out"].reshape(1, S, D)
```
